# Optimizing a Trainium2 kernel written in Bass

```python
import numpy as np
import jax
import jax.numpy as jnp

def _softmax(x, axis=-1):
    return jax.nn.softmax(x, axis=axis)

def _gelu(x):
    return jax.nn.gelu(x, approximate=True)

def _silu(x):
    return jax.nn.silu(x)

def _sigmoid(x):
    return jax.nn.sigmoid(x)

def _layernorm(x, axis=-1, eps=1e-05):
    m = jnp.mean(x, axis=axis, keepdims=True)
    v = jnp.var(x, axis=axis, keepdims=True)
    return (x - m) / jnp.sqrt(v + eps)

def _scatter_add(tgt, idx, src, axis=0):
    return tgt.at[idx].add(src)

def _segment_sum(src, seg, n):
    return jax.ops.segment_sum(src, seg, n)
kernel_name = 'mk_flamingo_gated_d2_seqx_r8_03a5b6'

def setup_inputs(seed: int=0):
    np.random.seed(seed)
    _w = jnp.asarray

    def _rec_inputs():
        import jax
        import jax.numpy as jnp
        _rk = jax.random.key(seed)
        x = -0.0002928 + 1 * jax.random.normal(jax.random.fold_in(_rk, 1), (8, 128, 128), jnp.float32)
        _lenS = 128 - jax.random.randint(jax.random.fold_in(_rk, 7), (8,), 0, max(1, 128 // 4) + 1, jnp.int32)
        _lenS2 = 128 - jax.random.randint(jax.random.fold_in(_rk, 8), (8,), 0, max(1, 128 // 4) + 1, jnp.int32)
        _ctx_1024P = jax.random.normal(jax.random.fold_in(_rk, 11), (8, 16, 128), jnp.float32)
        _ctx_1024c = jax.random.dirichlet(jax.random.fold_in(_rk, 511), 0.3 * jnp.ones((16,), jnp.float32), (8, 128))
        _ctx_1024t = jnp.einsum('bsk,bkd->bsd', _ctx_1024c, _ctx_1024P)
        _ctx_1024t = _ctx_1024t * jax.lax.rsqrt(jnp.mean(jnp.square(_ctx_1024t)) + 1e-12) * 0.953939
        ctx_1024 = -1.39393e-06 + 0.999914 * (_ctx_1024t + 0.3 * jax.random.normal(jax.random.fold_in(_rk, 611), (8, 128, 128), jnp.float32))
        _g = jax.random.normal(jax.random.fold_in(_rk, 9001), (2, 2), jnp.float32)
        _g = jnp.sign(_g) * jnp.maximum(jnp.abs(_g), 1.0) + (_g == 0) * 1.0
        g_xattn = _g[0]
        g_ffn = _g[1]
        return (x, ctx_1024, g_xattn, g_ffn)
    x, ctx_1024, g_xattn, g_ffn = _rec_inputs()

    def _L0_xattn_setup():
        import jax, jax.numpy as jnp
        import numpy as np
        B, S, D, H = (2, 256, 128, 16)
        DK = D // H
        key = jax.random.key(seed)
        ks = jax.random.split(key, 8)

        def xavier(k, shape):
            fan_in, fan_out = (shape[1], shape[0])
            a = np.sqrt(6.0 / (fan_in + fan_out)).astype(np.float32)
            return jax.random.uniform(k, shape, jnp.float32, -a, a)
        return {'q': jax.random.normal(ks[0], (B, S, D), jnp.float32), 'k': jax.random.normal(ks[1], (B, S, D), jnp.float32), 'v': jax.random.normal(ks[2], (B, S, D), jnp.float32), 'W_q': xavier(ks[3], (D, D)), 'W_k': xavier(ks[4], (D, D)), 'W_v': xavier(ks[5], (D, D)), 'W_o': xavier(ks[6], (D, D)), 'b_o': jnp.zeros((D,), jnp.float32)}
    _L0_xattn_all = _L0_xattn_setup()
    _L0_xattn_in = {k: v for k, v in _L0_xattn_all.items() if k in ('W_q', 'W_k', 'W_v', 'W_o', 'b_o')}
    del _L0_xattn_all

    def _L0_ffn_setup():
        import jax, jax.numpy as jnp
        import numpy as np
        HIDDEN = 128
        INNER = 512

        def _weight_quant(w):
            scale = 1.0 / jnp.clip(jnp.mean(jnp.abs(w)), 1e-05)
            wq = jnp.clip(jnp.round(w * scale), -1.0, 1.0) / scale
            return w + jax.lax.stop_gradient(wq - w)

        def _act_quant(x):
            scale = 127.0 / jnp.clip(jnp.max(jnp.abs(x), axis=-1, keepdims=True), 1e-05)
            xq = jnp.clip(jnp.round(x * scale), -128.0, 127.0) / scale
            return x + jax.lax.stop_gradient(xq - x)

        def _bitlinear(x, w):
            return jnp.einsum('bsi,oi->bso', _act_quant(x), _weight_quant(w))
        key = jax.random.key(seed)
        k0, k1, k2, k3 = jax.random.split(key, 4)
        x = jax.random.normal(k0, (4, 256, HIDDEN), dtype=jnp.float32)
        w_gate = jax.random.normal(k1, (INNER, HIDDEN), dtype=jnp.float32) / np.sqrt(HIDDEN)
        w_up = jax.random.normal(k2, (INNER, HIDDEN), dtype=jnp.float32) / np.sqrt(HIDDEN)
        w_down = jax.random.normal(k3, (HIDDEN, INNER), dtype=jnp.float32) / np.sqrt(INNER)
        return {'x': x, 'w_gate': w_gate, 'w_up': w_up, 'w_down': w_down}
    _L0_ffn_all = _L0_ffn_setup()
    _L0_ffn_in = {k: v for k, v in _L0_ffn_all.items() if k in ('w_gate', 'w_up', 'w_down')}
    del _L0_ffn_all

    def _L1_xattn_setup():
        import jax, jax.numpy as jnp
        import numpy as np
        import math
        D_KEY = 128
        SCALE = math.sqrt(D_KEY)
        MASK_VAL = 10000000000.0
        key = jax.random.key(seed)
        kq, kk, kv = jax.random.split(key, 3)
        B, L, D = (16, 256, 128)
        return {'query': jax.random.normal(kq, (B, L, D), dtype=jnp.float32), 'key': jax.random.normal(kk, (B, L, D), dtype=jnp.float32), 'value': jax.random.normal(kv, (B, L, D), dtype=jnp.float32)}
    _L1_xattn_all = _L1_xattn_setup()
    _L1_xattn_in = {k: v for k, v in _L1_xattn_all.items() if k in ()}
    del _L1_xattn_all

    def _L1_ffn_setup():
        import math
        import jax, jax.numpy as jnp
        import numpy as np
        HIDDEN = 128
        INTER = 512
        EXPERTS = 8
        B, T = (4, 256)
        EPS = 1e-12
        CAP_FACTOR = 1.0
        MIN_CAP = 4

        def layer_norm(x, g, b, eps=EPS):
            m = jnp.mean(x, axis=-1, keepdims=True)
            v = jnp.var(x, axis=-1, keepdims=True)
            return (x - m) * jax.lax.rsqrt(v + eps) * g + b

        def top1_gate(x, wg, capacity):
            logits = x @ wg
            gates = jax.nn.softmax(logits, axis=-1)
            E = wg.shape[-1]
            idx = jnp.argmax(gates, axis=-1)
            mask1 = jax.nn.one_hot(idx, E, dtype=gates.dtype)
            locations = jnp.cumsum(mask1, axis=0) - mask1
            mask1 = mask1 * (locations < capacity).astype(gates.dtype)
            gates1_s = jnp.sum(gates * mask1, axis=-1)
            loc_s = jnp.sum(locations * mask1, axis=-1).astype(jnp.int32)
            loc_oh = jax.nn.one_hot(loc_s, capacity, dtype=gates.dtype)
            combine = gates1_s[:, None, None] * mask1[:, :, None] * loc_oh[:, None, :]
            dispatch = jax.lax.stop_gradient((combine > 0).astype(x.dtype))
            return (combine, dispatch)
        key = jax.random.key(seed)
        ks = jax.random.split(key, 8)
        s = 0.02
        return {'x': jax.random.normal(ks[0], (B, T, HIDDEN), jnp.float32), 'attn_nw': jnp.ones((HIDDEN,), jnp.float32), 'attn_nb': jnp.zeros((HIDDEN,), jnp.float32), 'wg': jax.random.normal(ks[1], (HIDDEN, EXPERTS), jnp.float32) * s, 'inter_w': jax.random.normal(ks[2], (EXPERTS, HIDDEN, INTER), jnp.float32) * s, 'inter_b': jnp.zeros((EXPERTS, INTER), jnp.float32), 'output_w': jax.random.normal(ks[3], (EXPERTS, INTER, HIDDEN), jnp.float32) * s, 'output_b': jnp.zeros((EXPERTS, HIDDEN), jnp.float32), 'res_inter_w': jax.random.normal(ks[4], (HIDDEN, INTER), jnp.float32) * s, 'res_inter_b': jnp.zeros((INTER,), jnp.float32), 'res_output_w': jax.random.normal(ks[5], (INTER, HIDDEN), jnp.float32) * s, 'res_output_b': jnp.zeros((HIDDEN,), jnp.float32), 'res_coef': jax.random.normal(ks[6], (HIDDEN, 2), jnp.float32) * s}
    _L1_ffn_all = _L1_ffn_setup()
    _L1_ffn_in = {k: v for k, v in _L1_ffn_all.items() if k in ('attn_nw', 'attn_nb', 'wg', 'inter_w', 'inter_b', 'output_w', 'output_b', 'res_inter_w', 'res_inter_b', 'res_output_w', 'res_output_b', 'res_coef')}
    del _L1_ffn_all
    return {'x': x, 'ctx_1024': ctx_1024, 'g_xattn': g_xattn, 'g_ffn': g_ffn, 'L0_xattn_W_q': _L0_xattn_in['W_q'], 'L0_xattn_W_k': _L0_xattn_in['W_k'], 'L0_xattn_W_v': _L0_xattn_in['W_v'], 'L0_xattn_W_o': _L0_xattn_in['W_o'], 'L0_xattn_b_o': _L0_xattn_in['b_o'], 'L0_ffn_w_gate': _L0_ffn_in['w_gate'], 'L0_ffn_w_up': _L0_ffn_in['w_up'], 'L0_ffn_w_down': _L0_ffn_in['w_down'], 'L1_ffn_attn_nw': _L1_ffn_in['attn_nw'], 'L1_ffn_attn_nb': _L1_ffn_in['attn_nb'], 'L1_ffn_wg': _L1_ffn_in['wg'], 'L1_ffn_inter_w': _L1_ffn_in['inter_w'], 'L1_ffn_inter_b': _L1_ffn_in['inter_b'], 'L1_ffn_output_w': _L1_ffn_in['output_w'], 'L1_ffn_output_b': _L1_ffn_in['output_b'], 'L1_ffn_res_inter_w': _L1_ffn_in['res_inter_w'], 'L1_ffn_res_inter_b': _L1_ffn_in['res_inter_b'], 'L1_ffn_res_output_w': _L1_ffn_in['res_output_w'], 'L1_ffn_res_output_b': _L1_ffn_in['res_output_b'], 'L1_ffn_res_coef': _L1_ffn_in['res_coef']}

def reference(x, ctx_1024, g_xattn, g_ffn, L0_xattn_W_q, L0_xattn_W_k, L0_xattn_W_v, L0_xattn_W_o, L0_xattn_b_o, L0_ffn_w_gate, L0_ffn_w_up, L0_ffn_w_down, L1_ffn_attn_nw, L1_ffn_attn_nb, L1_ffn_wg, L1_ffn_inter_w, L1_ffn_inter_b, L1_ffn_output_w, L1_ffn_output_b, L1_ffn_res_inter_w, L1_ffn_res_inter_b, L1_ffn_res_output_w, L1_ffn_res_output_b, L1_ffn_res_coef):
    import jax
    import jax.numpy as jnp

    def _L0_xattn_ref(q, k, v, W_q, W_k, W_v, W_o, b_o):
        import jax, jax.numpy as jnp
        import numpy as np
        B, S, D, H = (2, 256, 128, 16)
        DK = D // H
        b, s, d = q.shape
        qh = (q @ W_q.T).reshape(b, s, H, DK).transpose(0, 2, 1, 3)
        kh = (k @ W_k.T).reshape(b, s, H, DK).transpose(0, 2, 1, 3)
        vh = (v @ W_v.T).reshape(b, s, H, DK).transpose(0, 2, 1, 3)
        scores = jnp.einsum('bhqd,bhkd->bhqk', qh, kh)
        causal = jnp.triu(jnp.ones((s, s), bool), k=1)
        scores = jnp.where(causal, -jnp.inf, scores)
        attn = jax.nn.softmax(scores / np.sqrt(DK).astype(np.float32), axis=-1)
        ctx = jnp.einsum('bhqk,bhkd->bhqd', attn, vh)
        ctx = ctx.transpose(0, 2, 1, 3).reshape(b, s, d)
        return ctx @ W_o.T + b_o

    def _L0_ffn_ref(x, w_gate, w_up, w_down):
        import jax, jax.numpy as jnp
        import numpy as np
        HIDDEN = 128
        INNER = 512

        def _weight_quant(w):
            scale = 1.0 / jnp.clip(jnp.mean(jnp.abs(w)), 1e-05)
            wq = jnp.clip(jnp.round(w * scale), -1.0, 1.0) / scale
            return w + jax.lax.stop_gradient(wq - w)

        def _act_quant(x):
            scale = 127.0 / jnp.clip(jnp.max(jnp.abs(x), axis=-1, keepdims=True), 1e-05)
            xq = jnp.clip(jnp.round(x * scale), -128.0, 127.0) / scale
            return x + jax.lax.stop_gradient(xq - x)

        def _bitlinear(x, w):
            return jnp.einsum('bsi,oi->bso', _act_quant(x), _weight_quant(w))
        gate = jax.nn.silu(_bitlinear(x, w_gate))
        up = _bitlinear(x, w_up)
        return _bitlinear(gate * up, w_down)

    def _L1_xattn_ref(query, key, value):
        import jax, jax.numpy as jnp
        import numpy as np
        import math
        D_KEY = 128
        SCALE = math.sqrt(D_KEY)
        MASK_VAL = 10000000000.0
        scores = jnp.einsum('bqd,bkd->bqk', query, key)
        L = key.shape[1]
        tri = jnp.triu(jnp.ones((L, L), dtype=scores.dtype), k=1) * MASK_VAL
        scores = scores - tri[None, :, :]
        probs = jax.nn.softmax(scores / SCALE, axis=-1)
        return jnp.einsum('bqk,bkd->bqd', probs, value)

    def _L1_ffn_ref(x, attn_nw, attn_nb, wg, inter_w, inter_b, output_w, output_b, res_inter_w, res_inter_b, res_output_w, res_output_b, res_coef):
        import math
        import jax, jax.numpy as jnp
        import numpy as np
        HIDDEN = 128
        INTER = 512
        EXPERTS = 8
        B, T = (4, 256)
        EPS = 1e-12
        CAP_FACTOR = 1.0
        MIN_CAP = 4

        def layer_norm(x, g, b, eps=EPS):
            m = jnp.mean(x, axis=-1, keepdims=True)
            v = jnp.var(x, axis=-1, keepdims=True)
            return (x - m) * jax.lax.rsqrt(v + eps) * g + b

        def top1_gate(x, wg, capacity):
            logits = x @ wg
            gates = jax.nn.softmax(logits, axis=-1)
            E = wg.shape[-1]
            idx = jnp.argmax(gates, axis=-1)
            mask1 = jax.nn.one_hot(idx, E, dtype=gates.dtype)
            locations = jnp.cumsum(mask1, axis=0) - mask1
            mask1 = mask1 * (locations < capacity).astype(gates.dtype)
            gates1_s = jnp.sum(gates * mask1, axis=-1)
            loc_s = jnp.sum(locations * mask1, axis=-1).astype(jnp.int32)
            loc_oh = jax.nn.one_hot(loc_s, capacity, dtype=gates.dtype)
            combine = gates1_s[:, None, None] * mask1[:, :, None] * loc_oh[:, None, :]
            dispatch = jax.lax.stop_gradient((combine > 0).astype(x.dtype))
            return (combine, dispatch)
        Bx, Tx, M = x.shape
        S = Bx * Tx
        E = wg.shape[-1]
        capacity = max(MIN_CAP, math.ceil(S / E * CAP_FACTOR))
        residual = x.reshape(S, M)
        attn_out = layer_norm(residual, attn_nw, attn_nb)
        combine, dispatch = top1_gate(attn_out, wg, capacity)
        dispatched = jnp.einsum('sec,sm->ecm', dispatch, attn_out)
        h = jax.nn.gelu(jnp.einsum('ecm,emi->eci', dispatched, inter_w) + inter_b[:, None, :], approximate=True)
        expert_out = jnp.einsum('eci,eim->ecm', h, output_w) + output_b[:, None, :]
        moe_out = jnp.einsum('sec,ecm->sm', combine, expert_out)
        rh = jax.nn.gelu(attn_out @ res_inter_w + res_inter_b, approximate=True)
        res_mlp_out = rh @ res_output_w + res_output_b
        coef = jax.nn.softmax(attn_out @ res_coef, axis=-1)
        out = res_mlp_out * coef[:, :1] + moe_out * coef[:, 1:]
        out = out + residual
        return out.reshape(Bx, Tx, M)
    x = x + jnp.tanh(g_xattn[0]) * _L0_xattn_ref(_layernorm(x, axis=-1), ctx_1024, ctx_1024, L0_xattn_W_q, L0_xattn_W_k, L0_xattn_W_v, L0_xattn_W_o, L0_xattn_b_o)
    x = x + jnp.tanh(g_ffn[0]) * _L0_ffn_ref(_layernorm(x, axis=-1), L0_ffn_w_gate, L0_ffn_w_up, L0_ffn_w_down)
    x = x + jnp.tanh(g_xattn[1]) * _L1_xattn_ref(_layernorm(x, axis=-1), ctx_1024, ctx_1024)
    x = x + jnp.tanh(g_ffn[1]) * _L1_ffn_ref(_layernorm(x, axis=-1), L1_ffn_attn_nw, L1_ffn_attn_nb, L1_ffn_wg, L1_ffn_inter_w, L1_ffn_inter_b, L1_ffn_output_w, L1_ffn_output_b, L1_ffn_res_inter_w, L1_ffn_res_inter_b, L1_ffn_res_output_w, L1_ffn_res_output_b, L1_ffn_res_coef)
    return x

_drawn_inputs = setup_inputs


def setup_inputs(seed=0):
    import zlib

    import numpy as np

    out = dict(_drawn_inputs(seed))
    spreads = {'g_ffn': (-1.0, 0.2),
     'L0_xattn_b_o': (0.0, 0.1),
     'L1_ffn_attn_nw': (1.0, 0.6),
     'L1_ffn_attn_nb': (0.0, 0.683),
     'L1_ffn_inter_b': (0.0, 0.8),
     'L1_ffn_output_b': (0.0, 0.417),
     'L1_ffn_res_inter_b': (0.0, 0.276),
     'L1_ffn_res_output_b': (0.0, 0.1)}
    factors = {'L1_ffn_inter_w': 5.429, 'L1_ffn_output_w': 4.884}
    for name, (base, spread) in spreads.items():
        noise = np.random.default_rng([zlib.crc32(name.encode()), seed]).standard_normal(out[name].shape)
        drawn = base * np.exp(spread * noise) if base else spread * noise
        out[name] = jnp.asarray(drawn.astype(out[name].dtype))
    for name, factor in factors.items():
        out[name] = (out[name] * factor).astype(out[name].dtype)
    return out
```

```python
from contextlib import ExitStack

import numpy as np

import concourse.bass as bass
from concourse import mybir

F32 = mybir.dt.float32
BF16 = mybir.dt.bfloat16
I32 = mybir.dt.int32
ALU = mybir.AluOpType
ACT = mybir.ActivationFunctionType
AX = mybir.AxisListType

P = 128
NB = 8
T = NB * P
H, DK = 16, 8
HU = 4
NU = H // HU
FI = 512
NC = FI // P
E = 8
CAP = T // E
ROWS = 6 * DK
MROW = 3
SLOTS = 32
EPS = 1e-5
EPS_IN = 1e-12
ROUND = 12582912.0
NEG = -1e30
QMAX = 127.0


def gated_flamingo(nc, a):
    ctx = ExitStack()
    with ctx:
        def sb(name, shape, dt=F32):
            return ctx.enter_context(nc.sbuf_tensor(name, shape, dt))

        def sem(name):
            return ctx.enter_context(nc.semaphore(name))

        def dram(name, shape, dt):
            return nc.dram_tensor(name, shape, dt, kind="Internal").ap()

        bank = [ctx.enter_context(nc.psum_tensor(f"bank{i}", [P, 512], F32)) for i in range(8)]
        S_BANK, ST_BANK = bank[0:2], bank[2:4]
        O_BANK, W_BANK = bank[4], bank[5]
        F_BANK, G_BANK = bank[6], bank[7]

        q_dram = dram("q_dram", [2, P, 3, 512], BF16)
        k_dram = dram("k_dram", [2, P, 3, 512], BF16)
        m_dram = dram("m_dram", [NB, ROWS, P], BF16)
        disp_dram = dram("disp_dram", [E * CAP, P], F32)
        y_dram = dram("y_dram", [E * CAP, P], F32)

        x = sb("x", [P, NB, P])
        ctx_tok = sb("ctx_tok", [P, NB, P])
        ctx_t = sb("ctx_t", [P, T])
        wq, wk, wv, wo = (sb(n, [P, P]) for n in ("wq", "wk", "wv", "wo"))
        bo = sb("bo", [P, P])
        g4 = sb("g4", [P, 4])
        tg = sb("tg", [P, 4])
        w_raw = sb("w_raw", [P, 3, FI])
        w_tern = sb("w_tern", [P, 3, FI], BF16)
        w_sum = sb("w_sum", [P, 3])
        w_step = sb("w_step", [P, 4])
        w_inv = sb("w_inv", [P, 3])
        ident = sb("ident", [P, P])
        ident_b = sb("ident_b", [P, P], BF16)
        ones = sb("ones", [P, P])
        ones_b = sb("ones_b", [P, P], BF16)
        before_b = sb("before_b", [P, P], BF16)
        mask_b = sb("mask_b", [P, P], BF16)
        mask1 = sb("mask1", [P, P])
        half_neg = sb("half_neg", [P, NB])
        ranks = sb("ranks", [P, E])
        zeros = sb("zeros", [P, T])
        nw = sb("nw", [P, 1])
        nb = sb("nb", [P, 1])
        wgc = sb("wgc", [P, E + 2])
        ri = sb("ri", [P, FI])
        rib = sb("rib", [P, NC])
        ro = sb("ro", [P, NC, P])
        rob = sb("rob", [P, P])
        iw = sb("iw", [P, E, FI])
        ib = sb("ib", [P, E, NC])
        ow = sb("ow", [P, E, NC, P])
        ob = sb("ob", [P, E, P])

        st0 = sb("st0", [P, NB, 6])
        mv0 = sb("mv0", [P, NB, 2])
        rs0 = sb("rs0", [P, NB])
        xn = sb("xn", [P, NB, P])
        xn_t = sb("xn_t", [P, T])
        part = sb("part", [P, 4, 3, 512], BF16)
        rest = sb("rest", [P, 2, 512])
        q_st = sb("q_st", [P, NB, T], BF16)
        k_st = sb("k_st", [P, NB, T], BF16)
        v_st = sb("v_st", [P, NB, H, SLOTS])
        nmax = sb("nmax", [P, 2, 2, NB])
        nm_r = sb("nm_r", [P, 2, NB])
        nm_p = sb("nm_p", [P, 2, 2, MROW, NB], BF16)
        nm_t = sb("nm_t", [ROWS, 2, P], BF16)
        pr = sb("pr", [P, 4, HU, P])
        o_sb = sb("o_sb", [P, 2, 512])
        rsum = sb("rsum", [P, 2, H])
        c_tok = sb("c_tok", [P, 2, H, DK])
        c_t = sb("c_t", [P, 2, P])

        st = sb("st", [P, 3, 2, 6])
        mv = sb("mv", [P, 3, 2, 2])
        rs = sb("rs", [P, 3, 2, 1])
        ve = sb("ve", [P, 3, 2, 1])
        fx = sb("fx", [P, 2, P])
        fr = sb("fr", [P, 2, P])
        fq = sb("fq", [P, 2, P], BF16)
        fq_t = sb("fq_t", [P, 2, P], BF16)
        fa = sb("fa", [P, 2, 8])
        sg = sb("sg", [P, 2, FI])
        ft = sb("ft", [P, 2, FI])
        ftr = sb("ftr", [P, FI])
        ftq = sb("ftq", [P, 2, FI], BF16)
        ftq_t = sb("ftq_t", [P, 2, NC, P], BF16)
        ax = sb("ax", [P, 2, P])
        ax_t = sb("ax_t", [P, 2, P])
        asc = sb("asc", [P, 2, P])
        ap_ = sb("ap_", [P, 2, P])
        ap_t = sb("ap_t", [P, 2, P])
        am = sb("am", [P, 2, 5])
        r_tok = sb("r_tok", [P, 2, P])
        z_tok = sb("z_tok", [P, NB, P])
        a_t = sb("a_t", [P, T])
        v1 = sb("v1", [P, 2, 3])
        rs2 = sb("rs2", [P, 2, 1])
        lg = sb("lg", [P, NB, E + 2])
        gm = sb("gm", [P, NB, 2])
        ge = sb("ge", [P, NB, E + 2])
        gs = sb("gs", [P, NB, 2])
        gv = sb("gv", [P, NB, E])
        gvm = sb("gvm", [P, NB])
        onehot = sb("onehot", [P, NB, E])
        onehot_b = sb("onehot_b", [P, NB, E], BF16)
        gl = sb("gl", [P, NB, E])
        loc = sb("loc", [P, NB])
        keep = sb("keep", [P, NB])
        slot = sb("slot", [P, NB])
        drop = sb("drop", [P, NB])
        put_f = sb("put_f", [P, NB])
        get_f = sb("get_f", [P, NB])
        put_i = sb("put_i", [P, NB], I32)
        get_i = sb("get_i", [P, NB], I32)
        coef = sb("coef", [P, 2, NB])
        gk = sb("gk", [P, NB])
        rh = q_st[:, :, :].rearrange("p h t -> p (h t)").bitcast(F32).rearrange(
            "p (c t) -> p c t", c=NC)
        disp, d_t = xn, xn_t[:, :].rearrange("p (e t) -> p e t", e=E)
        h_t = sb("h_t", [P, 2, NC, P])
        y = sb("y", [P, E, P])
        moe = sb("moe", [P, NB, P])

        names = """x_in0 x_in1 ctx_in wk_in wq_in wv_in small_in wffn_in ctxtok_in late_in iw_in ow_in
            zero_out consts pool_step dve_step act_step tanh_done
            ln0_var ln0_rstd ln0_done xt_ready xt_copied proj_ready part_h rest1 rest2 part_m part_l
            v_ready v_copied v_ones vst_zero kst_ones k_out q_out k_loaded q_loaded0 q_loaded1 bo_added
            wsum_ready wsum_all tern_ready
            s_ready max_done nm_split nmt_ready nm_copied m_out m_loaded0 m_loaded1
            st_ready exp_done masked pv_done o_copied ot_ready c_norm ct_ready ct_copied wo_ready
            x1_done
            f_var f_rstd fq_ready fqt_ready fqt_copied gate_ready up_ready silu_done ftq_ready
            ftt_ready ftt_copied down_ready x2_done
            a_var a_rstd ax_ready axt_ready axt_copied as_ready asc_ready p_done pt_ready pt_copied
            av_ready x3_done
            e_var e_rstd e_var2 e_rstd2 z_ready zt_ready at_ready lg_ready lg_copied x4_done
            lg_max g_exp onehot_ready loc_ready idx_ready coef_ready
            r1_ready rh_ready put_out disp_in dt_ready dt_copied h_ready h_done y_ready y_done y_out
            get_in r2_ready x5_done x6_done final_out""".split()
        s = {n: sem(n) for n in names}

        block = ctx.enter_context(nc.Block())
        STEPS = NB + 5

        def stage(i, lag):
            b = i - lag
            return b if 0 <= b < NB else None

        A, B, C, F, D, R = range(6)

        def unit_cols(u):
            return u % 2, (u // 2) * HU

        @block.sync
        def _(sp):
            for half in range(2):
                sl = slice(half * NB // 2, (half + 1) * NB // 2)
                sp.dma_start(x[:, sl, :], a["x"][:, sl, :]).then_inc(s[f"x_in{half}"], 16)
            sp.dma_start(ctx_t[:, :], a["ctx_t"]).then_inc(s["ctx_in"], 16)
            sp.dma_start(wk[:, :], a["wk"]).then_inc(s["wk_in"], 16)
            sp.dma_start(wq[:, :], a["wq"]).then_inc(s["wq_in"], 16)
            sp.dma_start(wv[:, :], a["wv"]).then_inc(s["wv_in"], 16)
            for dst, src in ((g4[:, 0:2], a["gx"].partition_broadcast(P)),
                             (g4[:, 2:4], a["gf"].partition_broadcast(P)),
                             (bo[:, :], a["bo"].partition_broadcast(P)), (wo[:, :], a["wo"])):
                sp.dma_start(dst, src).then_inc(s["small_in"], 16)
            for n, w in enumerate(("w_gate", "w_up", "w_down")):
                sp.dma_start(w_raw[:, n, :], a[w]).then_inc(s["wffn_in"], 16)

            def stack(dst, src, half, order, sem_):
                for side in range(2):
                    row, p = 0, 0
                    while p < 6:
                        n = 1
                        while p + n < 6 and order[p + n] == order[p] + n:
                            n += 1
                        for k in range(n):
                            pass
                        v = src[half].rearrange("(s hp d) p t -> s p d hp t", s=2, d=DK)[side]
                        o = dst[64 * side + DK * row:64 * side + DK * (row + n), :,
                                512 * half:512 * half + 512]
                        for k in range(n):
                            sp.dma_start(o[DK * k:DK * (k + 1)], v[order[p] + k]).then_inc(sem_, 16)
                        p += n
                        row += n

            sp.wait_ge(s["kst_ones"], 2)
            for half in range(2):
                sp.wait_ge(s["part_l"], half + 1)
                sp.dma_start(k_dram[half], part[:, half, :, :]).then_inc(s["k_out"], 16)
                sp.wait_ge(s["k_out"], 16 * (half + 1))
                stack(k_st, k_dram, half, K_ORDER, s["k_loaded"])
            for half in range(2):
                sp.wait_ge(s["part_l"], half + 3)
                sp.dma_start(q_dram[half], part[:, 2 + half, :, :]).then_inc(s["q_out"], 16)
                sp.wait_ge(s["q_out"], 16 * (half + 1))
                stack(q_st, q_dram, half, Q_ORDER, s[f"q_loaded{half}"])
            sp.dma_start(ctx_tok[:, :, :], a["ctx_tok"]).then_inc(s["ctxtok_in"], 16)
            for dst, src in ((nw[:, :], a["nw"]), (nb[:, :], a["nb"]), (wgc[:, 0:E], a["wg"]),
                             (wgc[:, E:E + 2], a["coef"]), (ri[:, :], a["ri"]), (rib[:, :], a["rib"]),
                             (ro[:, :, :], a["ro"]), (rob[:, :], a["rob"].partition_broadcast(P)),
                             (ib[:, :, :], a["ib"]), (ob[:, :, :], a["ob"].partition_broadcast(P))):
                sp.dma_start(dst, src).then_inc(s["late_in"], 16)
            sp.wait_ge(s["vst_zero"], 2)
            sp.dma_start(disp_dram.rearrange("(p c) d -> p (c d)", p=P), zeros[:, :]).then_inc(
                s["zero_out"], 16)
            for b in range(NB):
                sp.wait_ge(s["nm_copied"], b + 1)
                sp.dma_start(m_dram[b], nm_t[:, b % 2, :]).then_inc(s["m_out"], 16)
                sp.wait_ge(s["m_out"], 16 * (b + 1))
                for side in range(2):
                    sp.dma_start(q_st[64 * side + ROWS:64 * side + ROWS + MROW, :, P * b:P * b + P],
                                 m_dram[b].rearrange("(s c hp) t -> s c hp t", s=2, c=MROW)[side]
                                 ).then_inc(s[f"m_loaded{b % 2}"], 16)
                if b == 1:
                    sp.dma_start(iw[:, :, :], a["iw"]).then_inc(s["iw_in"], 16)
                if b == 2:
                    sp.dma_start(ow[:, :, :, :], a["ow"]).then_inc(s["ow_in"], 16)
            sp.wait_ge(s["put_out"], 16 * NB)
            sp.dma_start(disp[:, :, :], disp_dram.rearrange("(e p) d -> p e d", p=P)).then_inc(
                s["disp_in"], 16)
            for e in range(E):
                sp.wait_ge(s["y_done"], e + 1)
                sp.dma_start(y_dram[CAP * e:CAP * e + CAP, :], y[:, e, :]).then_inc(s["y_out"], 16)
            for b in range(NB):
                sp.wait_ge(s["x6_done"], b + 1)
                sp.dma_start(a["out"][:, b, :], x[:, b, :]).then_inc(s["final_out"], 16)
            sp.wait_ge(s["final_out"], 16 * NB)

        @block.gpsimd
        def _(g):
            steps = [0]

            def then(ins):
                steps[0] += 1
                ins.then_inc(s["pool_step"], 1)
                g.wait_ge(s["pool_step"], steps[0])

            g.memset(half_neg[:, :], -0.5).then_inc(s["consts"], 1)
            g.memset(ones[:, :], 1.0).then_inc(s["consts"], 1)
            then(g.memset(ident[:, :], 0.0))
            g.affine_select(out=ident[:, :], in_=ident[:, :], compare_op=ALU.not_equal, fill=1.0,
                            base=0, pattern=[[-1, P]], channel_multiplier=1).then_inc(s["consts"], 1)

            for half in range(2):
                sl = slice(half * NB // 2, (half + 1) * NB // 2)
                g.wait_ge(s["ln0_var"], half + 1)
                then(g.tensor_scalar(rs0[:, sl], mv0[:, sl, 1], EPS, None, ALU.add))
                g.tensor_tensor(rs0[:, sl], rs0[:, sl], half_neg[:, 0:NB // 2], ALU.pow).then_inc(
                    s["ln0_rstd"], 1)
            g.wait_ge(s["ln0_rstd"], 2)
            for n, r in enumerate((32, 96)):
                if n:
                    g.wait_ge(s["kst_ones"], n)
                g.memset(k_st[r:r + 32, :, :], 1.0).then_inc(s["kst_ones"], 1)
            g.wait_ge(s["kst_ones"], 2)
            g.memset(v_st[:, :, :, :], 0.0).then_inc(s["vst_zero"], 1)
            g.memset(zeros[:, :], 0.0).then_inc(s["vst_zero"], 1)
            g.wait_ge(s["vst_zero"], 1)
            g.memset(v_st[:, :, :, DK], 1.0).then_inc(s["v_ones"], 1)
            then(g.memset(ident_b[:, :], 0.0))
            g.affine_select(out=ident_b[:, :], in_=ident_b[:, :], compare_op=ALU.not_equal, fill=1.0,
                            base=0, pattern=[[-1, P]], channel_multiplier=1).then_inc(s["consts"], 1)
            then(g.memset(mask_b[:, :], 0.0))
            g.affine_select(out=mask_b[:, :], in_=mask_b[:, :], compare_op=ALU.is_ge, fill=NEG,
                            base=0, pattern=[[-1, P]], channel_multiplier=1).then_inc(
                                s["consts"], 1)
            then(g.memset(mask1[:, :], 0.0))
            g.affine_select(out=mask1[:, :], in_=mask1[:, :], compare_op=ALU.is_ge, fill=-1e10,
                            base=0, pattern=[[-1, P]], channel_multiplier=1).then_inc(s["consts"], 1)
            g.wait_ge(s["tanh_done"], 1)
            then(g.tensor_scalar(bo[:, :], bo[:, :], tg[:, 0:1], None, ALU.mult))
            g.wait_ge(s["ln0_done"], NB)
            for b in range(NB):
                g.tensor_tensor(x[:, b, :], x[:, b, :], bo[:, :], ALU.add).then_inc(s["bo_added"], 1)
            then(g.memset(ones_b[:, :], 1.0))
            g.affine_select(out=before_b[:, :], in_=ones_b[:, :], compare_op=ALU.is_ge, fill=0.0,
                            base=-1, pattern=[[1, P]], channel_multiplier=-1).then_inc(s["consts"], 1)
            for e in range(E):
                g.memset(ranks[:, e:e + 1], float(E - e)).then_inc(s["consts"], 1)

            def mask_unit(b, u):
                n = NU * b + u
                g.wait_ge(s["exp_done"], n + 1)
                g.affine_select(out=pr[:, n % 4, :, :], in_=pr[:, n % 4, :, :], compare_op=ALU.is_ge,
                                fill=0.0, base=0, pattern=[[0, HU], [1, P]],
                                channel_multiplier=-1).then_inc(s["masked"], 1)

            def rstd(k, b, var_sem, out_sem):
                g.wait_ge(s[var_sem], b + 1)
                then(g.tensor_scalar(ve[:, k, b % 2, :], mv[:, k, b % 2, 1:2], EPS, None, ALU.add))
                g.tensor_tensor(rs[:, k, b % 2, :], ve[:, k, b % 2, :], half_neg[:, 0:1],
                                ALU.pow).then_inc(s[out_sem], 1)

            for i in range(STEPS):
                b1, c, f, d, r = (stage(i, k) for k in (B, C, F, D, R))
                if b1 is not None:
                    mask_unit(b1, 0)
                if c is not None:
                    rstd(0, c, "f_var", "f_rstd")
                if b1 is not None:
                    mask_unit(b1, 1)
                if f is not None:
                    rstd(1, f, "a_var", "a_rstd")
                if b1 is not None:
                    mask_unit(b1, 2)
                if d is not None:
                    rstd(2, d, "e_var", "e_rstd")
                    g.wait_ge(s["e_var2"], d + 1)
                    g.tensor_tensor(rs2[:, d % 2, :], v1[:, d % 2, 2:3], half_neg[:, 0:1],
                                    ALU.pow).then_inc(s["e_rstd2"], 1)
                if b1 is not None:
                    mask_unit(b1, 3)

            g.wait_ge(s["idx_ready"], 1)
            g.wait_ge(s["zero_out"], 16)
            for b in range(NB):
                g.indirect_dma_start(
                    out=disp_dram, out_offset=bass.IndirectOffsetOnAxis(ap=put_i[:, b:b + 1], axis=0),
                    in_=z_tok[:, b, :], in_offset=None, bounds_check=E * CAP - 1,
                    oob_is_err=False).then_inc(s["put_out"], 16)
            g.wait_ge(s["y_out"], 16 * E)
            for b in range(NB):
                g.indirect_dma_start(
                    out=moe[:, b, :], out_offset=None, in_=y_dram,
                    in_offset=bass.IndirectOffsetOnAxis(ap=get_i[:, b:b + 1], axis=0),
                    bounds_check=E * CAP - 1, oob_is_err=False).then_inc(s["get_in"], 16)

        @block.scalar
        def _(act):
            def part_h(n):
                act.wait_ge(s["proj_ready"], n + 1)
                act.copy(part[:, n, 0, :], PROJ[n]).then_inc(s["part_h"], 1)

            def part_m(n):
                act.wait_ge(s["rest1"], n + 1)
                act.copy(part[:, n, 1, :], rest[:, n % 2, :]).then_inc(s["part_m"], 1)

            PROJ = [bank[0][:, :], bank[1][:, :], bank[2][:, :], bank[3][:, :]]
            act.wait_ge(s["small_in"], 64)
            act.activation(tg[:, :], g4[:, :], ACT.Tanh).then_inc(s["tanh_done"], 1)
            for n in range(2):
                part_h(n)
                part_m(n)
            for half in range(2):
                act.wait_ge(s["xt_ready"], half + 1)
                act.copy(xn_t[:, 512 * half:512 * half + 512], bank[4 + half][:, :]).then_inc(
                    s["xt_copied"], 1)
            for n in range(2, 4):
                part_h(n)
                part_m(n)
            act.wait_ge(s["v_ones"], 1)
            for half in range(2):
                act.wait_ge(s["v_ready"], half + 1)
                act.copy(v_st[:, 4 * half:4 * half + 4, :, 0:DK],
                         bank[6 + half][:, :].rearrange("p (b h d) -> p b h d", b=4, d=DK)).then_inc(
                             s["v_copied"], 1)

            def exp_unit(b, u):
                n = NU * b + u
                act.wait_ge(s["st_ready"], n + 1)
                if n >= 4:
                    act.wait_ge(s["pv_done"], n - 3)
                act.activation(pr[:, n % 4, :, :],
                               ST_BANK[n % 2][:, :].rearrange("p (j q) -> p j q", j=HU), ACT.Exp,
                               scale=float(DK) ** -0.5).then_inc(s["exp_done"], 1)

            def copy_o(b):
                act.wait_ge(s["pv_done"], NU * (b + 1))
                if b >= 2:
                    act.wait_ge(s["ot_ready"], b - 1)
                act.copy(o_sb[:, b % 2, :], O_BANK[:, :]).then_inc(s["o_copied"], 1)

            def copy_ct(b):
                act.wait_ge(s["ct_ready"], b + 1)
                if b >= 2:
                    act.wait_ge(s["wo_ready"], b - 1)
                act.copy(c_t[:, b % 2, :], W_BANK[:, 0:P]).then_inc(s["ct_copied"], 1)

            def copy_fq(b):
                act.wait_ge(s["fqt_ready"], b + 1)
                if b >= 2:
                    act.wait_ge(s["up_ready"], b - 1)
                act.copy(fq_t[:, b % 2, :], F_BANK[:, 0:P // 2].bitcast(BF16)).then_inc(
                    s["fqt_copied"], 1)

            def silu(b):
                act.wait_ge(s["gate_ready"], b + 1)
                if b >= 2:
                    act.wait_ge(s["ftq_ready"], b - 1)
                act.activation(sg[:, b % 2, :], F_BANK[:, :], ACT.Silu,
                               scale=fa[:, b % 2, 3:4]).then_inc(s["silu_done"], 1)

            def copy_ft(b):
                act.wait_ge(s["ftt_ready"], b + 1)
                if b >= 2:
                    act.wait_ge(s["down_ready"], b - 1)
                act.copy(ftq_t[:, b % 2, :, :], G_BANK[:, 0:FI // 2].bitcast(BF16).rearrange(
                    "p (c t) -> p c t", c=NC)).then_inc(s["ftt_copied"], 1)

            def copy_ax(b):
                act.wait_ge(s["axt_ready"], b + 1)
                if b >= 2:
                    act.wait_ge(s["as_ready"], b - 1)
                act.copy(ax_t[:, b % 2, :], F_BANK[:, 0:P]).then_inc(s["axt_copied"], 1)

            def exp1(b):
                act.wait_ge(s["asc_ready"], b + 1)
                if b >= 2:
                    act.wait_ge(s["pt_ready"], b - 1)
                    act.wait_ge(s["x3_done"], b - 1)
                act.activation(ap_[:, b % 2, :], asc[:, b % 2, :], ACT.Exp, bias=am[:, b % 2, 1:2],
                               scale=float(P) ** -0.5, accum_out=am[:, b % 2, 2:3]).then_inc(
                                   s["p_done"], 1)

            def copy_pt(b):
                act.wait_ge(s["pt_ready"], b + 1)
                if b >= 2:
                    act.wait_ge(s["av_ready"], b - 1)
                act.copy(ap_t[:, b % 2, :], F_BANK[:, 0:P]).then_inc(s["pt_copied"], 1)

            def copy_at(b):
                act.wait_ge(s["zt_ready"], b + 1)
                act.activation(a_t[:, P * b:P * b + P], G_BANK[:, 0:P], ACT.Identity,
                               bias=nb[:, 0:1], scale=nw[:, 0:1]).then_inc(s["at_ready"], 1)

            def copy_lg(b):
                act.wait_ge(s["lg_ready"], b + 1)
                act.copy(lg[:, b, :], G_BANK[:, 128:128 + E + 2]).then_inc(s["lg_copied"], 1)

            act.wait_ge(s["late_in"], 160)
            for i in range(STEPS):
                b1, c, f, d, r = (stage(i, k) for k in (B, C, F, D, R))
                if f is not None:
                    copy_fq(f)
                if b1 is not None:
                    exp_unit(b1, 0)
                if f is not None:
                    silu(f)
                if d is not None:
                    copy_ax(d)
                if c is not None:
                    copy_ct(c)
                if b1 is not None:
                    exp_unit(b1, 1)
                if f is not None:
                    copy_ft(f)
                if b1 is not None:
                    exp_unit(b1, 2)
                if d is not None:
                    exp1(d)
                    copy_pt(d)
                if r is not None:
                    copy_at(r)
                if b1 is not None:
                    exp_unit(b1, 3)
                if r is not None:
                    copy_lg(r)
                if b1 is not None:
                    copy_o(b1)

            act.wait_ge(s["lg_max"], 1)
            act.activation(ge[:, :, :], lg[:, :, :], ACT.Exp).then_inc(s["g_exp"], 1)

            for n in range(2 * NC):
                half, k = n // NC, n % NC
                act.wait_ge(s["r1_ready"], n + 1)
                act.activation(rh[:, k, 512 * half:512 * half + 512], bank[n % 4][:, :],
                               ACT.Gelu_apprx_tanh, bias=rib[:, k:k + 1]).then_inc(s["rh_ready"], 1)
            for half in range(2):
                act.wait_ge(s["dt_ready"], half + 1)
                act.activation(d_t[:, 4 * half:4 * half + 4, :],
                               bank[4 + half][:, :].rearrange("p (e t) -> p e t", e=4), ACT.Identity,
                               bias=nb[:, 0:1], scale=nw[:, 0:1]).then_inc(s["dt_copied"], 1)
            for e in range(E):
                act.wait_ge(s["h_ready"], e + 1)
                if e >= 2:
                    act.wait_ge(s["y_ready"], e - 1)
                for k in range(NC):
                    act.activation(h_t[:, e % 2, k, :], bank[e % 2][:, P * k:P * k + P],
                                   ACT.Gelu_apprx_tanh, bias=ib[:, e, k:k + 1]).then_inc(
                                       s["h_done"], 1)

        @block.vector
        def _(v):
            steps = [0]

            def then(ins):
                steps[0] += 1
                ins.then_inc(s["dve_step"], 1)
                v.wait_ge(s["dve_step"], steps[0])

            def ln0_stats(half):
                v.wait_ge(s[f"x_in{half}"], 16)
                for b in range(4 * half, 4 * half + 4):
                    then(v.bn_stats(st0[:, b, :], x[:, b, :]))
                    ins = v.bn_aggr(mv0[:, b, :], st0[:, b, :])
                    if b % 4 == 3:
                        ins.then_inc(s["ln0_var"], 1)
                    else:
                        then(ins)

            def ln0_norm(half):
                v.wait_ge(s["ln0_rstd"], half + 1)
                for b in range(4 * half, 4 * half + 4):
                    v.tensor_scalar(xn[:, b, :], x[:, b, :], mv0[:, b, 0:1], rs0[:, b:b + 1],
                                    ALU.subtract, ALU.mult).then_inc(s["ln0_done"], 1)

            def parts(n):
                v.wait_ge(s["part_h"], n + 1)
                if n >= 2:
                    v.wait_ge(s["part_m"], n - 1)
                v.tensor_tensor(rest[:, n % 2, :], bank[n][:, :], part[:, n, 0, :],
                                ALU.subtract).then_inc(s["rest1"], 1)
                v.wait_ge(s["part_m"], n + 1)
                v.tensor_tensor(part[:, n, 2, :], rest[:, n % 2, :], part[:, n, 1, :],
                                ALU.subtract).then_inc(s["part_l"], 1)

            ln0_stats(0)
            ln0_stats(1)
            ln0_norm(0)
            ln0_norm(1)
            for n in range(4):
                parts(n)

            v.wait_ge(s["wffn_in"], 48)
            v.tensor_reduce(w_sum[:, :], w_raw[:, :, :], AX.X, ALU.add,
                            apply_absolute_value=True).then_inc(s["wsum_ready"], 1)
            v.wait_ge(s["wsum_all"], 1)
            then(v.tensor_scalar(w_step[:, 0:3], bank[4][:, 0:3], 1.0 / (P * FI), EPS, ALU.mult,
                                 ALU.max))
            then(v.reciprocal(w_inv[:, :], w_step[:, 0:3]))
            v.wait_ge(s["tanh_done"], 1)
            v.tensor_scalar(w_step[:, 3:4], w_step[:, 2:3], tg[:, 2:3], None, ALU.mult).then_inc(
                s["dve_step"], 1)
            for n in range(3):
                v.tensor_scalar(w_raw[:, n, :], w_raw[:, n, :], w_inv[:, n:n + 1], 1.0, ALU.mult,
                                ALU.min).then_inc(s["dve_step"], 1)
            steps[0] += 4
            v.wait_ge(s["dve_step"], steps[0])
            then(v.tensor_scalar(w_raw[:, :, :], w_raw[:, :, :], -1.0, ROUND, ALU.max, ALU.add))
            v.tensor_scalar(w_tern[:, :, :], w_raw[:, :, :], -ROUND, None, ALU.add).then_inc(
                s["tern_ready"], 1)

            def max_unit(b, u):
                n = NU * b + u
                side, hp = unit_cols(u)
                v.wait_ge(s["s_ready"], n + 1)
                v.tensor_reduce(nmax[:, b % 2, side, hp:hp + HU],
                                S_BANK[n % 2][:, :].rearrange("p (j k) -> p j k", j=HU), AX.X,
                                ALU.max, negate=True).then_inc(s["max_done"], 1)

            def split_max(b):
                v.wait_ge(s["max_done"], NU * (b + 1))
                if b >= 2:
                    v.wait_ge(s["nmt_ready"], b - 1)
                p_, m_ = nm_p[:, b % 2], nmax[:, b % 2]
                then(v.tensor_copy(p_[:, :, 0, :], m_))
                then(v.tensor_tensor(nm_r[:, :, :], m_, p_[:, :, 0, :], ALU.subtract))
                then(v.tensor_copy(p_[:, :, 1, :], nm_r[:, :, :]))
                v.tensor_tensor(p_[:, :, 2, :], nm_r[:, :, :], p_[:, :, 1, :],
                                ALU.subtract).then_inc(s["nm_split"], 1)

            def copy_nm(b):
                v.wait_ge(s["nmt_ready"], b + 1)
                if b >= 2:
                    v.wait_ge(s["m_out"], 16 * (b - 1))
                v.tensor_copy(nm_t[:, b % 2, :], S_BANK[0][0:ROWS, 0:P // 2].bitcast(BF16)).then_inc(
                    s["nm_copied"], 1)

            def norm_c(b):
                o = W_BANK[:, :].rearrange("p (h c) -> p h c", c=SLOTS)
                v.wait_ge(s["ot_ready"], b + 1)
                if b >= 2:
                    v.wait_ge(s["ct_ready"], b - 1)
                then(v.reciprocal(rsum[:, b % 2, :], o[:, :, DK]))
                v.tensor_tensor(c_tok[:, b % 2], o[:, :, 0:DK],
                                rsum[:, b % 2, :].unsqueeze(2).to_broadcast([P, H, DK]),
                                ALU.mult).then_inc(s["c_norm"], 1)

            def x1(b):
                v.wait_ge(s["wo_ready"], b + 1)
                v.wait_ge(s["bo_added"], NB)
                v.scalar_tensor_tensor(x[:, b, :], W_BANK[:, P:2 * P], tg[:, 0:1], x[:, b, :],
                                       ALU.mult, ALU.add).then_inc(s["x1_done"], 1)

            def stats(k, b, x_sem, var_sem):
                v.wait_ge(s[x_sem], b + 1)
                then(v.bn_stats(st[:, k, b % 2, :], x[:, b, :]))
                v.bn_aggr(mv[:, k, b % 2, :], st[:, k, b % 2, :]).then_inc(s[var_sem], 1)

            def ffn_in(b):
                j = b % 2
                v.wait_ge(s["f_rstd"], b + 1)
                if b >= 2:
                    v.wait_ge(s["fqt_ready"], b - 1)
                    v.wait_ge(s["silu_done"], b - 1)
                then(v.tensor_scalar(fx[:, j, :], x[:, b, :], mv[:, 0, j, 0:1], rs[:, 0, j, :],
                                     ALU.subtract, ALU.mult))
                then(v.tensor_reduce(fa[:, j, 0:1], fx[:, j, :], AX.X, ALU.max,
                                     apply_absolute_value=True))
                then(v.tensor_scalar(fa[:, j, 1:2], fa[:, j, 0:1], EPS, 1.0 / QMAX, ALU.max,
                                     ALU.mult))
                then(v.reciprocal(fa[:, j, 2:3], fa[:, j, 1:2]))
                then(v.tensor_scalar(fr[:, j, :], fx[:, j, :], fa[:, j, 2:3], ROUND, ALU.mult,
                                     ALU.add))
                then(v.tensor_scalar(fa[:, j, 3:5], w_step[:, 0:2], fa[:, j, 1:2], None, ALU.mult))
                v.tensor_scalar(fq[:, j, :], fr[:, j, :], -ROUND, QMAX, ALU.add,
                                ALU.min).then_inc(s["fq_ready"], 1)

            def ffn_mid(b):
                j = b % 2
                v.wait_ge(s["up_ready"], b + 1)
                v.wait_ge(s["silu_done"], b + 1)
                if b >= 2:
                    v.wait_ge(s["ftt_ready"], b - 1)
                then(v.scalar_tensor_tensor(ft[:, j, :], G_BANK[:, :], fa[:, j, 4:5], sg[:, j, :],
                                            ALU.mult, ALU.mult))
                then(v.tensor_reduce(fa[:, j, 5:6], ft[:, j, :], AX.X, ALU.max,
                                     apply_absolute_value=True))
                then(v.tensor_scalar(fa[:, j, 6:7], fa[:, j, 5:6], EPS, 1.0 / QMAX, ALU.max,
                                     ALU.mult))
                then(v.reciprocal(fa[:, j, 7:8], fa[:, j, 6:7]))
                then(v.tensor_scalar(ftr[:, :], ft[:, j, :], fa[:, j, 7:8], ROUND, ALU.mult,
                                     ALU.add))
                then(v.tensor_scalar(fa[:, j, 0:1], fa[:, j, 6:7], w_step[:, 3:4], None, ALU.mult))
                v.tensor_scalar(ftq[:, j, :], ftr[:, :], -ROUND, QMAX, ALU.add, ALU.min).then_inc(
                    s["ftq_ready"], 1)

            def x2(b):
                v.wait_ge(s["down_ready"], b + 1)
                v.scalar_tensor_tensor(x[:, b, :], G_BANK[:, 256:256 + P], fa[:, b % 2, 0:1],
                                       x[:, b, :], ALU.mult, ALU.add).then_inc(s["x2_done"], 1)

            def att_in(b):
                v.wait_ge(s["a_rstd"], b + 1)
                if b >= 2:
                    v.wait_ge(s["axt_ready"], b - 1)
                v.tensor_scalar(ax[:, b % 2, :], x[:, b, :], mv[:, 1, b % 2, 0:1], rs[:, 1, b % 2, :],
                                ALU.subtract, ALU.mult).then_inc(s["ax_ready"], 1)

            def att_max(b):
                j = b % 2
                v.wait_ge(s["as_ready"], b + 1)
                if b >= 2:
                    v.wait_ge(s["p_done"], b - 1)
                then(v.tensor_tensor(asc[:, j, :], F_BANK[:, 128:256], mask1[:, :], ALU.add))
                then(v.tensor_reduce(am[:, j, 0:1], asc[:, j, :], AX.X, ALU.max))
                v.tensor_scalar(am[:, j, 1:2], am[:, j, 0:1], -float(P) ** -0.5, None,
                                ALU.mult).then_inc(s["asc_ready"], 1)

            def x3(b):
                j = b % 2
                v.wait_ge(s["p_done"], b + 1)
                then(v.reciprocal(am[:, j, 3:4], am[:, j, 2:3]))
                then(v.tensor_scalar(am[:, j, 4:5], am[:, j, 3:4], tg[:, 1:2], None, ALU.mult))
                v.wait_ge(s["av_ready"], b + 1)
                v.scalar_tensor_tensor(x[:, b, :], F_BANK[:, 256:384], am[:, j, 4:5], x[:, b, :],
                                       ALU.mult, ALU.add).then_inc(s["x3_done"], 1)

            def router_var(b):
                j = b % 2
                v.wait_ge(s["e_rstd"], b + 1)
                then(v.tensor_scalar(v1[:, j, 0:1], mv[:, 2, j, 1:2], rs[:, 2, j, :], None, ALU.mult))
                v.tensor_scalar(v1[:, j, 1:2], v1[:, j, 0:1], rs[:, 2, j, :], None,
                                ALU.mult).then_inc(s["dve_step"], 1)
                steps[0] += 1
                v.wait_ge(s["dve_step"], steps[0])
                v.tensor_scalar(v1[:, j, 2:3], v1[:, j, 1:2], EPS_IN, None, ALU.add).then_inc(
                    s["e_var2"], 1)
                v.tensor_scalar(r_tok[:, j, :], x[:, b, :], mv[:, 2, j, 0:1], rs[:, 2, j, :],
                                ALU.subtract, ALU.mult).then_inc(s["dve_step"], 1)
                steps[0] += 1

            def router_in(b):
                j = b % 2
                v.wait_ge(s["e_rstd2"], b + 1)
                v.wait_ge(s["dve_step"], steps[0])
                v.tensor_scalar(z_tok[:, b, :], r_tok[:, j, :], rs2[:, j, :], None,
                                ALU.mult).then_inc(s["z_ready"], 1)
                v.scalar_tensor_tensor(x[:, b, :], r_tok[:, j, :], tg[:, 3:4], x[:, b, :], ALU.mult,
                                       ALU.add).then_inc(s["x4_done"], 1)

            for i in range(STEPS):
                a0, b1, c, f, d, r = (stage(i, k) for k in (A, B, C, F, D, R))
                if c is not None:
                    norm_c(c)
                if a0 is not None:
                    max_unit(a0, 0)
                if f is not None:
                    ffn_mid(f)
                if a0 is not None:
                    max_unit(a0, 1)
                if c is not None:
                    x1(c)
                    stats(0, c, "x1_done", "f_var")
                if d is not None:
                    att_max(d)
                if a0 is not None:
                    max_unit(a0, 2)
                if c is not None:
                    ffn_in(c)
                if f is not None:
                    x2(f)
                    stats(1, f, "x2_done", "a_var")
                if a0 is not None:
                    max_unit(a0, 3)
                    split_max(a0)
                if f is not None:
                    att_in(f)
                if d is not None:
                    x3(d)
                    stats(2, d, "x3_done", "e_var")
                    router_var(d)
                if a0 is not None:
                    copy_nm(a0)
                if d is not None:
                    router_in(d)

            v.wait_ge(s["lg_copied"], NB)
            logit, clog = lg[:, :, 0:E], lg[:, :, E:E + 2]
            v.tensor_reduce(gm[:, :, 0], logit, AX.X, ALU.max).then_inc(s["dve_step"], 1)
            v.tensor_reduce(gm[:, :, 1], clog, AX.X, ALU.max).then_inc(s["dve_step"], 1)
            steps[0] += 2
            v.wait_ge(s["dve_step"], steps[0])
            then(v.tensor_tensor(gv[:, :, :], logit, gm[:, :, 0:1].to_broadcast([P, NB, E]),
                                 ALU.is_equal))
            then(v.tensor_tensor(gv[:, :, :], gv[:, :, :],
                                 ranks[:, :].unsqueeze(1).to_broadcast([P, NB, E]), ALU.mult))
            then(v.tensor_reduce(gvm[:, :], gv[:, :, :], AX.X, ALU.max))
            then(v.tensor_tensor(onehot[:, :, :], gv[:, :, :],
                                 gvm[:, :].unsqueeze(2).to_broadcast([P, NB, E]), ALU.is_equal))
            v.tensor_copy(onehot_b[:, :, :], onehot[:, :, :]).then_inc(s["onehot_ready"], 1)
            then(v.tensor_tensor(logit, logit, gm[:, :, 0:1].to_broadcast([P, NB, E]), ALU.subtract))
            v.tensor_tensor(clog, clog, gm[:, :, 1:2].to_broadcast([P, NB, 2]),
                            ALU.subtract).then_inc(s["lg_max"], 1)
            v.wait_ge(s["loc_ready"], 1)
            then(v.tensor_tensor(gl[:, :, :], bank[4][:, 0:NB * E].rearrange("p (b e) -> p b e", e=E),
                                 onehot[:, :, :], ALU.mult))
            then(v.tensor_reduce(loc[:, :], gl[:, :, :], AX.X, ALU.add))
            then(v.tensor_scalar(keep[:, :], loc[:, :], float(CAP), None, ALU.is_lt))
            then(v.scalar_tensor_tensor(slot[:, :], gvm[:, :], -float(CAP), loc[:, :], ALU.mult,
                                        ALU.add))
            then(v.tensor_scalar(slot[:, :], slot[:, :], float(E * CAP), None, ALU.add))
            then(v.tensor_scalar(drop[:, :], keep[:, :], -4.0 * E * CAP, 4.0 * E * CAP, ALU.mult,
                                 ALU.add))
            then(v.tensor_tensor(put_f[:, :], slot[:, :], drop[:, :], ALU.add))
            then(v.tensor_tensor(get_f[:, :], slot[:, :], keep[:, :], ALU.mult))
            then(v.tensor_copy(get_i[:, :], get_f[:, :]))
            v.tensor_copy(put_i[:, :], put_f[:, :]).then_inc(s["idx_ready"], 1)
            v.wait_ge(s["g_exp"], 1)
            v.tensor_reduce(gs[:, :, 0], ge[:, :, 0:E], AX.X, ALU.add).then_inc(s["dve_step"], 1)
            v.tensor_reduce(gs[:, :, 1], ge[:, :, E:E + 2], AX.X, ALU.add).then_inc(
                s["dve_step"], 1)
            steps[0] += 2
            v.wait_ge(s["dve_step"], steps[0])
            then(v.reciprocal(gs[:, :, :], gs[:, :, :]))
            then(v.tensor_scalar(gs[:, :, 1], gs[:, :, 1], tg[:, 3:4], None, ALU.mult))
            then(v.tensor_tensor(coef[:, 0, :], ge[:, :, E], gs[:, :, 1], ALU.mult))
            then(v.tensor_tensor(coef[:, 1, :], ge[:, :, E + 1], gs[:, :, 1], ALU.mult))
            then(v.tensor_tensor(gk[:, :], gs[:, :, 0], keep[:, :], ALU.mult))
            then(v.tensor_tensor(coef[:, 1, :], coef[:, 1, :], gk[:, :], ALU.mult))
            v.wait_ge(s["x4_done"], NB)
            for b in range(NB):
                v.scalar_tensor_tensor(x[:, b, :], rob[:, :], coef[:, 0, b:b + 1], x[:, b, :],
                                       ALU.mult, ALU.add).then_inc(s["coef_ready"], 1)

            for e in range(E):
                v.wait_ge(s["y_ready"], e + 1)
                v.tensor_tensor(y[:, e, :], bank[4 + e % 2][:, 0:P], ob[:, e, :], ALU.add).then_inc(
                    s["y_done"], 1)
            v.wait_ge(s["coef_ready"], NB)
            for b in range(NB):
                v.wait_ge(s["r2_ready"], b + 1)
                v.scalar_tensor_tensor(x[:, b, :], bank[(6, 7, 2, 3)[b % 4]][:, 0:P],
                                       coef[:, 0, b:b + 1], x[:, b, :], ALU.mult,
                                       ALU.add).then_inc(s["x5_done"], 1)
            for b in range(NB):
                v.wait_ge(s["x5_done"], b + 1)
                v.wait_ge(s["get_in"], 16 * NB)
                v.scalar_tensor_tensor(x[:, b, :], moe[:, b, :], coef[:, 1, b:b + 1], x[:, b, :],
                                       ALU.mult, ALU.add).then_inc(s["x6_done"], 1)

        @block.tensor
        def _(pe):
            pe.wait_ge(s["ctx_in"], 16)
            pe.wait_ge(s["wk_in"], 16)
            for half in range(2):
                pe.matmul(bank[half][:, :], wk[:, :], ctx_t[:, 512 * half:512 * half + 512],
                          start=True, stop=True).then_inc(s["proj_ready"], 1)
            pe.wait_ge(s["consts"], 3)
            pe.wait_ge(s["wq_in"], 16)
            for half in range(2):
                for b in range(4):
                    pe.wait_ge(s["ln0_done"], 4 * half + b + 1)
                    last = pe.transpose(bank[4 + half][:, P * b:P * b + P], xn[:, 4 * half + b, :],
                                        ident[:, :])
                last.then_inc(s["xt_ready"], 1)
                pe.wait_ge(s["xt_copied"], half + 1)
                pe.matmul(bank[2 + half][:, :], wq[:, :], xn_t[:, 512 * half:512 * half + 512],
                          start=True, stop=True).then_inc(s["proj_ready"], 1)
            pe.wait_ge(s["wv_in"], 16)
            for half in range(2):
                for b in range(4):
                    n = 4 * half + b
                    last = pe.matmul(bank[6 + half][:, P * b:P * b + P], ctx_t[:, P * n:P * n + P],
                                     wv[:, :], start=True, stop=True)
                last.then_inc(s["v_ready"], 1)
            pe.wait_ge(s["wsum_ready"], 1)
            pe.matmul(bank[4][:, 0:3], ones[:, :], w_sum[:, :], start=True, stop=True).then_inc(
                s["wsum_all"], 1)

            def scores(b, u):
                n = NU * b + u
                side, hp = unit_cols(u)
                if n < 2:
                    pe.wait_ge(s["part_l"], n + 1)
                else:
                    pe.wait_ge(s["max_done"], n - 1)
                if u == 0 and b > 0:
                    pe.wait_ge(s["nm_copied"], b)
                o = S_BANK[n % 2]
                rows = slice(64 * side, 64 * side + ROWS)
                for j in range(HU):
                    pe.matmul(o[:, P * j:P * j + P], ident_b[:, :], mask_b[:, :], start=True,
                              stop=False)
                    last = pe.matmul(o[:, P * j:P * j + P], q_st[rows, hp + j, P * b:P * b + P],
                                     k_st[rows, hp + j, P * b:P * b + P], start=False, stop=True)
                last.then_inc(s["s_ready"], 1)

            def turn_max(b):
                pe.wait_ge(s["nm_split"], b + 1)
                pe.transpose(S_BANK[0][0:ROWS, 0:P // 2].bitcast(BF16),
                             nm_p[:, b % 2].rearrange("p s c h -> p (s c h)"),
                             ident_b[:, :]).then_inc(s["nmt_ready"], 1)

            def scores_t(b, u):
                n = NU * b + u
                side, hp = unit_cols(u)
                if u == 0:
                    pe.wait_ge(s[f"m_loaded{b % 2}"], 32 * (b // 2 + 1))
                if n < 2:
                    pe.wait_ge(s["part_l"], n + 3)
                else:
                    pe.wait_ge(s["exp_done"], n - 1)
                o = ST_BANK[n % 2]
                for j in range(HU):
                    rows = slice(64 * side, 64 * side + ROWS + MROW)
                    last = pe.matmul(o[:, P * j:P * j + P], k_st[rows, hp + j, P * b:P * b + P],
                                     q_st[rows, hp + j, P * b:P * b + P], start=True, stop=True)
                last.then_inc(s["st_ready"], 1)

            def values(b, u):
                n = NU * b + u
                pe.wait_ge(s["masked"], n + 1)
                if u == 0 and b > 0:
                    pe.wait_ge(s["o_copied"], b)
                for j in range(HU):
                    last = pe.matmul(O_BANK[32 * j:32 * j + 32, P * u:P * u + P],
                                     v_st[:, b, HU * u + j, :], pr[:, n % 4, j, :], start=True,
                                     stop=True)
                last.then_inc(s["pv_done"], 1)

            def turn_o(b):
                pe.wait_ge(s["o_copied"], b + 1)
                if b > 0:
                    pe.wait_ge(s["x1_done"], b)
                for u in range(NU):
                    last = pe.transpose(W_BANK[:, P * u:P * u + P],
                                        o_sb[:, b % 2, P * u:P * u + P], ident[:, :])
                last.then_inc(s["ot_ready"], 1)

            def turn_c(b):
                pe.wait_ge(s["c_norm"], b + 1)
                pe.transpose(W_BANK[:, 0:P], c_tok[:, b % 2].rearrange("p h d -> p (h d)"),
                             ident[:, :]).then_inc(s["ct_ready"], 1)

            def out_proj(b):
                pe.wait_ge(s["ct_copied"], b + 1)
                pe.matmul(W_BANK[:, P:2 * P], c_t[:, b % 2, :], wo[:, :], start=True,
                          stop=True).then_inc(s["wo_ready"], 1)

            def turn_fq(b):
                pe.wait_ge(s["fq_ready"], b + 1)
                if b >= 2:
                    pe.wait_ge(s["x3_done"], b - 1)
                pe.transpose(F_BANK[:, 0:P // 2].bitcast(BF16), fq[:, b % 2, :],
                             ident_b[:, :]).then_inc(s["fqt_ready"], 1)

            def gate_up(b):
                pe.wait_ge(s["fqt_copied"], b + 1)
                pe.matmul(F_BANK[:, :], fq_t[:, b % 2, :], w_tern[:, 0, :], start=True,
                          stop=True).then_inc(s["gate_ready"], 1)
                if b >= 3:
                    pe.wait_ge(s["lg_copied"], b - 2)
                if b >= 1:
                    pe.wait_ge(s["x2_done"], b)
                pe.matmul(G_BANK[:, :], fq_t[:, b % 2, :], w_tern[:, 1, :], start=True,
                          stop=True).then_inc(s["up_ready"], 1)

            def turn_ft(b):
                pe.wait_ge(s["ftq_ready"], b + 1)
                for k in range(NC):
                    last = pe.transpose(G_BANK[:, 0:FI // 2].bitcast(BF16)[:, P * k:P * k + P],
                                        ftq[:, b % 2, P * k:P * k + P], ident_b[:, :])
                last.then_inc(s["ftt_ready"], 1)

            def down(b):
                pe.wait_ge(s["ftt_copied"], b + 1)
                for k in range(NC):
                    last = pe.matmul(G_BANK[:, 256:256 + P], ftq_t[:, b % 2, k, :],
                                     w_tern[:, 2, P * k:P * k + P], start=(k == 0),
                                     stop=(k == NC - 1))
                last.then_inc(s["down_ready"], 1)

            def turn_ax(b):
                pe.wait_ge(s["ax_ready"], b + 1)
                pe.wait_ge(s["silu_done"], min(b + 2, NB))
                if b > 0:
                    pe.wait_ge(s["x3_done"], b)
                pe.transpose(F_BANK[:, 0:P], ax[:, b % 2, :], ident[:, :]).then_inc(
                    s["axt_ready"], 1)

            def att_scores(b):
                pe.wait_ge(s["axt_copied"], b + 1)
                pe.matmul(F_BANK[:, 128:256], ax_t[:, b % 2, :], ctx_t[:, P * b:P * b + P],
                          start=True, stop=True).then_inc(s["as_ready"], 1)

            def turn_p(b):
                pe.wait_ge(s["p_done"], b + 1)
                pe.transpose(F_BANK[:, 0:P], ap_[:, b % 2, :], ident[:, :]).then_inc(
                    s["pt_ready"], 1)

            def att_values(b):
                pe.wait_ge(s["pt_copied"], b + 1)
                pe.matmul(F_BANK[:, 256:384], ap_t[:, b % 2, :], ctx_tok[:, b, :], start=True,
                          stop=True).then_inc(s["av_ready"], 1)

            def turn_z(b):
                pe.wait_ge(s["z_ready"], b + 1)
                pe.wait_ge(s["x2_done"], min(b + 3, NB))
                if b > 0:
                    pe.wait_ge(s["lg_copied"], b)
                pe.transpose(G_BANK[:, 0:P], z_tok[:, b, :], ident[:, :]).then_inc(
                    s["zt_ready"], 1)

            def logits(b):
                pe.wait_ge(s["at_ready"], b + 1)
                pe.matmul(G_BANK[:, 128:128 + E + 2], a_t[:, P * b:P * b + P], wgc[:, :],
                          start=True, stop=True).then_inc(s["lg_ready"], 1)

            pe.wait_ge(s["consts"], 6)
            pe.wait_ge(s["v_copied"], 2)
            pe.wait_ge(s["k_loaded"], 2 * 12 * 16)
            pe.wait_ge(s["late_in"], 160)
            pe.wait_ge(s["ctxtok_in"], 16)
            for i in range(STEPS):
                a0, b1, c, f, d, r = (stage(i, k) for k in (A, B, C, F, D, R))
                if a0 is not None and a0 % 4 == 0:
                    pe.wait_ge(s[f"q_loaded{a0 // 4}"], 12 * 16)
                if f is not None:
                    if f == 0:
                        pe.wait_ge(s["tern_ready"], 1)
                    turn_fq(f)
                if c is not None:
                    turn_o(c)
                if a0 is not None:
                    scores(a0, 0)
                if f is not None:
                    gate_up(f)
                if b1 is not None:
                    scores_t(b1, 0)
                if c is not None:
                    turn_c(c)
                if d is not None:
                    turn_ax(d)
                if a0 is not None:
                    scores(a0, 1)
                if c is not None:
                    out_proj(c)
                if d is not None:
                    att_scores(d)
                if b1 is not None:
                    scores_t(b1, 1)
                    values(b1, 0)
                if a0 is not None:
                    scores(a0, 2)
                if f is not None:
                    turn_ft(f)
                if b1 is not None:
                    scores_t(b1, 2)
                    values(b1, 1)
                if f is not None:
                    down(f)
                if d is not None:
                    turn_p(d)
                if a0 is not None:
                    scores(a0, 3)
                if r is not None:
                    turn_z(r)
                if d is not None:
                    att_values(d)
                if b1 is not None:
                    scores_t(b1, 3)
                    values(b1, 2)
                if r is not None:
                    logits(r)
                if a0 is not None:
                    turn_max(a0)
                if b1 is not None:
                    values(b1, 3)

            pe.wait_ge(s["onehot_ready"], 1)
            pe.wait_ge(s["consts"], 7)
            for b in range(NB):
                for before in range(b + 1):
                    last = pe.matmul(bank[4][:, E * b:E * b + E],
                                     (before_b if before == b else ones_b)[:, :],
                                     onehot_b[:, before, :], start=(before == 0),
                                     stop=(before == b))
            last.then_inc(s["loc_ready"], 1)
            for n in range(2 * NC):
                half, k = n // NC, n % NC
                if n >= 4:
                    pe.wait_ge(s["rh_ready"], n - 3)
                pe.matmul(bank[n % 4][:, :], ri[:, P * k:P * k + P],
                          a_t[:, 512 * half:512 * half + 512], start=True, stop=True).then_inc(
                              s["r1_ready"], 1)
            pe.wait_ge(s["disp_in"], 16)
            pe.wait_ge(s["idx_ready"], 1)
            for half in range(2):
                for e in range(4 * half, 4 * half + 4):
                    last = pe.transpose(bank[4 + half][:, P * (e % 4):P * (e % 4) + P],
                                        disp[:, e, :], ident[:, :])
                last.then_inc(s["dt_ready"], 1)
            pe.wait_ge(s["iw_in"], 16)
            pe.wait_ge(s["ow_in"], 16)

            def hidden(e):
                if e < 2:
                    pe.wait_ge(s["rh_ready"], 5 + e)
                else:
                    pe.wait_ge(s["h_done"], NC * (e - 1))
                pe.wait_ge(s["dt_copied"], e // 4 + 1)
                for k in range(NC):
                    last = pe.matmul(bank[e % 2][:, P * k:P * k + P], iw[:, e, P * k:P * k + P],
                                     d_t[:, e, :], start=True, stop=True)
                last.then_inc(s["h_ready"], 1)

            hidden(0)
            for e in range(E):
                if e + 1 < E:
                    hidden(e + 1)
                pe.wait_ge(s["h_done"], NC * (e + 1))
                if e < 2:
                    pe.wait_ge(s["dt_copied"], 2)
                else:
                    pe.wait_ge(s["y_done"], e - 1)
                for k in range(NC):
                    last = pe.matmul(bank[4 + e % 2][:, 0:P], h_t[:, e % 2, k, :], ow[:, e, k, :],
                                     start=(k == 0), stop=(k == NC - 1))
                last.then_inc(s["y_ready"], 1)
            pe.wait_ge(s["rh_ready"], 2 * NC)
            for b in range(NB):
                if b >= 4:
                    pe.wait_ge(s["x5_done"], b - 3)
                for k in range(NC):
                    last = pe.matmul(bank[(6, 7, 2, 3)[b % 4]][:, 0:P], rh[:, k, P * b:P * b + P],
                                     ro[:, k, :], start=(k == 0), stop=(k == NC - 1))
                last.then_inc(s["r2_ready"], 1)


Q_ORDER = (0, 0, 0, 1, 1, 2)
K_ORDER = (0, 1, 2, 0, 1, 0)


def layout(i):
    def heads(w):
        return w.T.reshape(P, 2, 2, HU, DK).transpose(0, 2, 1, 3, 4).reshape(P, P)

    return {
        "x": i["x"].transpose(1, 0, 2), "ctx_tok": i["ctx_1024"].transpose(1, 0, 2),
        "ctx_t": i["ctx_1024"].transpose(2, 0, 1).reshape(P, T),
        "wq": heads(i["L0_xattn_W_q"]), "wk": heads(i["L0_xattn_W_k"]),
        "wv": i["L0_xattn_W_v"].T, "wo": i["L0_xattn_W_o"].T, "bo": i["L0_xattn_b_o"],
        "gx": i["g_xattn"], "gf": i["g_ffn"],
        "w_gate": i["L0_ffn_w_gate"].T, "w_up": i["L0_ffn_w_up"].T,
        "w_down": i["L0_ffn_w_down"].T.reshape(NC, P, P).transpose(1, 0, 2).reshape(P, FI),
        "nw": i["L1_ffn_attn_nw"].reshape(P, 1), "nb": i["L1_ffn_attn_nb"].reshape(P, 1),
        "wg": i["L1_ffn_wg"], "coef": i["L1_ffn_res_coef"],
        "ri": i["L1_ffn_res_inter_w"], "rib": i["L1_ffn_res_inter_b"].reshape(NC, P).T,
        "ro": i["L1_ffn_res_output_w"].reshape(NC, P, P).transpose(1, 0, 2),
        "rob": i["L1_ffn_res_output_b"],
        "iw": i["L1_ffn_inter_w"].transpose(1, 0, 2),
        "ib": i["L1_ffn_inter_b"].reshape(E, NC, P).transpose(2, 0, 1),
        "ow": i["L1_ffn_output_w"].reshape(E, NC, P, P).transpose(2, 0, 1, 3),
        "ob": i["L1_ffn_output_b"],
    }


def kernel(**inputs):
    import concourse.bacc as bacc
    from concourse.bass_utils import run_bass_kernel_spmd

    arrays = {n: np.ascontiguousarray(v) for n, v in
              layout({n: np.asarray(v) for n, v in inputs.items()}).items()}
    nc = bacc.Bacc("TRN2", target_bir_lowering=False, num_devices=1)
    aps = {n: nc.dram_tensor(f"{n}_in", v.shape, F32, kind="ExternalInput").ap()
           for n, v in arrays.items()}
    aps["out"] = nc.dram_tensor("tokens_out", (P, NB, P), F32, kind="ExternalOutput").ap()
    gated_flamingo(nc, aps)
    r = run_bass_kernel_spmd(nc, [{f"{n}_in": v for n, v in arrays.items()}], core_ids=[0])
    return np.ascontiguousarray(r.results[0]["tokens_out"].transpose(1, 0, 2))
```

```python
from contextlib import ExitStack

import numpy as np

import concourse.bass as bass
from concourse import mybir

F32 = mybir.dt.float32
BF16 = mybir.dt.bfloat16
I32 = mybir.dt.int32
ALU = mybir.AluOpType
ACT = mybir.ActivationFunctionType
AX = mybir.AxisListType

P = 128
NB = 8
T = NB * P
H, DK = 16, 8
HU = 4
NU = H // HU
FI = 512
NC = FI // P
E = 8
CAP = T // E
ROWS = 6 * DK
MROW = 3
SLOTS = 32
EPS = 1e-5
EPS_IN = 1e-12
ROUND = 12582912.0
NEG = -1e30
QMAX = 127.0


def gated_flamingo(nc, a):
    ctx = ExitStack()
    with ctx:
        def sb(name, shape, dt=F32):
            return ctx.enter_context(nc.sbuf_tensor(name, shape, dt))

        def sem(name):
            return ctx.enter_context(nc.semaphore(name))

        def dram(name, shape, dt):
            return nc.dram_tensor(name, shape, dt, kind="Internal").ap()

        bank = [ctx.enter_context(nc.psum_tensor(f"bank{i}", [P, 512], F32)) for i in range(8)]
        S_BANK, ST_BANK = bank[0:2], bank[2:4]
        O_BANK, W_BANK = bank[4], bank[5]
        F_BANK, G_BANK = bank[6], bank[7]

        q_dram = dram("q_dram", [2, 6, P, 512], BF16)
        k_dram = dram("k_dram", [2, 6, P, 512], BF16)
        m_dram = dram("m_dram", [NB, ROWS, P], BF16)
        disp_dram = dram("disp_dram", [E * CAP, P], F32)
        y_dram = dram("y_dram", [E * CAP, P], F32)

        x = sb("x", [P, NB, P])
        ctx_tok = sb("ctx_tok", [P, NB, P])
        ctx_t = sb("ctx_t", [P, T])
        w_att = sb("w_att", [P, 4, P])
        wk, wq, wv, wo = (w_att[:, n, :] for n in range(4))
        rows = sb("rows", [P, ROWS_N])
        bo, g4, rob = rows[:, 0:P], rows[:, P:P + 4], rows[:, P + 4:2 * P + 4]
        ob = rows[:, 2 * P + 4:].rearrange("p (e d) -> p e d", e=E)
        tg = sb("tg", [P, 4])
        w_raw = sb("w_raw", [P, 3, FI])
        w_tern = sb("w_tern", [P, 3, FI], BF16)
        w_sum = sb("w_sum", [P, 3])
        w_step = sb("w_step", [P, 6])
        w_inv = sb("w_inv", [P, 3])
        ident = sb("ident", [P, P])
        ident_b = sb("ident_b", [P, P], BF16)
        ones = sb("ones", [P, P])
        ones_b = sb("ones_b", [P, P], BF16)
        before_b = sb("before_b", [P, P], BF16)
        mask_b = sb("mask_b", [P, P], BF16)
        mask1 = sb("mask1", [P, P])
        half_neg = sb("half_neg", [P, NB])
        ranks = sb("ranks", [P, E])
        zeros = sb("zeros", [P, T])
        cols = sb("cols", [P, COLS_N])
        nw, nb, wgc = cols[:, 0:1], cols[:, 1:2], cols[:, 2:E + 4]
        rib = cols[:, E + 4:E + 4 + NC]
        ib = cols[:, E + 4 + NC:].rearrange("p (e c) -> p e c", e=E)
        w_res = sb("w_res", [P, 2 * FI])
        ri = w_res[:, 0:FI]
        ro = w_res[:, FI:].rearrange("p (c d) -> p c d", c=NC)
        iw = sb("iw", [P, E, FI])
        ow = sb("ow", [P, E, NC, P])

        st0 = sb("st0", [P, NB, 6])
        mv0 = sb("mv0", [P, NB, 2])
        rs0 = sb("rs0", [P, NB])
        xn = sb("xn", [P, NB, P])
        xn_t = sb("xn_t", [P, T])
        part = sb("part", [P, 4, 3, 512], BF16)
        rest = sb("rest", [P, 4, 512])
        q_st = sb("q_st", [P, 2, NB, 512], BF16)
        k_st = sb("k_st", [P, 2, NB, 512], BF16)
        v_st = sb("v_st", [P, NB, H, SLOTS])
        nmax = sb("nmax", [P, 2, 2, NB])
        nm_r = sb("nm_r", [P, 2, NB])
        nm_p = sb("nm_p", [P, 2, 2, MROW, NB], BF16)
        nm_t = sb("nm_t", [ROWS, 2, P], BF16)
        pr = sb("pr", [P, 4, HU, P])
        o_sb = sb("o_sb", [P, 2, 512])
        rsum = sb("rsum", [P, 2, H])
        c_tok = sb("c_tok", [P, 2, H, DK])
        c_t = sb("c_t", [P, 2, P])

        st = sb("st", [P, 3, 2, 6])
        mv = sb("mv", [P, 3, 2, 2])
        rs = sb("rs", [P, 3, 2, 2])
        nmr = sb("nmr", [P, 3, 2, 2])
        ve = sb("ve", [P, 3, 2, 2])
        fx = sb("fx", [P, 2, P])
        fr = sb("fr", [P, 2, P])
        fq = sb("fq", [P, 2, P], BF16)
        fq_t = sb("fq_t", [P, 2, P], BF16)
        fa = sb("fa", [P, 2, 8])
        sg = sb("sg", [P, 2, FI])
        ft = sb("ft", [P, 2, FI])
        ftr = sb("ftr", [P, 2, FI])
        ftq = sb("ftq", [P, 2, FI], BF16)
        ftq_t = sb("ftq_t", [P, 2, NC, P], BF16)
        ax = sb("ax", [P, 2, P])
        ax_t = sb("ax_t", [P, 2, P])
        asc = sb("asc", [P, 2, P])
        ap_ = sb("ap_", [P, 2, P])
        ap_t = sb("ap_t", [P, 2, P])
        am = sb("am", [P, 2, 5])
        r_tok = sb("r_tok", [P, 2, P])
        z_tok = sb("z_tok", [P, NB, P])
        a_t = sb("a_t", [P, T])
        lg = sb("lg", [P, NB, E + 2])
        gm = sb("gm", [P, NB, 2])
        ge = sb("ge", [P, NB, E + 2])
        gs = sb("gs", [P, NB, 2])
        gv = sb("gv", [P, NB, E])
        gvm = sb("gvm", [P, NB])
        onehot = sb("onehot", [P, NB, E])
        onehot_b = sb("onehot_b", [P, NB, E], BF16)
        gl = sb("gl", [P, NB, E])
        loc = sb("loc", [P, NB])
        keep = sb("keep", [P, NB])
        slot = sb("slot", [P, NB])
        drop = sb("drop", [P, NB])
        put_f = sb("put_f", [P, NB])
        get_f = sb("get_f", [P, NB])
        put_i = sb("put_i", [P, NB], I32)
        get_i = sb("get_i", [P, NB], I32)
        coef = sb("coef", [P, 2, NB])
        gk = sb("gk", [P, NB])
        rh = q_st[:, :, :, :].rearrange("p s h t -> p (s h t)").bitcast(F32).rearrange(
            "p (c t) -> p c t", c=NC)
        disp, d_t = xn, xn_t[:, :].rearrange("p (e t) -> p e t", e=E)
        h_t = sb("h_t", [P, 2, NC, P])
        y = zeros[:, :].rearrange("p (e d) -> p e d", e=E)
        moe = sb("moe", [P, NB, P])

        names = """x_in0 x_in1 ctx_in watt_in rows_in wffn_in ctxtok_in cols_in wres_in iw_in ow_in
            zero_out consts ones_made ones_in pool_step dve_step tanh_done
            ln0_var ln0_rstd ln0_done xt_ready xt_copied proj_ready part_h rest1 part_m part_l
            v_ready v_copied v_ones vst_zero k_out0 k_out1 q_out0 q_out1 k_loaded q_loaded0 q_loaded1
            bo_added wsum_ready wsum_all wstep_ready tern_ready
            s_ready max_done nm_split nmt_ready nm_copied m_out m_loaded0 m_loaded1
            st_ready exp_done masked pv_done o_copied ot_ready c_norm ct_ready ct_copied wo_ready
            x1_done
            f_var f_rstd f_norm fq_ready fqt_ready fqt_copied gate_ready up_ready tanh_g gate_read
            up_read ft_ready ftr_ready ftq_ready ftt_ready ftt_copied down_ready x2_done
            a_var a_rstd ax_ready axt_ready axt_copied as_ready as_read asc_ready p_done pt_ready
            pt_copied av_ready x3_done
            e_var e_rstd r_ready z_ready zt_ready at_ready lg_ready lg_copied x4_done
            lg_max g_exp onehot_ready loc_ready loc_read idx_ready coef_ready
            r1_ready rh_ready put_out disp_in dt_ready dt_copied h_ready h_done y_ready y_done y_out
            get_in r2_ready x5_done x6_done final_out""".split()
        s = {n: sem(n) for n in names}

        block = ctx.enter_context(nc.Block())
        SLOTS_N = NU * (NB - 1) + LAST + 1

        def batch_at(t, lag):
            b, rest_ = divmod(t - lag, NU)
            return b if rest_ == 0 and 0 <= b < NB else None

        def at(b):
            return b // 4, slice(P * (b % 4), P * (b % 4) + P)

        def unit_cols(u):
            return u % 2, (u // 2) * HU

        @block.sync
        def _(sp):
            for half in range(2):
                sl = slice(half * NB // 2, (half + 1) * NB // 2)
                sp.dma_start(x[:, sl, :], a["x"][:, sl, :]).then_inc(s[f"x_in{half}"], 16)
            sp.dma_start(ctx_t[:, :], a["ctx_t"]).then_inc(s["ctx_in"], 16)
            sp.dma_start(w_att[:, :, :], a["w_att"]).then_inc(s["watt_in"], 16)
            sp.dma_start(rows[:, :], a["rows"].partition_broadcast(P)).then_inc(s["rows_in"], 16)
            sp.dma_start(w_raw[:, :, :], a["w_ffn"]).then_inc(s["wffn_in"], 16)
            sp.wait_ge(s["ones_made"], 1)
            for side in range(2):
                sp.dma_start(k_st[64 * side + ROWS:64 * side + ROWS + MROW].rearrange(
                    "p s h t -> p (s h t)"),
                    ones_b[0:MROW, :].unsqueeze(1).to_broadcast([MROW, T * NB // P, P])).then_inc(
                        s["ones_in"], 16)

            def stack(st_, dr, n, half, order, out_sem, in_sem):
                runs = [r for r in order if r[0] in (0, 1, 2)]
                for need, p, count, first, step in runs:
                    sp.wait_ge(s[("part_h", "part_m", "part_l")[need]], n + 1)
                    src = part[:, n, first:first + (count if step else 1), :]
                    if not step:
                        src = src.to_broadcast([P, count, 512])
                    sp.dma_start(dr[half, p:p + count].rearrange("p r t -> r p t"), src).then_inc(
                        s[out_sem], 16)
                sp.wait_ge(s[out_sem], 16 * len(runs))
                for side in range(2):
                    sp.dma_start(
                        st_[64 * side:64 * side + ROWS, half, :, :],
                        dr[half].rearrange("p (s d h) t -> s p d (h t)", s=2, d=DK)[side]).then_inc(
                            s[in_sem], 16)

            for half in range(2):
                stack(k_st, k_dram, half, half, K_RUNS, f"k_out{half}", "k_loaded")
            for half in range(2):
                stack(q_st, q_dram, 2 + half, half, Q_RUNS, f"q_out{half}", f"q_loaded{half}")
            sp.dma_start(cols[:, :], a["cols"]).then_inc(s["cols_in"], 16)
            sp.dma_start(ctx_tok[:, :, :], a["ctx_tok"]).then_inc(s["ctxtok_in"], 16)
            sp.wait_ge(s["vst_zero"], 2)
            sp.dma_start(disp_dram.rearrange("(p c) d -> p (c d)", p=P), zeros[:, :]).then_inc(
                s["zero_out"], 16)
            for b in range(NB):
                sp.wait_ge(s["nm_copied"], b + 1)
                sp.dma_start(m_dram[b], nm_t[:, b % 2, :]).then_inc(s["m_out"], 16)
                sp.wait_ge(s["m_out"], 16 * (b + 1))
                for side in range(2):
                    half, tok = at(b)
                    sp.dma_start(q_st[64 * side + ROWS:64 * side + ROWS + MROW, half, :, tok],
                                 m_dram[b].rearrange("(s c hp) t -> s c hp t", s=2, c=MROW)[side]
                                 ).then_inc(s[f"m_loaded{b % 2}"], 16)
                if b == 1:
                    sp.dma_start(w_res[:, :], a["w_res"]).then_inc(s["wres_in"], 16)
                    sp.dma_start(iw[:, :, :], a["iw"]).then_inc(s["iw_in"], 16)
                if b == 2:
                    sp.dma_start(ow[:, :, :, :], a["ow"]).then_inc(s["ow_in"], 16)
            sp.wait_ge(s["put_out"], 16 * NB)
            sp.dma_start(disp[:, :, :], disp_dram.rearrange("(e p) d -> p e d", p=P)).then_inc(
                s["disp_in"], 16)
            for e in range(E):
                sp.wait_ge(s["y_done"], e + 1)
                sp.dma_start(y_dram[CAP * e:CAP * e + CAP, :], y[:, e, :]).then_inc(s["y_out"], 16)
            for b in range(NB):
                sp.wait_ge(s["x6_done"], b + 1)
                sp.dma_start(a["out"][:, b, :], x[:, b, :]).then_inc(s["final_out"], 16)
            sp.wait_ge(s["final_out"], 16 * NB)

        @block.gpsimd
        def _(g):
            steps = [0]

            def then(ins):
                steps[0] += 1
                ins.then_inc(s["pool_step"], 1)
                g.wait_ge(s["pool_step"], steps[0])

            g.memset(half_neg[:, :], -0.5).then_inc(s["consts"], 1)
            g.memset(ones[:, :], 1.0).then_inc(s["consts"], 1)
            then(g.memset(ident[:, :], 0.0))
            g.affine_select(out=ident[:, :], in_=ident[:, :], compare_op=ALU.not_equal, fill=1.0,
                            base=0, pattern=[[-1, P]], channel_multiplier=1).then_inc(s["consts"], 1)

            for half in range(2):
                sl = slice(half * NB // 2, (half + 1) * NB // 2)
                g.wait_ge(s["ln0_var"], half + 1)
                then(g.tensor_scalar(rs0[:, sl], mv0[:, sl, 1], EPS, None, ALU.add))
                g.tensor_tensor(rs0[:, sl], rs0[:, sl], half_neg[:, 0:NB // 2], ALU.pow).then_inc(
                    s["ln0_rstd"], 1)
            g.memset(v_st[:, :, :, :], 0.0).then_inc(s["vst_zero"], 1)
            g.wait_ge(s["vst_zero"], 1)
            g.memset(v_st[:, :, :, DK], 1.0).then_inc(s["v_ones"], 1)
            then(g.memset(ident_b[:, :], 0.0))
            g.affine_select(out=ident_b[:, :], in_=ident_b[:, :], compare_op=ALU.not_equal, fill=1.0,
                            base=0, pattern=[[-1, P]], channel_multiplier=1).then_inc(s["consts"], 1)
            then(g.memset(mask_b[:, :], 0.0))
            g.affine_select(out=mask_b[:, :], in_=mask_b[:, :], compare_op=ALU.is_ge, fill=NEG,
                            base=0, pattern=[[-1, P]], channel_multiplier=1).then_inc(s["consts"], 1)
            g.memset(zeros[:, :], 0.0).then_inc(s["vst_zero"], 1)
            g.wait_ge(s["tanh_done"], 1)
            then(g.tensor_scalar(bo, bo, tg[:, 0:1], None, ALU.mult))
            g.wait_ge(s["ln0_done"], NB)
            for b in range(NB):
                g.tensor_tensor(x[:, b, :], x[:, b, :], bo, ALU.add).then_inc(s["bo_added"], 1)
            then(g.memset(mask1[:, :], 0.0))
            g.affine_select(out=mask1[:, :], in_=mask1[:, :], compare_op=ALU.is_ge, fill=-1e10,
                            base=0, pattern=[[-1, P]], channel_multiplier=1).then_inc(s["consts"], 1)
            g.wait_ge(s["ones_made"], 1)
            g.affine_select(out=before_b[:, :], in_=ones_b[:, :], compare_op=ALU.is_ge, fill=0.0,
                            base=-1, pattern=[[1, P]], channel_multiplier=-1).then_inc(s["consts"], 1)
            for e in range(E):
                g.memset(ranks[:, e:e + 1], float(E - e)).then_inc(s["consts"], 1)

            def split_max(b):
                g.wait_ge(s["max_done"], NU * (b + 1))
                if b >= 2:
                    g.wait_ge(s["nmt_ready"], b - 1)
                p_, m_ = nm_p[:, b % 2], nmax[:, b % 2]
                then(g.tensor_copy(p_[:, :, 0, :], m_))
                then(g.tensor_tensor(nm_r[:, :, :], m_, p_[:, :, 0, :], ALU.subtract))
                then(g.tensor_copy(p_[:, :, 1, :], nm_r[:, :, :]))
                g.tensor_tensor(p_[:, :, 2, :], nm_r[:, :, :], p_[:, :, 1, :],
                                ALU.subtract).then_inc(s["nm_split"], 1)

            def mask_unit(u):
                def step(b):
                    n = NU * b + u
                    g.wait_ge(s["exp_done"], n + 1)
                    g.affine_select(out=pr[:, n % 4, :, :], in_=pr[:, n % 4, :, :],
                                    compare_op=ALU.is_ge, fill=0.0, base=0,
                                    pattern=[[0, HU], [1, P]],
                                    channel_multiplier=-1).then_inc(s["masked"], 1)
                return step

            def rstd(k, var_sem, out_sem):
                def step(b):
                    m, v_, r_ = mv[:, k, b % 2], ve[:, k, b % 2, 0:1], rs[:, k, b % 2, 0:1]
                    g.wait_ge(s[var_sem], b + 1)
                    then(g.tensor_scalar(v_, m[:, 1:2], EPS, None, ALU.add))
                    then(g.tensor_tensor(r_, v_, half_neg[:, 0:1], ALU.pow))
                    g.tensor_scalar(nmr[:, k, b % 2, 0:1], m[:, 0:1], r_, -1.0, ALU.mult,
                                    ALU.mult).then_inc(s[out_sem], 1)
                return step

            def rstd_router(b):
                m, v_, r_ = mv[:, 2, b % 2], ve[:, 2, b % 2], rs[:, 2, b % 2, :]
                g.wait_ge(s["e_var"], b + 1)
                then(g.tensor_scalar(v_[:, 0:1], m[:, 1:2], EPS, None, ALU.add))
                then(g.tensor_scalar(v_[:, 1:2], v_[:, 0:1], EPS_IN, m[:, 1:2], ALU.mult, ALU.add))
                then(g.tensor_tensor(r_, v_, half_neg[:, 0:2], ALU.pow))
                then(g.tensor_scalar(r_[:, 0:1], r_[:, 0:1], tg[:, 3:4], None, ALU.mult))
                g.tensor_scalar(nmr[:, 2, b % 2, :], r_, m[:, 0:1], -1.0, ALU.mult,
                                ALU.mult).then_inc(s["e_rstd"], 1)

            def quant_ft(b):
                g.wait_ge(s["ftr_ready"], b + 1)
                if b >= 2:
                    g.wait_ge(s["ftt_ready"], b - 1)
                g.tensor_scalar(ftq[:, b % 2, :], ftr[:, b % 2, :], -ROUND, QMAX, ALU.add,
                                ALU.min).then_inc(s["ftq_ready"], 1)

            def x4(b):
                g.wait_ge(s["r_ready"], b + 1)
                g.tensor_tensor(x[:, b, :], r_tok[:, b % 2, :], x[:, b, :], ALU.add).then_inc(
                    s["x4_done"], 1)

            steps_of = {"split_max": split_max, "rstd_f": rstd(0, "f_var", "f_rstd"),
                        "rstd_a": rstd(1, "a_var", "a_rstd"), "rstd_e": rstd_router,
                        "quant_ft": quant_ft, "x4": x4}
            steps_of.update({f"mask{u}": mask_unit(u) for u in range(NU)})
            for t in range(SLOTS_N):
                for lag, name in POOL_PLAN:
                    b = batch_at(t, lag)
                    if b is not None:
                        steps_of[name](b)

            g.wait_ge(s["idx_ready"], 1)
            g.wait_ge(s["zero_out"], 16)
            for b in range(NB):
                g.indirect_dma_start(
                    out=disp_dram, out_offset=bass.IndirectOffsetOnAxis(ap=put_i[:, b:b + 1], axis=0),
                    in_=z_tok[:, b, :], in_offset=None, bounds_check=E * CAP - 1,
                    oob_is_err=False).then_inc(s["put_out"], 16)
            g.wait_ge(s["y_out"], 16 * E)
            for b in range(NB):
                g.indirect_dma_start(
                    out=moe[:, b, :], out_offset=None, in_=y_dram,
                    in_offset=bass.IndirectOffsetOnAxis(ap=get_i[:, b:b + 1], axis=0),
                    bounds_check=E * CAP - 1, oob_is_err=False).then_inc(s["get_in"], 16)

        @block.scalar
        def _(act):
            act.wait_ge(s["rows_in"], 16)
            act.activation(tg[:, :], g4, ACT.Tanh).then_inc(s["tanh_done"], 1)

            def part_h(n):
                act.wait_ge(s["proj_ready"], n + 1)
                act.copy(part[:, n, 0, :], bank[n][:, :]).then_inc(s["part_h"], 1)

            def part_m(n):
                act.wait_ge(s["rest1"], n + 1)
                act.copy(part[:, n, 1, :], rest[:, n, :]).then_inc(s["part_m"], 1)

            def copy_xt(half):
                act.wait_ge(s["xt_ready"], half + 1)
                act.copy(xn_t[:, 512 * half:512 * half + 512], bank[4 + half][:, :]).then_inc(
                    s["xt_copied"], 1)

            part_h(0)
            part_h(1)
            copy_xt(0)
            part_m(0)
            copy_xt(1)
            part_m(1)
            part_h(2)
            part_h(3)
            part_m(2)
            part_m(3)
            act.wait_ge(s["v_ones"], 1)
            for half in range(2):
                act.wait_ge(s["v_ready"], half + 1)
                act.copy(v_st[:, 4 * half:4 * half + 4, :, 0:DK],
                         bank[6 + half][:, :].rearrange("p (b h d) -> p b h d", b=4, d=DK)).then_inc(
                             s["v_copied"], 1)

            def copy_nm(b):
                act.wait_ge(s["nmt_ready"], b + 1)
                if b >= 2:
                    act.wait_ge(s["m_out"], 16 * (b - 1))
                act.copy(nm_t[:, b % 2, :], S_BANK[0][0:ROWS, 0:P // 2].bitcast(BF16)).then_inc(
                    s["nm_copied"], 1)

            def exp_unit(u):
                def step(b):
                    n = NU * b + u
                    act.wait_ge(s["st_ready"], n + 1)
                    if n >= 4:
                        act.wait_ge(s["pv_done"], n - 3)
                    act.activation(pr[:, n % 4, :, :],
                                   ST_BANK[n % 2][:, :].rearrange("p (j q) -> p j q", j=HU),
                                   ACT.Exp, scale=float(DK) ** -0.5).then_inc(s["exp_done"], 1)
                return step

            def copy_o(b):
                act.wait_ge(s["pv_done"], NU * (b + 1))
                if b >= 2:
                    act.wait_ge(s["ot_ready"], b - 1)
                act.copy(o_sb[:, b % 2, :], O_BANK[:, :]).then_inc(s["o_copied"], 1)

            def copy_ct(b):
                act.wait_ge(s["ct_ready"], b + 1)
                if b >= 2:
                    act.wait_ge(s["wo_ready"], b - 1)
                act.copy(c_t[:, b % 2, :], W_BANK[:, 0:P]).then_inc(s["ct_copied"], 1)

            def norm(k, out, rstd_sem, used_sem, out_sem):
                def step(b):
                    act.wait_ge(s[rstd_sem], b + 1)
                    if b >= 2:
                        act.wait_ge(s[used_sem], b - 1)
                    act.activation(out[:, b % 2, :], x[:, b, :], ACT.Identity,
                                   bias=nmr[:, k, b % 2, 0:1],
                                   scale=rs[:, k, b % 2, 0:1]).then_inc(s[out_sem], 1)
                return step

            def norm_z(b):
                act.wait_ge(s["e_rstd"], b + 1)
                act.activation(z_tok[:, b, :], x[:, b, :], ACT.Identity, bias=nmr[:, 2, b % 2, 1:2],
                               scale=rs[:, 2, b % 2, 1:2]).then_inc(s["z_ready"], 1)

            def copy_fq(b):
                act.wait_ge(s["fqt_ready"], b + 1)
                if b >= 2:
                    act.wait_ge(s["up_ready"], b - 1)
                act.copy(fq_t[:, b % 2, :], F_BANK[:, 0:P // 2].bitcast(BF16)).then_inc(
                    s["fqt_copied"], 1)

            def tanh_g(b):
                act.wait_ge(s["gate_ready"], b + 1)
                if b >= 2:
                    act.wait_ge(s["gate_read"], b - 1)
                act.activation(sg[:, b % 2, :], F_BANK[:, :], ACT.Tanh,
                               scale=fa[:, b % 2, 3:4]).then_inc(s["tanh_g"], 1)

            def round_ft(b):
                act.wait_ge(s["ft_ready"], b + 1)
                if b >= 2:
                    act.wait_ge(s["ftq_ready"], b - 1)
                act.activation(ftr[:, b % 2, :], ft[:, b % 2, :], ACT.Copy, bias=ROUND,
                               scale=fa[:, b % 2, 7:8]).then_inc(s["ftr_ready"], 1)

            def copy_ft(b):
                act.wait_ge(s["ftt_ready"], b + 1)
                if b >= 2:
                    act.wait_ge(s["down_ready"], b - 1)
                act.copy(ftq_t[:, b % 2, :, :], G_BANK[:, 0:FI // 2].bitcast(BF16).rearrange(
                    "p (c t) -> p c t", c=NC)).then_inc(s["ftt_copied"], 1)

            def copy_ax(b):
                act.wait_ge(s["axt_ready"], b + 1)
                if b >= 2:
                    act.wait_ge(s["as_ready"], b - 1)
                act.copy(ax_t[:, b % 2, :], F_BANK[:, 0:P]).then_inc(s["axt_copied"], 1)

            def exp1(b):
                act.wait_ge(s["asc_ready"], b + 1)
                if b >= 2:
                    act.wait_ge(s["pt_ready"], b - 1)
                    act.wait_ge(s["x3_done"], b - 1)
                act.activation(ap_[:, b % 2, :], asc[:, b % 2, :], ACT.Exp, bias=am[:, b % 2, 1:2],
                               scale=float(P) ** -0.5, accum_out=am[:, b % 2, 2:3]).then_inc(
                                   s["p_done"], 1)

            def copy_pt(b):
                act.wait_ge(s["pt_ready"], b + 1)
                if b >= 2:
                    act.wait_ge(s["av_ready"], b - 1)
                act.copy(ap_t[:, b % 2, :], F_BANK[:, 0:P]).then_inc(s["pt_copied"], 1)

            def copy_at(b):
                act.wait_ge(s["zt_ready"], b + 1)
                if b == 0:
                    act.wait_ge(s["cols_in"], 16)
                act.activation(a_t[:, P * b:P * b + P], G_BANK[:, 0:P], ACT.Identity,
                               bias=nb, scale=nw).then_inc(s["at_ready"], 1)

            def copy_lg(b):
                act.wait_ge(s["lg_ready"], b + 1)
                act.copy(lg[:, b, :], G_BANK[:, 128:128 + E + 2]).then_inc(s["lg_copied"], 1)

            steps_of = {"copy_nm": copy_nm, "copy_o": copy_o, "copy_ct": copy_ct,
                        "norm_f": norm(0, fx, "f_rstd", "fq_ready", "f_norm"), "copy_fq": copy_fq,
                        "tanh_g": tanh_g, "round_ft": round_ft, "copy_ft": copy_ft,
                        "norm_a": norm(1, ax, "a_rstd", "axt_ready", "ax_ready"),
                        "copy_ax": copy_ax, "exp_a": exp1, "copy_pt": copy_pt,
                        "norm_r": norm(2, r_tok, "e_rstd", "x4_done", "r_ready"),
                        "norm_z": norm_z, "copy_at": copy_at, "copy_lg": copy_lg}
            steps_of.update({f"exp{u}": exp_unit(u) for u in range(NU)})
            for t in range(SLOTS_N):
                for lag, name in ACT_PLAN:
                    b = batch_at(t, lag)
                    if b is not None:
                        steps_of[name](b)

            act.wait_ge(s["lg_max"], 1)
            act.activation(ge[:, :, :], lg[:, :, :], ACT.Exp).then_inc(s["g_exp"], 1)

            for n in range(2 * NC):
                half, k = n // NC, n % NC
                act.wait_ge(s["r1_ready"], n + 1)
                act.activation(rh[:, k, 512 * half:512 * half + 512], bank[n % 4][:, :],
                               ACT.Gelu_apprx_tanh, bias=rib[:, k:k + 1]).then_inc(s["rh_ready"], 1)
            for half in range(2):
                act.wait_ge(s["dt_ready"], half + 1)
                act.activation(d_t[:, 4 * half:4 * half + 4, :],
                               bank[4 + half][:, :].rearrange("p (e t) -> p e t", e=4), ACT.Identity,
                               bias=nb, scale=nw).then_inc(s["dt_copied"], 1)
            for e in range(E):
                act.wait_ge(s["h_ready"], e + 1)
                if e >= 2:
                    act.wait_ge(s["y_ready"], e - 1)
                for k in range(NC):
                    act.activation(h_t[:, e % 2, k, :], bank[e % 2][:, P * k:P * k + P],
                                   ACT.Gelu_apprx_tanh, bias=ib[:, e, k:k + 1]).then_inc(
                                       s["h_done"], 1)

        @block.vector
        def _(v):
            steps = [0]

            def then(ins):
                steps[0] += 1
                ins.then_inc(s["dve_step"], 1)
                v.wait_ge(s["dve_step"], steps[0])

            v.memset(ones_b[:, :], 1.0).then_inc(s["ones_made"], 1)

            def ln0_stats(half):
                v.wait_ge(s[f"x_in{half}"], 16)
                for b in range(4 * half, 4 * half + 4):
                    then(v.bn_stats(st0[:, b, :], x[:, b, :]))
                    ins = v.bn_aggr(mv0[:, b, :], st0[:, b, :])
                    if b % 4 == 3:
                        ins.then_inc(s["ln0_var"], 1)
                    else:
                        then(ins)

            def ln0_norm(half):
                v.wait_ge(s["ln0_rstd"], half + 1)
                for b in range(4 * half, 4 * half + 4):
                    v.tensor_scalar(xn[:, b, :], x[:, b, :], mv0[:, b, 0:1], rs0[:, b:b + 1],
                                    ALU.subtract, ALU.mult).then_inc(s["ln0_done"], 1)

            def rest_of(n):
                v.wait_ge(s["part_h"], n + 1)
                v.tensor_tensor(rest[:, n, :], bank[n][:, :], part[:, n, 0, :],
                                ALU.subtract).then_inc(s["rest1"], 1)

            def part_l(n):
                v.wait_ge(s["part_m"], n + 1)
                v.tensor_tensor(part[:, n, 2, :], rest[:, n, :], part[:, n, 1, :],
                                ALU.subtract).then_inc(s["part_l"], 1)

            ln0_stats(0)
            ln0_stats(1)
            ln0_norm(0)
            ln0_norm(1)
            rest_of(0)
            rest_of(1)
            part_l(0)
            part_l(1)
            rest_of(2)
            rest_of(3)
            part_l(2)
            part_l(3)

            v.wait_ge(s["wffn_in"], 16)
            v.tensor_reduce(w_sum[:, :], w_raw[:, :, :], AX.X, ALU.add,
                            apply_absolute_value=True).then_inc(s["wsum_ready"], 1)
            v.wait_ge(s["wsum_all"], 1)
            v.tensor_scalar(w_step[:, 0:3], bank[4][:, 0:3], 1.0 / (P * FI), EPS, ALU.mult,
                            ALU.max).then_inc(s["wstep_ready"], 1)
            v.wait_ge(s["wstep_ready"], 1)
            then(v.reciprocal(w_inv[:, :], w_step[:, 0:3]))
            for n in range(3):
                then(v.tensor_scalar(w_raw[:, n, :], w_raw[:, n, :], w_inv[:, n:n + 1], 1.0,
                                     ALU.mult, ALU.min))
            then(v.tensor_scalar(w_step[:, 3:4], w_step[:, 0:1], 0.5, None, ALU.mult))
            then(v.tensor_scalar(w_step[:, 4:5], w_step[:, 3:4], w_step[:, 1:2], None, ALU.mult))
            v.wait_ge(s["tanh_done"], 1)
            then(v.tensor_scalar(w_step[:, 5:6], w_step[:, 2:3], tg[:, 2:3], None, ALU.mult))
            then(v.tensor_scalar(w_raw[:, :, :], w_raw[:, :, :], -1.0, ROUND, ALU.max, ALU.add))
            v.tensor_scalar(w_tern[:, :, :], w_raw[:, :, :], -ROUND, None, ALU.add).then_inc(
                s["tern_ready"], 1)

            def max_unit(u):
                def step(b):
                    n = NU * b + u
                    side, hp = unit_cols(u)
                    v.wait_ge(s["s_ready"], n + 1)
                    if u == 0 and b >= 2:
                        v.wait_ge(s["nm_split"], b - 1)
                    v.tensor_reduce(nmax[:, b % 2, side, hp:hp + HU],
                                    S_BANK[n % 2][:, :].rearrange("p (j k) -> p j k", j=HU), AX.X,
                                    ALU.max, negate=True).then_inc(s["max_done"], 1)
                return step

            def norm_c(b):
                o = W_BANK[:, :].rearrange("p (h c) -> p h c", c=SLOTS)
                v.wait_ge(s["ot_ready"], b + 1)
                if b >= 2:
                    v.wait_ge(s["ct_ready"], b - 1)
                then(v.reciprocal(rsum[:, b % 2, :], o[:, :, DK]))
                v.tensor_tensor(c_tok[:, b % 2], o[:, :, 0:DK],
                                rsum[:, b % 2, :].unsqueeze(2).to_broadcast([P, H, DK]),
                                ALU.mult).then_inc(s["c_norm"], 1)

            def x1(b):
                v.wait_ge(s["wo_ready"], b + 1)
                v.wait_ge(s["bo_added"], NB)
                v.scalar_tensor_tensor(x[:, b, :], W_BANK[:, P:2 * P], tg[:, 0:1], x[:, b, :],
                                       ALU.mult, ALU.add).then_inc(s["x1_done"], 1)

            def stats(k, x_sem, used_sem, var_sem):
                def step(b):
                    v.wait_ge(s[x_sem], b + 1)
                    if b >= 2:
                        v.wait_ge(s[used_sem], b - 1)
                    then(v.bn_stats(st[:, k, b % 2, :], x[:, b, :]))
                    v.bn_aggr(mv[:, k, b % 2, :], st[:, k, b % 2, :]).then_inc(s[var_sem], 1)
                return step

            def ffn_in(b):
                j = b % 2
                v.wait_ge(s["f_norm"], b + 1)
                if b >= 2:
                    v.wait_ge(s["fqt_ready"], b - 1)
                    v.wait_ge(s["tanh_g"], b - 1)
                then(v.tensor_reduce(fa[:, j, 0:1], fx[:, j, :], AX.X, ALU.max,
                                     apply_absolute_value=True))
                then(v.tensor_scalar(fa[:, j, 1:2], fa[:, j, 0:1], EPS, 1.0 / QMAX, ALU.max,
                                     ALU.mult))
                then(v.reciprocal(fa[:, j, 2:3], fa[:, j, 1:2]))
                then(v.tensor_scalar(fr[:, j, :], fx[:, j, :], fa[:, j, 2:3], ROUND, ALU.mult,
                                     ALU.add))
                v.tensor_scalar(fq[:, j, :], fr[:, j, :], -ROUND, QMAX, ALU.add,
                                ALU.min).then_inc(s["fq_ready"], 1)
                v.tensor_scalar(fa[:, j, 3:4], w_step[:, 3:4], fa[:, j, 1:2], None,
                                ALU.mult).then_inc(s["dve_step"], 1)
                steps[0] += 1
                then(v.tensor_scalar(fa[:, j, 4:5], fa[:, j, 1:2], fa[:, j, 1:2], w_step[:, 4:5],
                                     ALU.mult, ALU.mult))

            def ffn_mid(b):
                j = b % 2
                v.wait_ge(s["tanh_g"], b + 1)
                if b >= 2:
                    v.wait_ge(s["ftr_ready"], b - 1)
                v.scalar_tensor_tensor(ft[:, j, :], sg[:, j, :], 1.0, F_BANK[:, :], ALU.add,
                                       ALU.mult).then_inc(s["gate_read"], 1)
                v.wait_ge(s["gate_read"], b + 1)
                v.wait_ge(s["up_ready"], b + 1)
                v.scalar_tensor_tensor(ft[:, j, :], G_BANK[:, :], fa[:, j, 4:5], ft[:, j, :],
                                       ALU.mult, ALU.mult).then_inc(s["up_read"], 1)
                v.wait_ge(s["up_read"], b + 1)
                then(v.tensor_reduce(fa[:, j, 5:6], ft[:, j, :], AX.X, ALU.max,
                                     apply_absolute_value=True))
                then(v.tensor_scalar(fa[:, j, 6:7], fa[:, j, 5:6], EPS, 1.0 / QMAX, ALU.max,
                                     ALU.mult))
                v.reciprocal(fa[:, j, 7:8], fa[:, j, 6:7]).then_inc(s["ft_ready"], 1)
                v.tensor_scalar(fa[:, j, 0:1], fa[:, j, 6:7], w_step[:, 5:6], None,
                                ALU.mult).then_inc(s["dve_step"], 1)
                steps[0] += 1

            def x2(b):
                v.wait_ge(s["down_ready"], b + 1)
                v.wait_ge(s["dve_step"], steps[0])
                v.scalar_tensor_tensor(x[:, b, :], G_BANK[:, 256:256 + P], fa[:, b % 2, 0:1],
                                       x[:, b, :], ALU.mult, ALU.add).then_inc(s["x2_done"], 1)

            def att_max(b):
                j = b % 2
                v.wait_ge(s["as_ready"], b + 1)
                v.wait_ge(s["consts"], 6)
                if b >= 2:
                    v.wait_ge(s["p_done"], b - 1)
                v.tensor_tensor(asc[:, j, :], F_BANK[:, 128:256], mask1[:, :], ALU.add).then_inc(
                    s["as_read"], 1)
                v.wait_ge(s["as_read"], b + 1)
                then(v.tensor_reduce(am[:, j, 0:1], asc[:, j, :], AX.X, ALU.max))
                v.tensor_scalar(am[:, j, 1:2], am[:, j, 0:1], -float(P) ** -0.5, None,
                                ALU.mult).then_inc(s["asc_ready"], 1)

            def x3(b):
                j = b % 2
                v.wait_ge(s["p_done"], b + 1)
                then(v.reciprocal(am[:, j, 3:4], am[:, j, 2:3]))
                then(v.tensor_scalar(am[:, j, 4:5], am[:, j, 3:4], tg[:, 1:2], None, ALU.mult))
                v.wait_ge(s["av_ready"], b + 1)
                v.scalar_tensor_tensor(x[:, b, :], F_BANK[:, 256:384], am[:, j, 4:5], x[:, b, :],
                                       ALU.mult, ALU.add).then_inc(s["x3_done"], 1)

            steps_of = {"norm_c": norm_c, "x1": x1, "stats_f": stats(0, "x1_done", "f_norm", "f_var"),
                        "ffn_in": ffn_in, "ffn_mid": ffn_mid, "x2": x2,
                        "stats_a": stats(1, "x2_done", "ax_ready", "a_var"), "att_max": att_max,
                        "x3": x3, "stats_e": stats(2, "x3_done", "z_ready", "e_var")}
            steps_of.update({f"max{u}": max_unit(u) for u in range(NU)})
            for t in range(SLOTS_N):
                for lag, name in DVE_PLAN:
                    b = batch_at(t, lag)
                    if b is not None:
                        steps_of[name](b)

            v.wait_ge(s["lg_copied"], NB)
            logit, clog = lg[:, :, 0:E], lg[:, :, E:E + 2]
            v.tensor_reduce(gm[:, :, 0], logit, AX.X, ALU.max).then_inc(s["dve_step"], 1)
            v.tensor_reduce(gm[:, :, 1], clog, AX.X, ALU.max).then_inc(s["dve_step"], 1)
            steps[0] += 2
            v.wait_ge(s["dve_step"], steps[0])
            then(v.tensor_tensor(gv[:, :, :], logit, gm[:, :, 0:1].to_broadcast([P, NB, E]),
                                 ALU.is_equal))
            then(v.tensor_tensor(gv[:, :, :], gv[:, :, :],
                                 ranks[:, :].unsqueeze(1).to_broadcast([P, NB, E]), ALU.mult))
            then(v.tensor_reduce(gvm[:, :], gv[:, :, :], AX.X, ALU.max))
            then(v.tensor_tensor(onehot[:, :, :], gv[:, :, :],
                                 gvm[:, :].unsqueeze(2).to_broadcast([P, NB, E]), ALU.is_equal))
            v.tensor_copy(onehot_b[:, :, :], onehot[:, :, :]).then_inc(s["onehot_ready"], 1)
            then(v.tensor_tensor(logit, logit, gm[:, :, 0:1].to_broadcast([P, NB, E]), ALU.subtract))
            v.tensor_tensor(clog, clog, gm[:, :, 1:2].to_broadcast([P, NB, 2]),
                            ALU.subtract).then_inc(s["lg_max"], 1)
            v.wait_ge(s["loc_ready"], 1)
            v.wait_ge(s["loc_ready"], 1)
            then(v.tensor_tensor(gl[:, :, :], bank[4][:, 0:NB * E].rearrange("p (b e) -> p b e", e=E),
                                 onehot[:, :, :], ALU.mult))
            then(v.tensor_reduce(loc[:, :], gl[:, :, :], AX.X, ALU.add))
            then(v.tensor_scalar(keep[:, :], loc[:, :], float(CAP), None, ALU.is_lt))
            then(v.scalar_tensor_tensor(slot[:, :], gvm[:, :], -float(CAP), loc[:, :], ALU.mult,
                                        ALU.add))
            then(v.tensor_scalar(slot[:, :], slot[:, :], float(E * CAP), None, ALU.add))
            then(v.tensor_scalar(drop[:, :], keep[:, :], -4.0 * E * CAP, 4.0 * E * CAP, ALU.mult,
                                 ALU.add))
            then(v.tensor_tensor(put_f[:, :], slot[:, :], drop[:, :], ALU.add))
            then(v.tensor_tensor(get_f[:, :], slot[:, :], keep[:, :], ALU.mult))
            then(v.tensor_copy(get_i[:, :], get_f[:, :]))
            v.tensor_copy(put_i[:, :], put_f[:, :]).then_inc(s["idx_ready"], 1)
            v.wait_ge(s["g_exp"], 1)
            v.tensor_reduce(gs[:, :, 0], ge[:, :, 0:E], AX.X, ALU.add).then_inc(s["dve_step"], 1)
            v.tensor_reduce(gs[:, :, 1], ge[:, :, E:E + 2], AX.X, ALU.add).then_inc(
                s["dve_step"], 1)
            steps[0] += 2
            v.wait_ge(s["dve_step"], steps[0])
            then(v.reciprocal(gs[:, :, :], gs[:, :, :]))
            then(v.tensor_scalar(gs[:, :, 1], gs[:, :, 1], tg[:, 3:4], None, ALU.mult))
            then(v.tensor_tensor(coef[:, 0, :], ge[:, :, E], gs[:, :, 1], ALU.mult))
            then(v.tensor_tensor(coef[:, 1, :], ge[:, :, E + 1], gs[:, :, 1], ALU.mult))
            then(v.tensor_tensor(gk[:, :], gs[:, :, 0], keep[:, :], ALU.mult))
            then(v.tensor_tensor(coef[:, 1, :], coef[:, 1, :], gk[:, :], ALU.mult))
            v.wait_ge(s["x4_done"], NB)
            for b in range(NB):
                v.scalar_tensor_tensor(x[:, b, :], rob, coef[:, 0, b:b + 1], x[:, b, :],
                                       ALU.mult, ALU.add).then_inc(s["coef_ready"], 1)

            for e in range(E):
                v.wait_ge(s["y_ready"], e + 1)
                v.tensor_tensor(y[:, e, :], bank[4 + e % 2][:, 0:P], ob[:, e, :], ALU.add).then_inc(
                    s["y_done"], 1)
            v.wait_ge(s["coef_ready"], NB)
            for b in range(NB):
                v.wait_ge(s["r2_ready"], b + 1)
                v.scalar_tensor_tensor(x[:, b, :], bank[(6, 7, 2, 3)[b % 4]][:, 0:P],
                                       coef[:, 0, b:b + 1], x[:, b, :], ALU.mult,
                                       ALU.add).then_inc(s["x5_done"], 1)
            for b in range(NB):
                v.wait_ge(s["x5_done"], b + 1)
                v.wait_ge(s["get_in"], 16 * NB)
                v.scalar_tensor_tensor(x[:, b, :], moe[:, b, :], coef[:, 1, b:b + 1], x[:, b, :],
                                       ALU.mult, ALU.add).then_inc(s["x6_done"], 1)

        @block.tensor
        def _(pe):
            last_use = {}

            def take(k, reader, count):
                if k in last_use:
                    pe.wait_ge(s[last_use[k][0]], last_use[k][1])
                last_use[k] = (reader, count)

            pe.wait_ge(s["ctx_in"], 16)
            pe.wait_ge(s["watt_in"], 16)
            for half in range(2):
                take(half, "rest1", half + 1)
                pe.matmul(bank[half][:, :], wk, ctx_t[:, 512 * half:512 * half + 512],
                          start=True, stop=True).then_inc(s["proj_ready"], 1)
            pe.wait_ge(s["consts"], 3)
            for half in range(2):
                take(4 + half, "xt_copied", half + 1)
                for b in range(4):
                    pe.wait_ge(s["ln0_done"], 4 * half + b + 1)
                    last = pe.transpose(bank[4 + half][:, P * b:P * b + P], xn[:, 4 * half + b, :],
                                        ident[:, :])
                last.then_inc(s["xt_ready"], 1)
                pe.wait_ge(s["xt_copied"], half + 1)
                take(2 + half, "rest1", half + 3)
                pe.matmul(bank[2 + half][:, :], wq, xn_t[:, 512 * half:512 * half + 512],
                          start=True, stop=True).then_inc(s["proj_ready"], 1)
            for half in range(2):
                take(6 + half, "v_copied", half + 1)
                for b in range(4):
                    n = 4 * half + b
                    last = pe.matmul(bank[6 + half][:, P * b:P * b + P], ctx_t[:, P * n:P * n + P],
                                     wv, start=True, stop=True)
                last.then_inc(s["v_ready"], 1)
            pe.wait_ge(s["wsum_ready"], 1)
            take(4, "wstep_ready", 1)
            pe.matmul(bank[4][:, 0:3], ones[:, :], w_sum[:, :], start=True, stop=True).then_inc(
                s["wsum_all"], 1)

            def scores(u):
                def step(b):
                    n = NU * b + u
                    side, hp = unit_cols(u)
                    rows_ = slice(64 * side, 64 * side + ROWS)
                    half, tok = at(b)
                    if u == 0 and b == 0:
                        pe.wait_ge(s["k_loaded"], 4 * 16)
                    if u == 0 and b % 4 == 0:
                        pe.wait_ge(s[f"q_loaded{half}"], 2 * 16)
                    take(n % 2, "max_done", n + 1)
                    o = S_BANK[n % 2]
                    for j in range(HU):
                        pe.matmul(o[:, P * j:P * j + P], ident_b[:, :], mask_b[:, :], start=True,
                                  stop=False)
                        last = pe.matmul(o[:, P * j:P * j + P], q_st[rows_, half, hp + j, tok],
                                         k_st[rows_, half, hp + j, tok], start=False, stop=True)
                    last.then_inc(s["s_ready"], 1)
                return step

            def turn_max(b):
                pe.wait_ge(s["nm_split"], b + 1)
                take(0, "nm_copied", b + 1)
                pe.transpose(S_BANK[0][0:ROWS, 0:P // 2].bitcast(BF16),
                             nm_p[:, b % 2].rearrange("p s c h -> p (s c h)"),
                             ident_b[:, :]).then_inc(s["nmt_ready"], 1)

            def scores_t(u):
                def step(b):
                    n = NU * b + u
                    side, hp = unit_cols(u)
                    rows_ = slice(64 * side, 64 * side + ROWS + MROW)
                    half, tok = at(b)
                    if u == 0:
                        pe.wait_ge(s[f"m_loaded{b % 2}"], 32 * (b // 2 + 1))
                    if n == 0:
                        pe.wait_ge(s["ones_in"], 32)
                    take(2 + n % 2, "exp_done", n + 1)
                    o = ST_BANK[n % 2]
                    for j in range(HU):
                        last = pe.matmul(o[:, P * j:P * j + P], k_st[rows_, half, hp + j, tok],
                                         q_st[rows_, half, hp + j, tok], start=True, stop=True)
                    last.then_inc(s["st_ready"], 1)
                return step

            def values(u):
                def step(b):
                    n = NU * b + u
                    if n == 0:
                        pe.wait_ge(s["v_copied"], 2)
                    pe.wait_ge(s["masked"], n + 1)
                    if u == 0:
                        take(4, "o_copied", b + 1)
                    for j in range(HU):
                        last = pe.matmul(O_BANK[32 * j:32 * j + 32, P * u:P * u + P],
                                         v_st[:, b, HU * u + j, :], pr[:, n % 4, j, :], start=True,
                                         stop=True)
                    last.then_inc(s["pv_done"], 1)
                return step

            def turn_o(b):
                pe.wait_ge(s["o_copied"], b + 1)
                take(5, "c_norm", b + 1)
                for u in range(NU):
                    last = pe.transpose(W_BANK[:, P * u:P * u + P],
                                        o_sb[:, b % 2, P * u:P * u + P], ident[:, :])
                last.then_inc(s["ot_ready"], 1)

            def turn_c(b):
                take(5, "ct_copied", b + 1)
                pe.transpose(W_BANK[:, 0:P], c_tok[:, b % 2].rearrange("p h d -> p (h d)"),
                             ident[:, :]).then_inc(s["ct_ready"], 1)

            def out_proj(b):
                take(5, "x1_done", b + 1)
                pe.matmul(W_BANK[:, P:2 * P], c_t[:, b % 2, :], wo, start=True,
                          stop=True).then_inc(s["wo_ready"], 1)

            def turn_fq(b):
                pe.wait_ge(s["fq_ready"], b + 1)
                if b == 0:
                    pe.wait_ge(s["tern_ready"], 1)
                take(6, "fqt_copied", b + 1)
                pe.transpose(F_BANK[:, 0:P // 2].bitcast(BF16), fq[:, b % 2, :],
                             ident_b[:, :]).then_inc(s["fqt_ready"], 1)

            def gate_up(b):
                pe.wait_ge(s["fqt_copied"], b + 1)
                take(6, "gate_read", b + 1)
                pe.matmul(F_BANK[:, :], fq_t[:, b % 2, :], w_tern[:, 0, :], start=True,
                          stop=True).then_inc(s["gate_ready"], 1)
                take(7, "up_read", b + 1)
                pe.matmul(G_BANK[:, :], fq_t[:, b % 2, :], w_tern[:, 1, :], start=True,
                          stop=True).then_inc(s["up_ready"], 1)

            def turn_ft(b):
                pe.wait_ge(s["ftq_ready"], b + 1)
                take(7, "ftt_copied", b + 1)
                for k in range(NC):
                    last = pe.transpose(G_BANK[:, 0:FI // 2].bitcast(BF16)[:, P * k:P * k + P],
                                        ftq[:, b % 2, P * k:P * k + P], ident_b[:, :])
                last.then_inc(s["ftt_ready"], 1)

            def down(b):
                pe.wait_ge(s["ftt_copied"], b + 1)
                take(7, "x2_done", b + 1)
                for k in range(NC):
                    last = pe.matmul(G_BANK[:, 256:256 + P], ftq_t[:, b % 2, k, :],
                                     w_tern[:, 2, P * k:P * k + P], start=(k == 0),
                                     stop=(k == NC - 1))
                last.then_inc(s["down_ready"], 1)

            def turn_ax(b):
                pe.wait_ge(s["ax_ready"], b + 1)
                take(6, "axt_copied", b + 1)
                pe.transpose(F_BANK[:, 0:P], ax[:, b % 2, :], ident[:, :]).then_inc(
                    s["axt_ready"], 1)

            def att_scores(b):
                pe.wait_ge(s["axt_copied"], b + 1)
                take(6, "as_read", b + 1)
                pe.matmul(F_BANK[:, 128:256], ax_t[:, b % 2, :], ctx_t[:, P * b:P * b + P],
                          start=True, stop=True).then_inc(s["as_ready"], 1)

            def turn_p(b):
                pe.wait_ge(s["p_done"], b + 1)
                take(6, "pt_copied", b + 1)
                pe.transpose(F_BANK[:, 0:P], ap_[:, b % 2, :], ident[:, :]).then_inc(
                    s["pt_ready"], 1)

            def att_values(b):
                if b == 0:
                    pe.wait_ge(s["ctxtok_in"], 16)
                pe.wait_ge(s["pt_copied"], b + 1)
                take(6, "x3_done", b + 1)
                pe.matmul(F_BANK[:, 256:384], ap_t[:, b % 2, :], ctx_tok[:, b, :], start=True,
                          stop=True).then_inc(s["av_ready"], 1)

            def turn_z(b):
                pe.wait_ge(s["z_ready"], b + 1)
                take(7, "at_ready", b + 1)
                pe.transpose(G_BANK[:, 0:P], z_tok[:, b, :], ident[:, :]).then_inc(
                    s["zt_ready"], 1)

            def logits(b):
                pe.wait_ge(s["at_ready"], b + 1)
                take(7, "lg_copied", b + 1)
                pe.matmul(G_BANK[:, 128:128 + E + 2], a_t[:, P * b:P * b + P], wgc,
                          start=True, stop=True).then_inc(s["lg_ready"], 1)

            pe.wait_ge(s["consts"], 5)
            steps_of = {"turn_max": turn_max, "turn_o": turn_o, "turn_c": turn_c,
                        "out_proj": out_proj, "turn_fq": turn_fq, "gate_up": gate_up,
                        "turn_ft": turn_ft, "down": down, "turn_ax": turn_ax,
                        "att_scores": att_scores, "turn_p": turn_p, "att_values": att_values,
                        "turn_z": turn_z, "logits": logits}
            steps_of.update({f"scores{u}": scores(u) for u in range(NU)})
            steps_of.update({f"scores_t{u}": scores_t(u) for u in range(NU)})
            steps_of.update({f"values{u}": values(u) for u in range(NU)})
            for t in range(SLOTS_N):
                for lag, name in PE_PLAN:
                    b = batch_at(t, lag)
                    if b is not None:
                        steps_of[name](b)

            pe.wait_ge(s["onehot_ready"], 1)
            pe.wait_ge(s["consts"], 7)
            for b in range(NB):
                for before in range(b + 1):
                    last = pe.matmul(bank[4][:, E * b:E * b + E],
                                     (before_b if before == b else ones_b)[:, :],
                                     onehot_b[:, before, :], start=(before == 0),
                                     stop=(before == b))
            last.then_inc(s["loc_ready"], 1)
            pe.wait_ge(s["wres_in"], 16)
            for n in range(2 * NC):
                half, k = n // NC, n % NC
                take(n % 4, "rh_ready", n + 1)
                pe.matmul(bank[n % 4][:, :], ri[:, P * k:P * k + P],
                          a_t[:, 512 * half:512 * half + 512], start=True, stop=True).then_inc(
                              s["r1_ready"], 1)
            pe.wait_ge(s["disp_in"], 16)
            pe.wait_ge(s["idx_ready"], 1)
            for half in range(2):
                for e in range(4 * half, 4 * half + 4):
                    last = pe.transpose(bank[4 + half][:, P * (e % 4):P * (e % 4) + P],
                                        disp[:, e, :], ident[:, :])
                last.then_inc(s["dt_ready"], 1)
            pe.wait_ge(s["iw_in"], 16)
            pe.wait_ge(s["ow_in"], 16)

            def hidden(e):
                if e < 2:
                    pe.wait_ge(s["rh_ready"], 5 + e)
                else:
                    pe.wait_ge(s["h_done"], NC * (e - 1))
                pe.wait_ge(s["dt_copied"], e // 4 + 1)
                for k in range(NC):
                    last = pe.matmul(bank[e % 2][:, P * k:P * k + P], iw[:, e, P * k:P * k + P],
                                     d_t[:, e, :], start=True, stop=True)
                last.then_inc(s["h_ready"], 1)

            hidden(0)
            for e in range(E):
                if e + 1 < E:
                    hidden(e + 1)
                pe.wait_ge(s["h_done"], NC * (e + 1))
                if e < 2:
                    pe.wait_ge(s["dt_copied"], 2)
                else:
                    pe.wait_ge(s["y_done"], e - 1)
                for k in range(NC):
                    last = pe.matmul(bank[4 + e % 2][:, 0:P], h_t[:, e % 2, k, :], ow[:, e, k, :],
                                     start=(k == 0), stop=(k == NC - 1))
                last.then_inc(s["y_ready"], 1)
            pe.wait_ge(s["rh_ready"], 2 * NC)
            for b in range(NB):
                if b >= 4:
                    pe.wait_ge(s["x5_done"], b - 3)
                for k in range(NC):
                    last = pe.matmul(bank[(6, 7, 2, 3)[b % 4]][:, 0:P], rh[:, k, P * b:P * b + P],
                                     ro[:, k, :], start=(k == 0), stop=(k == NC - 1))
                last.then_inc(s["r2_ready"], 1)


Q_RUNS = ((0, 0, 3, 0, 0), (1, 3, 2, 1, 0), (2, 5, 1, 2, 0))
K_RUNS = ((2, 0, 3, 0, 1), (2, 3, 2, 0, 1), (2, 5, 1, 0, 1))

ROWS_N = P + 4 + P + E * P
COLS_N = 2 + E + 2 + NC + E * NC

def units(name, lag):
    return [(lag + u, f"{name}{u}") for u in range(NU)]


PE_PLAN = [
    (36, "att_values"), (19, "values2"), (30, "down"), (1, "scores1"), (4, "scores3"),
    (40, "turn_z"), (22, "out_proj"), (34, "turn_p"), (2, "scores2"), (16, "scores_t2"),
    (41, "logits"), (26, "gate_up"), (19, "values3"), (25, "turn_fq"), (15, "scores_t1"),
    (18, "values0"), (18, "values1"), (29, "turn_ft"), (8, "turn_max"), (33, "att_scores"),
    (20, "turn_o"), (0, "scores0"), (21, "turn_c"), (32, "turn_ax"), (17, "scores_t3"),
    (14, "scores_t0")]
ACT_PLAN = [
    (16, "exp1"), (34, "exp_a"), (39, "norm_z"), (34, "copy_pt"), (32, "copy_ax"), (7, "copy_nm"),
    (17, "exp2"), (40, "copy_lg"), (39, "norm_r"), (18, "exp3"), (26, "tanh_g"), (31, "norm_a"),
    (14, "exp0"), (25, "copy_fq"), (22, "norm_f"), (27, "round_ft"), (39, "copy_at"),
    (18, "copy_o"), (29, "copy_ft"), (21, "copy_ct")]
DVE_PLAN = [
    (4, "max1"), (38, "x3"), (24, "x1"), (39, "stats_e"), (35, "att_max"), (26, "ffn_in"),
    (3, "max0"), (5, "max3"), (32, "x2"), (22, "norm_c"), (4, "max2"), (24, "stats_f"),
    (32, "stats_a"), (28, "ffn_mid")]
POOL_PLAN = [
    (17, "mask0"), (38, "rstd_e"), (28, "quant_ft"), (31, "rstd_a"), (18, "mask3"), (17, "mask1"),
    (22, "rstd_f"), (17, "mask2"), (45, "x4"), (3, "split_max")]
LAST = max(lag for plan in (PE_PLAN, ACT_PLAN, DVE_PLAN, POOL_PLAN) for lag, _ in plan)


def layout(i):
    def heads(w):
        return w.T.reshape(P, 2, 2, HU, DK).transpose(0, 2, 4, 1, 3).reshape(P, P)

    return {
        "x": i["x"].transpose(1, 0, 2), "ctx_tok": i["ctx_1024"].transpose(1, 0, 2),
        "ctx_t": i["ctx_1024"].transpose(2, 0, 1).reshape(P, T),
        "w_att": np.stack([heads(i["L0_xattn_W_k"]), heads(i["L0_xattn_W_q"]),
                           i["L0_xattn_W_v"].T, i["L0_xattn_W_o"].T], 1),
        "rows": np.concatenate([i["L0_xattn_b_o"], i["g_xattn"], i["g_ffn"],
                                i["L1_ffn_res_output_b"], i["L1_ffn_output_b"].reshape(-1)]),
        "w_ffn": np.stack([i["L0_ffn_w_gate"].T, i["L0_ffn_w_up"].T,
                           i["L0_ffn_w_down"].T.reshape(NC, P, P).transpose(1, 0, 2).reshape(
                               P, FI)], 1),
        "cols": np.concatenate([i["L1_ffn_attn_nw"].reshape(P, 1), i["L1_ffn_attn_nb"].reshape(P, 1),
                                i["L1_ffn_wg"], i["L1_ffn_res_coef"],
                                i["L1_ffn_res_inter_b"].reshape(NC, P).T,
                                i["L1_ffn_inter_b"].reshape(E * NC, P).T], 1),
        "w_res": np.concatenate([i["L1_ffn_res_inter_w"],
                                 i["L1_ffn_res_output_w"].reshape(NC, P, P).transpose(
                                     1, 0, 2).reshape(P, FI)], 1),
        "iw": i["L1_ffn_inter_w"].transpose(1, 0, 2),
        "ow": i["L1_ffn_output_w"].reshape(E, NC, P, P).transpose(2, 0, 1, 3),
    }


def kernel(**inputs):
    import concourse.bacc as bacc
    from concourse.bass_utils import run_bass_kernel_spmd

    arrays = {n: np.ascontiguousarray(v) for n, v in
              layout({n: np.asarray(v) for n, v in inputs.items()}).items()}
    nc = bacc.Bacc("TRN2", target_bir_lowering=False, num_devices=1)
    aps = {n: nc.dram_tensor(f"{n}_in", v.shape, F32, kind="ExternalInput").ap()
           for n, v in arrays.items()}
    aps["out"] = nc.dram_tensor("tokens_out", (P, NB, P), F32, kind="ExternalOutput").ap()
    gated_flamingo(nc, aps)
    r = run_bass_kernel_spmd(nc, [{f"{n}_in": v for n, v in arrays.items()}], core_ids=[0])
    return np.ascontiguousarray(r.results[0]["tokens_out"].transpose(1, 0, 2))
```

```python
from contextlib import ExitStack

import numpy as np

import concourse.bass as bass
from concourse import mybir

F32 = mybir.dt.float32
BF16 = mybir.dt.bfloat16
I32 = mybir.dt.int32
ALU = mybir.AluOpType
ACT = mybir.ActivationFunctionType
AX = mybir.AxisListType

P = 128
NB = 8
T = NB * P
H, DK = 16, 8
HU = 4
NU = H // HU
FI = 512
NC = FI // P
E = 8
CAP = T // E
ROWS = 6 * DK
MROW = 3
SLOTS = 32
EPS = 1e-5
EPS_IN = 1e-12
ROUND = 12582912.0
NEG = -1e30
QMAX = 127.0
NO_TOKEN = 4 * T
GROUP_ENDS = (3, 6, 7)
GROUP_OF = [sum(e < b for e in GROUP_ENDS) for b in range(NB)]
R2_BANKS = (6, 7, 2, 3)
R2_EARLY = 0


def gated_flamingo(nc, a):
    ctx = ExitStack()
    with ctx:
        def sb(name, shape, dt=F32):
            return ctx.enter_context(nc.sbuf_tensor(name, shape, dt))

        def sem(name):
            return ctx.enter_context(nc.semaphore(name))

        def dram(name, shape, dt):
            return nc.dram_tensor(name, shape, dt, kind="Internal").ap()

        bank = [ctx.enter_context(nc.psum_tensor(f"bank{i}", [P, 512], F32)) for i in range(8)]
        S_BANK, ST_BANK = bank[0:2], bank[2:4]
        O_BANK, W_BANK = bank[4], bank[5]
        F_BANK, G_BANK = bank[6], bank[7]
        LOC_BANK = bank[7]

        q_dram = dram("q_dram", [2, 6, P, 512], BF16)
        k_dram = dram("k_dram", [2, 6, P, 512], BF16)
        m_dram = dram("m_dram", [NB, ROWS, P], BF16)
        disp_dram = dram("disp_dram", [E * CAP, P + 1], F32)
        moe_dram = dram("moe_dram", [T, P], F32)

        x = sb("x", [P, NB, P])
        ctx_tok = sb("ctx_tok", [P, NB, P])
        ctx_t = sb("ctx_t", [P, T])
        w_att = sb("w_att", [P, 4, P])
        wk, wq, wv, wo = (w_att[:, n, :] for n in range(4))
        rows = sb("rows", [P, ROWS_N])
        bo, g4, rob = rows[:, 0:P], rows[:, P:P + 4], rows[:, P + 4:2 * P + 4]
        ob = rows[:, 2 * P + 4:].rearrange("p (e d) -> p e d", e=E)
        tg = sb("tg", [P, 4])
        w_raw = sb("w_raw", [P, 3, FI])
        w_tern = sb("w_tern", [P, 3, FI], BF16)
        w_sum = sb("w_sum", [P, 3])
        w_step = sb("w_step", [P, 6])
        w_inv = sb("w_inv", [P, 3])
        ident = sb("ident", [P, P])
        ident_b = sb("ident_b", [P, P], BF16)
        ones = sb("ones", [P, P])
        ones_b = sb("ones_b", [P, P], BF16)
        before_b = sb("before_b", [P, P], BF16)
        mask_b = sb("mask_b", [P, P], BF16)
        half_neg = sb("half_neg", [P, NB])
        ranks = sb("ranks", [P, E])
        zeros = sb("zeros", [P, T + E])
        cols = sb("cols", [P, COLS_N])
        nw, nb, wgc = cols[:, 0:1], cols[:, 1:2], cols[:, 2:E + 4]
        rib = cols[:, E + 4:E + 4 + NC]
        ib = cols[:, E + 4 + NC:].rearrange("p (e c) -> p e c", e=E)
        w_res = sb("w_res", [P, 2 * FI])
        ri = w_res[:, 0:FI]
        ro = w_res[:, FI:].rearrange("p (c d) -> p c d", c=NC)
        iw = sb("iw", [P, E, FI])
        ow = sb("ow", [P, E, NC, P])

        st0 = sb("st0", [P, NB, 6])
        mv0 = sb("mv0", [P, NB, 2])
        rs0 = sb("rs0", [P, NB])
        xn = sb("xn", [P, NB, P])
        xn_t = sb("xn_t", [P, T])
        part = sb("part", [P, 4, 3, 512], BF16)
        rest = sb("rest", [P, 4, 512])
        q_st = sb("q_st", [P, 2, NB, 512], BF16)
        k_st = sb("k_st", [P, 2, NB, 512], BF16)
        v_st = sb("v_st", [P, NB, H, SLOTS])
        nmax = sb("nmax", [P, 2, 2, NB])
        nm_r = sb("nm_r", [P, 2, 2, NB])
        nm_p = sb("nm_p", [P, 2, 2, MROW, NB], BF16)
        nm_t = sb("nm_t", [ROWS, 2, P], BF16)
        pr = sb("pr", [P, 4, HU, P])
        o_sb = sb("o_sb", [P, 2, 512])
        rsum = sb("rsum", [P, 2, H])
        c_tok = sb("c_tok", [P, 2, H, DK])
        c_t = sb("c_t", [P, 2, P])

        st = sb("st", [P, 3, 2, 6])
        mv = sb("mv", [P, 3, 2, 2])
        rs = sb("rs", [P, 3, 2, 2])
        nmr = sb("nmr", [P, 3, 2, 2])
        ve = sb("ve", [P, 3, 2, 2])
        fx = sb("fx", [P, 2, P])
        fr = sb("fr", [P, 2, P])
        fq = sb("fq", [P, 2, P], BF16)
        fq_t = sb("fq_t", [P, 2, P], BF16)
        fa = sb("fa", [P, 2, 8])
        sg = sb("sg", [P, 2, FI])
        ft = sb("ft", [P, 2, FI])
        ftr = sb("ftr", [P, 2, FI])
        ftq = sb("ftq", [P, 2, FI], BF16)
        ftq_t = sb("ftq_t", [P, 2, NC, P], BF16)
        ax = sb("ax", [P, 2, P])
        ax_t = sb("ax_t", [P, 2, P])
        ap_ = sb("ap_", [P, 2, P])
        ap_t = sb("ap_t", [P, 2, P])
        am = sb("am", [P, 2, 5])
        r_tok = sb("r_tok", [P, 2, P])
        z_tok = sb("z_tok", [P, NB, P + 1])
        a_t = sb("a_t", [P, T])
        lg = sb("lg", [P, NB, E + 2])
        gm = sb("gm", [P, NB, 2])
        ge = sb("ge", [P, NB, E + 2])
        gs = sb("gs", [P, NB, 2])
        gv = sb("gv", [P, NB, E])
        gvm = sb("gvm", [P, NB])
        onehot_b = sb("onehot_b", [P, NB, E], BF16)
        gl = sb("gl", [P, NB, E])
        loc = sb("loc", [P, NB])
        keep = sb("keep", [P, NB])
        slot = sb("slot", [P, NB])
        drop = sb("drop", [P, NB])
        put_f = sb("put_f", [P, NB])
        put_i = sb("put_i", [P, NB], I32)
        number = sb("number", [P, NB], I32)
        tok_f = sb("tok_f", [P, E])
        tok_i = sb("tok_i", [P, E], I32)
        coef = sb("coef", [P, 2, NB])
        gk = sb("gk", [P, NB])
        rh = q_st[:, :, :, :].rearrange("p s h t -> p (s h t)").bitcast(F32).rearrange(
            "p (c t) -> p c t", c=NC)
        disp = part[:, :, :, :].rearrange("p n c t -> p (n c t)").bitcast(F32)[
            :, 0:E * (P + 1)].rearrange("p (e d) -> p e d", e=E)
        d_t = xn_t[:, :].rearrange("p (e t) -> p e t", e=E)
        h_t = sb("h_t", [P, 2, NC, P])
        y = zeros[:, 0:T].rearrange("p (e d) -> p e d", e=E)
        moe = sb("moe", [P, NB, P])

        names = """x_in0 x_in1 ctx_in0 ctx_in1 watt_in rows_in wffn_in ctxtok_in cols_in wres_in iw_in ow_in
            zero_out consts ones_made ones_in pool_step dve_step tanh_done
            ln0_var ln0_rstd ln0_done xt_ready xt_copied proj_ready part_h rest1 part_m part_l
            v_ready v_copied v_ones vst_zero k_out0 k_out1 q_out0 q_out1 k_loaded0 k_loaded1 q_loaded0 q_loaded1
            bo_added wsum_ready wsum_all wstep_ready tern_ready
            s_ready max_done nm_split values_ready round_ready f_inv nmt_ready nm_copied m_out m_loaded0 m_loaded1
            st_ready exp_done masked pv_done o_copied ot_ready c_norm ct_ready ct_copied wo_ready
            x1_done
            f_var f_rstd f_norm fq_ready fqt_ready fqt_copied gate_ready up_ready tanh_g gate_read
            up_read ft_ready ftr_ready ftq_ready ftt_ready ftt_copied down_ready x2_done
            a_var a_rstd ax_ready axt_ready axt_copied as_ready asc_ready p_done pt_ready
            pt_copied av_ready x3_done
            e_var e_rstd r_ready z_ready zt_ready at_ready lg_ready lg_copied x4_done
            lg_max g_exp onehot_ready loc_ready loc_read idx_ready coef_ready
            r1_ready rh_ready put_out disp_in0 disp_in1 tok_ready number_ready dt_ready dt_copied
            h_ready h_done y_ready y_done moe_out moe_in0 moe_in1 r2_ready x5_done x6_done final_out""".split()
        s = {n: sem(n) for n in names}

        block = ctx.enter_context(nc.Block())
        SLOTS_N = NU * (NB - 1) + LAST + 1

        def batch_at(t, lag):
            b, rest_ = divmod(t - lag, NU)
            return b if rest_ == 0 and 0 <= b < NB else None

        def at(b):
            return b // 4, slice(P * (b % 4), P * (b % 4) + P)

        def group(b):
            ends = (-1,) + GROUP_ENDS
            return slice(ends[GROUP_OF[b]] + 1, b + 1)

        def unit_cols(u):
            return u % 2, (u // 2) * HU

        @block.sync
        def _(sp):
            def load_half(half):
                sl = slice(half * NB // 2, (half + 1) * NB // 2)
                sp.dma_start(x[:, sl, :], a["x"][:, sl, :]).then_inc(s[f"x_in{half}"], 16)
                if half == 0:
                    sp.dma_start(w_att[:, :, :], a["w_att"]).then_inc(s["watt_in"], 16)
                tok = slice(512 * half, 512 * half + 512)
                sp.dma_start(ctx_t[:, tok], a["ctx_t"][:, tok]).then_inc(s[f"ctx_in{half}"], 16)

            load_half(0)
            load_half(1)
            sp.dma_start(w_raw[:, :, :], a["w_ffn"]).then_inc(s["wffn_in"], 16)
            sp.dma_start(rows[:, :], a["rows"].partition_broadcast(P)).then_inc(s["rows_in"], 16)
            sp.dma_start(ctx_tok[:, :, :], a["ctx_tok"]).then_inc(s["ctxtok_in"], 16)

            def write_parts(dr, n, half, runs, out_sem):
                for need, p, count, first, step in runs:
                    sp.wait_ge(s[("part_h", "part_m", "part_l")[need]], n + 1)
                    src = part[:, n, first:first + (count if step else 1), :]
                    if not step:
                        src = src.to_broadcast([P, count, 512])
                    sp.dma_start(dr[half, p:p + count].rearrange("p r t -> r p t"), src).then_inc(
                        s[out_sem], 16)

            def read_stack(st_, dr, half, runs, out_sem, in_sem):
                sp.wait_ge(s[out_sem], 16 * len(runs))
                for side in range(2):
                    sp.dma_start(
                        st_[64 * side:64 * side + ROWS, half, :, :],
                        dr[half].rearrange("p (s d h) t -> s p d (h t)", s=2, d=DK)[side]).then_inc(
                            s[in_sem], 16)

            for half in range(2):
                write_parts(k_dram, 2 * half, half, K_RUNS, f"k_out{half}")
                write_parts(q_dram, 2 * half + 1, half, Q_RUNS, f"q_out{half}")
                read_stack(k_st, k_dram, half, K_RUNS, f"k_out{half}", f"k_loaded{half}")
                read_stack(q_st, q_dram, half, Q_RUNS, f"q_out{half}", f"q_loaded{half}")
                if half == 0:
                    sp.wait_ge(s["ones_made"], 1)
                    for side in range(2):
                        sp.dma_start(k_st[64 * side + ROWS:64 * side + ROWS + MROW].rearrange(
                            "p s h t -> p (s h t)"),
                            ones_b[0:MROW, :].unsqueeze(1).to_broadcast(
                                [MROW, T * NB // P, P])).then_inc(s["ones_in"], 16)
            sp.dma_start(cols[:, :], a["cols"]).then_inc(s["cols_in"], 16)
            for b in range(NB):
                sp.wait_ge(s["nm_copied"], b + 1)
                sp.dma_start(m_dram[b], nm_t[:, b % 2, :]).then_inc(s["m_out"], 16)
                sp.wait_ge(s["m_out"], 16 * (b + 1))
                for side in range(2):
                    half, tok = at(b)
                    sp.dma_start(q_st[64 * side + ROWS:64 * side + ROWS + MROW, half, :, tok],
                                 m_dram[b].rearrange("(s c hp) t -> s c hp t", s=2, c=MROW)[side]
                                 ).then_inc(s[f"m_loaded{b % 2}"], 16)
                if b == 1:
                    sp.wait_ge(s["vst_zero"], 2)
                    sp.dma_start(disp_dram.rearrange("(p c) d -> p (c d)", p=P),
                                 zeros[:, :]).then_inc(s["zero_out"], 16)
                    sp.dma_start(moe_dram.rearrange("(p c) d -> p (c d)", p=P),
                                 zeros[:, 0:T]).then_inc(s["zero_out"], 16)
                if b == 2:
                    sp.dma_start(w_res[:, :], a["w_res"]).then_inc(s["wres_in"], 16)
                    sp.dma_start(iw[:, :, :], a["iw"]).then_inc(s["iw_in"], 16)
                if b == 3:
                    sp.dma_start(ow[:, :, :, :], a["ow"]).then_inc(s["ow_in"], 16)
            sp.wait_ge(s["put_out"], 16 * NB)
            for half in range(2):
                sl = slice(half * E // 2, (half + 1) * E // 2)
                sp.dma_start(disp[:, sl, :], disp_dram.rearrange("(e p) d -> p e d", p=P)[:, sl, :]
                             ).then_inc(s[f"disp_in{half}"], 16)
            sp.wait_ge(s["moe_out"], 16 * E)
            for half in range(2):
                sl = slice(half * NB // 2, (half + 1) * NB // 2)
                sp.dma_start(moe[:, sl, :], moe_dram.rearrange("(b p) d -> p b d", p=P)[:, sl, :]
                             ).then_inc(s[f"moe_in{half}"], 16)
            for b in range(0, NB, 2):
                sp.wait_ge(s["x6_done"], b + 2)
                sp.dma_start(a["out"][:, b:b + 2, :], x[:, b:b + 2, :]).then_inc(
                    s["final_out"], 16)
            sp.wait_ge(s["final_out"], 16 * NB // 2)

        @block.gpsimd
        def _(g):
            steps = [0]

            def then(ins):
                steps[0] += 1
                ins.then_inc(s["pool_step"], 1)
                g.wait_ge(s["pool_step"], steps[0])

            written = {}

            def mark(key, ins):
                steps[0] += 1
                written[key] = steps[0]
                ins.then_inc(s["pool_step"], 1)

            def needs(key):
                g.wait_ge(s["pool_step"], written[key])

            g.memset(half_neg[:, :], -0.5).then_inc(s["consts"], 1)
            g.memset(ones[:, :], 1.0).then_inc(s["consts"], 1)
            then(g.memset(ident[:, :], 0.0))
            g.affine_select(out=ident[:, :], in_=ident[:, :], compare_op=ALU.not_equal, fill=1.0,
                            base=0, pattern=[[-1, P]], channel_multiplier=1).then_inc(s["consts"], 1)

            for half in range(2):
                sl = slice(half * NB // 2, (half + 1) * NB // 2)
                g.wait_ge(s["ln0_var"], half + 1)
                then(g.tensor_scalar(rs0[:, sl], mv0[:, sl, 1], EPS, None, ALU.add))
                g.tensor_tensor(rs0[:, sl], rs0[:, sl], half_neg[:, 0:NB // 2], ALU.pow).then_inc(
                    s["ln0_rstd"], 1)
            g.memset(v_st[:, :, :, :], 0.0).then_inc(s["vst_zero"], 1)
            g.wait_ge(s["vst_zero"], 1)
            g.memset(v_st[:, :, :, DK], 1.0).then_inc(s["v_ones"], 1)
            then(g.memset(ident_b[:, :], 0.0))
            g.affine_select(out=ident_b[:, :], in_=ident_b[:, :], compare_op=ALU.not_equal, fill=1.0,
                            base=0, pattern=[[-1, P]], channel_multiplier=1).then_inc(s["consts"], 1)
            then(g.memset(mask_b[:, :], 0.0))
            g.affine_select(out=mask_b[:, :], in_=mask_b[:, :], compare_op=ALU.is_ge, fill=NEG,
                            base=0, pattern=[[-1, P]], channel_multiplier=1).then_inc(s["consts"], 1)
            g.memset(zeros[:, :], 0.0).then_inc(s["vst_zero"], 1)
            g.wait_ge(s["tanh_done"], 1)
            then(g.tensor_scalar(bo, bo, tg[:, 0:1], None, ALU.mult))
            g.wait_ge(s["ln0_done"], NB)
            for b in range(NB):
                g.tensor_tensor(x[:, b, :], x[:, b, :], bo, ALU.add).then_inc(s["bo_added"], 1)
            g.wait_ge(s["ones_made"], 1)
            g.affine_select(out=before_b[:, :], in_=ones_b[:, :], compare_op=ALU.is_ge, fill=0.0,
                            base=-1, pattern=[[1, P]], channel_multiplier=-1).then_inc(s["consts"], 1)
            for e in range(E):
                g.memset(ranks[:, e:e + 1], float(E - e)).then_inc(s["consts"], 1)
            then(g.iota(number[:, :], [[P, NB]], base=-NO_TOKEN, channel_multiplier=1))
            g.tensor_copy(z_tok[:, :, P], number[:, :]).then_inc(s["number_ready"], 1)

            def max_h(b):
                g.wait_ge(s["max_done"], NU * (b + 1))
                if b >= 2:
                    g.wait_ge(s["nmt_ready"], b - 1)
                mark(("max_h", b), g.tensor_copy(nm_p[:, b % 2, :, 0, :], nmax[:, b % 2]))

            def max_rest(b):
                needs(("max_h", b))
                mark(("max_rest", b), g.tensor_tensor(nm_r[:, b % 2], nmax[:, b % 2],
                                                      nm_p[:, b % 2, :, 0, :], ALU.subtract))

            def max_m(b):
                needs(("max_rest", b))
                mark(("max_m", b), g.tensor_copy(nm_p[:, b % 2, :, 1, :], nm_r[:, b % 2]))

            def max_l(b):
                needs(("max_m", b))
                g.tensor_tensor(nm_p[:, b % 2, :, 2, :], nm_r[:, b % 2], nm_p[:, b % 2, :, 1, :],
                                ALU.subtract).then_inc(s["nm_split"], 1)

            def mask_unit(u):
                def step(b):
                    n = NU * b + u
                    g.wait_ge(s["exp_done"], n + 1)
                    g.affine_select(out=pr[:, n % 4, :, :], in_=pr[:, n % 4, :, :],
                                    compare_op=ALU.is_ge, fill=0.0, base=0,
                                    pattern=[[0, HU], [1, P]],
                                    channel_multiplier=-1).then_inc(s["masked"], 1)
                return step

            def var_eps(k, var_sem):
                def step(b):
                    m, v_ = mv[:, k, b % 2], ve[:, k, b % 2]
                    g.wait_ge(s[var_sem], b + 1)
                    ins = g.tensor_scalar(v_[:, 0:1], m[:, 1:2], EPS, None, ALU.add)
                    if k == 2:
                        then(ins)
                        ins = g.tensor_scalar(v_[:, 1:2], v_[:, 0:1], EPS_IN, m[:, 1:2], ALU.mult,
                                              ALU.add)
                    mark((k, "var", b), ins)
                return step

            def rstd(k):
                def step(b):
                    n = 2 if k == 2 else 1
                    needs((k, "var", b))
                    mark((k, "rstd", b), g.tensor_tensor(
                        rs[:, k, b % 2, 0:n], ve[:, k, b % 2, 0:n], half_neg[:, 0:n], ALU.pow))
                return step

            def shift(k, out_sem):
                def step(b):
                    n = 2 if k == 2 else 1
                    r_ = rs[:, k, b % 2, 0:n]
                    needs((k, "rstd", b))
                    if k == 2:
                        then(g.tensor_scalar(r_[:, 0:1], r_[:, 0:1], tg[:, 3:4], None, ALU.mult))
                    g.tensor_scalar(nmr[:, k, b % 2, 0:n], r_, mv[:, k, b % 2, 0:1], -1.0, ALU.mult,
                                    ALU.mult).then_inc(s[out_sem], 1)
                return step

            def x4(b):
                g.wait_ge(s["r_ready"], b + 1)
                g.wait_ge(s["z_ready"], b + 1)
                g.tensor_tensor(x[:, b, :], r_tok[:, b % 2, :], x[:, b, :], ALU.add).then_inc(
                    s["x4_done"], 1)

            def scatter(b):
                g.wait_ge(s["idx_ready"], GROUP_OF[b] + 1)
                if b == 0:
                    g.wait_ge(s["zero_out"], 32)
                    g.wait_ge(s["number_ready"], 1)
                g.wait_ge(s["z_ready"], b + 1)
                g.indirect_dma_start(
                    out=disp_dram, out_offset=bass.IndirectOffsetOnAxis(ap=put_i[:, b:b + 1], axis=0),
                    in_=z_tok[:, b, :], in_offset=None, bounds_check=E * CAP - 1,
                    oob_is_err=False).then_inc(s["put_out"], 16)

            steps_of = {"scatter": scatter, "max_h": max_h, "max_rest": max_rest, "max_m": max_m,
                        "max_l": max_l, "var_f": var_eps(0, "f_var"), "rstd_f": rstd(0),
                        "shift_f": shift(0, "f_rstd"), "var_a": var_eps(1, "a_var"),
                        "rstd_a": rstd(1), "shift_a": shift(1, "a_rstd"),
                        "var_e": var_eps(2, "e_var"), "rstd_e": rstd(2),
                        "shift_e": shift(2, "e_rstd"),
                        "x4": x4}
            steps_of.update({f"mask{u}": mask_unit(u) for u in range(NU)})
            for t in range(SLOTS_N):
                for lag, name in POOL_PLAN:
                    b = batch_at(t, lag)
                    if b is not None:
                        steps_of[name](b)

            g.wait_ge(s["tok_ready"], 1)
            for e in range(E):
                g.wait_ge(s["y_done"], e + 1)
                g.indirect_dma_start(
                    out=moe_dram, out_offset=bass.IndirectOffsetOnAxis(ap=tok_i[:, e:e + 1], axis=0),
                    in_=y[:, e, :], in_offset=None, bounds_check=T - 1,
                    oob_is_err=False).then_inc(s["moe_out"], 16)

        @block.scalar
        def _(act):
            def part_h(n):
                act.wait_ge(s["proj_ready"], n + 1)
                act.copy(part[:, n, 0, :], bank[n][:, :]).then_inc(s["part_h"], 1)

            def part_m(n):
                act.wait_ge(s["rest1"], n + 1)
                act.copy(part[:, n, 1, :], rest[:, n, :]).then_inc(s["part_m"], 1)

            def copy_xt(half):
                act.wait_ge(s["xt_ready"], half + 1)
                act.copy(xn_t[:, 512 * half:512 * half + 512], bank[4 + half][:, :]).then_inc(
                    s["xt_copied"], 1)

            part_h(0)
            copy_xt(0)
            part_m(0)
            part_h(1)
            part_m(1)
            copy_xt(1)
            part_h(2)
            part_m(2)
            part_h(3)
            part_m(3)
            act.wait_ge(s["rows_in"], 16)
            act.activation(tg[:, :], g4, ACT.Tanh).then_inc(s["tanh_done"], 1)
            act.wait_ge(s["v_ones"], 1)
            for half in range(2):
                act.wait_ge(s["v_ready"], half + 1)
                act.copy(v_st[:, 4 * half:4 * half + 4, :, 0:DK],
                         bank[6 + half][:, :].rearrange("p (b h d) -> p b h d", b=4, d=DK)).then_inc(
                             s["v_copied"], 1)

            act.wait_ge(s["ctxtok_in"], 16)
            act.wait_ge(s["tanh_done"], 1)
            act.activation(ctx_tok[:, :, :], ctx_tok[:, :, :], ACT.Copy, scale=tg[:, 1:2]).then_inc(
                s["values_ready"], 1)

            def copy_nm(b):
                act.wait_ge(s["nmt_ready"], b + 1)
                if b >= 2:
                    act.wait_ge(s["m_out"], 16 * (b - 1))
                act.copy(nm_t[:, b % 2, :], S_BANK[0][0:ROWS, 0:P // 2].bitcast(BF16)).then_inc(
                    s["nm_copied"], 1)

            def exp_unit(u):
                def step(b):
                    n = NU * b + u
                    act.wait_ge(s["st_ready"], n + 1)
                    if n >= 4:
                        act.wait_ge(s["pv_done"], n - 3)
                    act.activation(pr[:, n % 4, :, :],
                                   ST_BANK[n % 2][:, :].rearrange("p (j q) -> p j q", j=HU),
                                   ACT.Exp, scale=float(DK) ** -0.5).then_inc(s["exp_done"], 1)
                return step

            def copy_o(b):
                act.wait_ge(s["pv_done"], NU * (b + 1))
                if b >= 2:
                    act.wait_ge(s["ot_ready"], b - 1)
                act.copy(o_sb[:, b % 2, :], O_BANK[:, :]).then_inc(s["o_copied"], 1)

            def copy_ct(b):
                act.wait_ge(s["ct_ready"], b + 1)
                if b >= 2:
                    act.wait_ge(s["wo_ready"], b - 1)
                act.copy(c_t[:, b % 2, :], W_BANK[:, 0:P]).then_inc(s["ct_copied"], 1)

            def norm(k, out, rstd_sem, used_sem, out_sem):
                def step(b):
                    act.wait_ge(s[rstd_sem], b + 1)
                    if b >= 2:
                        act.wait_ge(s[used_sem], b - 1)
                    act.activation(out[:, b % 2, :], x[:, b, :], ACT.Identity,
                                   bias=nmr[:, k, b % 2, 0:1],
                                   scale=rs[:, k, b % 2, 0:1]).then_inc(s[out_sem], 1)
                return step

            def norm_z(b):
                act.wait_ge(s["e_rstd"], b + 1)
                act.activation(z_tok[:, b, 0:P], x[:, b, :], ACT.Identity, bias=nmr[:, 2, b % 2, 1:2],
                               scale=rs[:, 2, b % 2, 1:2]).then_inc(s["z_ready"], 1)

            def copy_fq(b):
                act.wait_ge(s["fqt_ready"], b + 1)
                if b >= 2:
                    act.wait_ge(s["up_ready"], b - 1)
                act.copy(fq_t[:, b % 2, :], F_BANK[:, 0:P // 2].bitcast(BF16)).then_inc(
                    s["fqt_copied"], 1)

            def round_f(b):
                act.wait_ge(s["f_inv"], b + 1)
                if b >= 2:
                    act.wait_ge(s["fq_ready"], b - 1)
                act.activation(fr[:, b % 2, :], fx[:, b % 2, :], ACT.Copy, bias=ROUND,
                               scale=fa[:, b % 2, 2:3]).then_inc(s["round_ready"], 1)

            def tanh_g(b):
                act.wait_ge(s["gate_ready"], b + 1)
                if b >= 2:
                    act.wait_ge(s["gate_read"], b - 1)
                act.activation(sg[:, b % 2, :], F_BANK[:, :], ACT.Tanh,
                               scale=fa[:, b % 2, 3:4]).then_inc(s["tanh_g"], 1)

            def round_ft(b):
                act.wait_ge(s["ft_ready"], b + 1)
                if b >= 2:
                    act.wait_ge(s["ftq_ready"], b - 1)
                act.activation(ftr[:, b % 2, :], ft[:, b % 2, :], ACT.Copy, bias=ROUND,
                               scale=fa[:, b % 2, 7:8]).then_inc(s["ftr_ready"], 1)

            def copy_ft(b):
                act.wait_ge(s["ftt_ready"], b + 1)
                if b >= 2:
                    act.wait_ge(s["down_ready"], b - 1)
                act.copy(ftq_t[:, b % 2, :, :], G_BANK[:, 0:FI // 2].bitcast(BF16).rearrange(
                    "p (c t) -> p c t", c=NC)).then_inc(s["ftt_copied"], 1)

            def copy_ax(b):
                act.wait_ge(s["axt_ready"], b + 1)
                if b >= 2:
                    act.wait_ge(s["as_ready"], b - 1)
                act.copy(ax_t[:, b % 2, :], F_BANK[:, 0:P]).then_inc(s["axt_copied"], 1)

            def exp1(b):
                act.wait_ge(s["asc_ready"], b + 1)
                if b >= 2:
                    act.wait_ge(s["pt_ready"], b - 1)
                    act.wait_ge(s["x3_done"], b - 1)
                act.activation(ap_[:, b % 2, :], F_BANK[:, 128:256], ACT.Exp, bias=am[:, b % 2, 1:2],
                               scale=float(P) ** -0.5, accum_out=am[:, b % 2, 2:3]).then_inc(
                                   s["p_done"], 1)

            def copy_pt(b):
                act.wait_ge(s["pt_ready"], b + 1)
                if b >= 2:
                    act.wait_ge(s["av_ready"], b - 1)
                act.copy(ap_t[:, b % 2, :], F_BANK[:, 0:P]).then_inc(s["pt_copied"], 1)

            def copy_at(b):
                act.wait_ge(s["zt_ready"], b + 1)
                if b == 0:
                    act.wait_ge(s["cols_in"], 16)
                act.activation(a_t[:, P * b:P * b + P], G_BANK[:, 0:P], ACT.Identity,
                               bias=nb, scale=nw).then_inc(s["at_ready"], 1)

            def copy_lg(b):
                act.wait_ge(s["lg_ready"], b + 1)
                act.copy(lg[:, b, :], G_BANK[:, 128:128 + E + 2]).then_inc(s["lg_copied"], 1)

            steps_of = {"copy_nm": copy_nm, "copy_o": copy_o, "copy_ct": copy_ct,
                        "norm_f": norm(0, fx, "f_rstd", "fq_ready", "f_norm"), "copy_fq": copy_fq, "round_f": round_f,
                        "tanh_g": tanh_g, "round_ft": round_ft, "copy_ft": copy_ft,
                        "norm_a": norm(1, ax, "a_rstd", "axt_ready", "ax_ready"),
                        "copy_ax": copy_ax, "exp_a": exp1, "copy_pt": copy_pt,
                        "norm_r": norm(2, r_tok, "e_rstd", "x4_done", "r_ready"),
                        "norm_z": norm_z, "copy_at": copy_at, "copy_lg": copy_lg}
            steps_of.update({f"exp{u}": exp_unit(u) for u in range(NU)})
            for t in range(SLOTS_N):
                for lag, name in ACT_PLAN:
                    b = batch_at(t, lag)
                    if b is not None:
                        steps_of[name](b)

            for n in range(2 * NC):
                half, k = n // NC, n % NC
                act.wait_ge(s["r1_ready"], n + 1)
                act.activation(rh[:, k, 512 * half:512 * half + 512], bank[n][:, :],
                               ACT.Gelu_apprx_tanh, bias=rib[:, k:k + 1]).then_inc(s["rh_ready"], 1)
            act.wait_ge(s["lg_max"], 1)
            act.activation(ge[:, :, :], lg[:, :, :], ACT.Exp).then_inc(s["g_exp"], 1)

            for e in range(E):
                act.wait_ge(s["h_ready"], e + 1)
                if e >= 2:
                    act.wait_ge(s["y_ready"], e - 1)
                for k in range(NC):
                    act.activation(h_t[:, e % 2, k, :], bank[e % 2][:, P * k:P * k + P],
                                   ACT.Gelu_apprx_tanh, bias=ib[:, e, k:k + 1]).then_inc(
                                       s["h_done"], 1)

        @block.vector
        def _(v):
            steps = [0]

            def then(ins):
                steps[0] += 1
                ins.then_inc(s["dve_step"], 1)
                v.wait_ge(s["dve_step"], steps[0])

            written = {}

            def mark(key, ins):
                steps[0] += 1
                written[key] = steps[0]
                ins.then_inc(s["dve_step"], 1)

            def needs(key):
                v.wait_ge(s["dve_step"], written[key])

            v.memset(ones_b[:, :], 1.0).then_inc(s["ones_made"], 1)

            def ln0_stats(half):
                v.wait_ge(s[f"x_in{half}"], 16)
                for b in range(4 * half, 4 * half + 4):
                    then(v.bn_stats(st0[:, b, :], x[:, b, :]))
                    ins = v.bn_aggr(mv0[:, b, :], st0[:, b, :])
                    if b % 4 == 3:
                        ins.then_inc(s["ln0_var"], 1)
                    else:
                        then(ins)

            def ln0_norm(half):
                v.wait_ge(s["ln0_rstd"], half + 1)
                for b in range(4 * half, 4 * half + 4):
                    v.tensor_scalar(xn[:, b, :], x[:, b, :], mv0[:, b, 0:1], rs0[:, b:b + 1],
                                    ALU.subtract, ALU.mult).then_inc(s["ln0_done"], 1)

            def rest_of(n):
                v.wait_ge(s["part_h"], n + 1)
                v.tensor_tensor(rest[:, n, :], bank[n][:, :], part[:, n, 0, :],
                                ALU.subtract).then_inc(s["rest1"], 1)

            def part_l(n):
                v.wait_ge(s["part_m"], n + 1)
                v.tensor_tensor(part[:, n, 2, :], rest[:, n, :], part[:, n, 1, :],
                                ALU.subtract).then_inc(s["part_l"], 1)

            ln0_stats(0)
            ln0_stats(1)
            ln0_norm(0)
            rest_of(0)
            ln0_norm(1)
            part_l(0)
            rest_of(1)
            part_l(1)
            rest_of(2)
            part_l(2)
            rest_of(3)
            part_l(3)

            v.wait_ge(s["wffn_in"], 16)
            v.tensor_reduce(w_sum[:, :], w_raw[:, :, :], AX.X, ALU.add,
                            apply_absolute_value=True).then_inc(s["wsum_ready"], 1)
            def ternary(b):
                if b > 0:
                    return
                v.wait_ge(s["wsum_all"], 1)
                v.tensor_scalar(w_step[:, 0:3], bank[4][:, 0:3], 1.0 / (P * FI), EPS, ALU.mult,
                                ALU.max).then_inc(s["wstep_ready"], 1)
                v.wait_ge(s["wstep_ready"], 1)
                then(v.reciprocal(w_inv[:, :], w_step[:, 0:3]))
                for n in range(3):
                    then(v.tensor_scalar(w_raw[:, n, :], w_raw[:, n, :], w_inv[:, n:n + 1], 1.0,
                                         ALU.mult, ALU.min))
                then(v.tensor_scalar(w_step[:, 3:4], w_step[:, 0:1], 0.5, None, ALU.mult))
                then(v.tensor_scalar(w_step[:, 4:5], w_step[:, 3:4], w_step[:, 1:2], None, ALU.mult))
                v.wait_ge(s["tanh_done"], 1)
                then(v.tensor_scalar(w_step[:, 5:6], w_step[:, 2:3], tg[:, 2:3], None, ALU.mult))
                then(v.tensor_scalar(w_raw[:, :, :], w_raw[:, :, :], -1.0, ROUND, ALU.max, ALU.add))
                v.tensor_scalar(w_tern[:, :, :], w_raw[:, :, :], -ROUND, None, ALU.add).then_inc(
                    s["tern_ready"], 1)

            def max_unit(u):
                def step(b):
                    n = NU * b + u
                    side, hp = unit_cols(u)
                    v.wait_ge(s["s_ready"], n + 1)
                    if u == 0 and b >= 2:
                        v.wait_ge(s["nm_split"], b - 1)
                    v.tensor_reduce(nmax[:, b % 2, side, hp:hp + HU],
                                    S_BANK[n % 2][:, :].rearrange("p (j k) -> p j k", j=HU), AX.X,
                                    ALU.max, negate=True).then_inc(s["max_done"], 1)
                return step

            def recip_c(b):
                v.wait_ge(s["ot_ready"], b + 1)
                mark(("recip_c", b), v.reciprocal(rsum[:, b % 2, :], W_BANK[:, :].rearrange(
                    "p (h c) -> p h c", c=SLOTS)[:, :, DK]))

            def norm_c(b):
                needs(("recip_c", b))
                if b >= 2:
                    v.wait_ge(s["ct_ready"], b - 1)
                v.tensor_tensor(c_tok[:, b % 2],
                                W_BANK[:, :].rearrange("p (h c) -> p h c", c=SLOTS)[:, :, 0:DK],
                                rsum[:, b % 2, :].unsqueeze(2).to_broadcast([P, H, DK]),
                                ALU.mult).then_inc(s["c_norm"], 1)

            def x1(b):
                v.wait_ge(s["wo_ready"], b + 1)
                v.wait_ge(s["bo_added"], NB)
                v.scalar_tensor_tensor(x[:, b, :], W_BANK[:, P:2 * P], tg[:, 0:1], x[:, b, :],
                                       ALU.mult, ALU.add).then_inc(s["x1_done"], 1)

            def stats(k, x_sem):
                def step(b):
                    v.wait_ge(s[x_sem], b + 1)
                    mark((k, "stats", b), v.bn_stats(st[:, k, b % 2, :], x[:, b, :]))
                return step

            def aggr(k, used_sems, var_sem):
                def step(b):
                    needs((k, "stats", b))
                    if b >= 2:
                        for used in used_sems:
                            v.wait_ge(s[used], b - 1)
                    v.bn_aggr(mv[:, k, b % 2, :], st[:, k, b % 2, :]).then_inc(s[var_sem], 1)
                return step

            def amax_f(b):
                v.wait_ge(s["f_norm"], b + 1)
                if b >= 2:
                    v.wait_ge(s["tanh_g"], b - 1)
                    v.wait_ge(s["x2_done"], b - 1)
                mark(("amax_f", b), v.tensor_reduce(fa[:, b % 2, 0:1], fx[:, b % 2, :], AX.X,
                                                    ALU.max, apply_absolute_value=True))

            def step_f(b):
                needs(("amax_f", b))
                mark(("step_f", b), v.tensor_scalar(fa[:, b % 2, 1:2], fa[:, b % 2, 0:1], EPS,
                                                    1.0 / QMAX, ALU.max, ALU.mult))

            def inv_f(b):
                j = b % 2
                needs(("step_f", b))
                if b >= 2:
                    v.wait_ge(s["round_ready"], b - 1)
                v.reciprocal(fa[:, j, 2:3], fa[:, j, 1:2]).then_inc(s["f_inv"], 1)
                mark(("scale_f", b), v.tensor_scalar(fa[:, j, 3:4], w_step[:, 3:4], fa[:, j, 1:2],
                                                     None, ALU.mult))
                mark(("scale_t", b), v.tensor_scalar(fa[:, j, 4:5], fa[:, j, 1:2], fa[:, j, 1:2],
                                                     w_step[:, 4:5], ALU.mult, ALU.mult))

            def quant_f(b):
                v.wait_ge(s["round_ready"], b + 1)
                if b >= 2:
                    v.wait_ge(s["fqt_ready"], b - 1)
                needs(("scale_t", b))
                v.tensor_scalar(fq[:, b % 2, :], fr[:, b % 2, :], -ROUND, QMAX, ALU.add,
                                ALU.min).then_inc(s["fq_ready"], 1)

            def gate_t(b):
                v.wait_ge(s["tanh_g"], b + 1)
                if b >= 2:
                    v.wait_ge(s["ftr_ready"], b - 1)
                v.scalar_tensor_tensor(ft[:, b % 2, :], sg[:, b % 2, :], 1.0, F_BANK[:, :], ALU.add,
                                       ALU.mult).then_inc(s["gate_read"], 1)

            def up_t(b):
                v.wait_ge(s["gate_read"], b + 1)
                v.wait_ge(s["up_ready"], b + 1)
                v.scalar_tensor_tensor(ft[:, b % 2, :], G_BANK[:, :], fa[:, b % 2, 4:5],
                                       ft[:, b % 2, :], ALU.mult, ALU.mult).then_inc(
                                           s["up_read"], 1)

            def amax_t(b):
                v.wait_ge(s["up_read"], b + 1)
                mark(("amax_t", b), v.tensor_reduce(fa[:, b % 2, 5:6], ft[:, b % 2, :], AX.X,
                                                    ALU.max, apply_absolute_value=True))

            def step_t(b):
                needs(("amax_t", b))
                mark(("step_t", b), v.tensor_scalar(fa[:, b % 2, 6:7], fa[:, b % 2, 5:6], EPS,
                                                    1.0 / QMAX, ALU.max, ALU.mult))

            def inv_t(b):
                needs(("step_t", b))
                v.reciprocal(fa[:, b % 2, 7:8], fa[:, b % 2, 6:7]).then_inc(s["ft_ready"], 1)
                mark(("scale_d", b), v.tensor_scalar(fa[:, b % 2, 0:1], fa[:, b % 2, 6:7],
                                                     w_step[:, 5:6], None, ALU.mult))

            def quant_t(b):
                v.wait_ge(s["ftr_ready"], b + 1)
                if b >= 2:
                    v.wait_ge(s["ftt_ready"], b - 1)
                v.tensor_scalar(ftq[:, b % 2, :], ftr[:, b % 2, :], -ROUND, QMAX, ALU.add,
                                ALU.min).then_inc(s["ftq_ready"], 1)

            def x2(b):
                v.wait_ge(s["down_ready"], b + 1)
                needs(("scale_d", b))
                v.scalar_tensor_tensor(x[:, b, :], G_BANK[:, 256:256 + P], fa[:, b % 2, 0:1],
                                       x[:, b, :], ALU.mult, ALU.add).then_inc(s["x2_done"], 1)

            def max_a(b):
                v.wait_ge(s["as_ready"], b + 1)
                mark(("max_a", b), v.tensor_reduce(am[:, b % 2, 0:1], F_BANK[:, 128:256], AX.X,
                                                   ALU.max, negate=True))

            def bias_a(b):
                needs(("max_a", b))
                if b >= 2:
                    v.wait_ge(s["p_done"], b - 1)
                v.tensor_scalar(am[:, b % 2, 1:2], am[:, b % 2, 0:1], float(P) ** -0.5, None,
                                ALU.mult).then_inc(s["asc_ready"], 1)

            def recip_a(b):
                v.wait_ge(s["p_done"], b + 1)
                mark(("recip_a", b), v.reciprocal(am[:, b % 2, 3:4], am[:, b % 2, 2:3]))

            def x3(b):
                needs(("recip_a", b))
                v.wait_ge(s["av_ready"], b + 1)
                v.scalar_tensor_tensor(x[:, b, :], F_BANK[:, 256:384], am[:, b % 2, 3:4],
                                       x[:, b, :], ALU.mult, ALU.add).then_inc(s["x3_done"], 1)

            def choose(b):
                if b not in GROUP_ENDS:
                    return
                g = group(b)
                n = g.stop - g.start
                v.wait_ge(s["lg_copied"], b + 1)
                v.wait_ge(s["consts"], 14)
                then(v.tensor_reduce(gm[:, g, 0], lg[:, g, 0:E], AX.X, ALU.max))
                then(v.tensor_tensor(gv[:, g, :], lg[:, g, 0:E],
                                     gm[:, g, 0:1].to_broadcast([P, n, E]), ALU.is_equal))
                then(v.tensor_tensor(gv[:, g, :], gv[:, g, :],
                                     ranks[:, :].unsqueeze(1).to_broadcast([P, n, E]), ALU.mult))
                then(v.tensor_reduce(gvm[:, g], gv[:, g, :], AX.X, ALU.max))
                v.tensor_tensor(onehot_b[:, g, :], gv[:, g, :],
                                gvm[:, g].unsqueeze(2).to_broadcast([P, n, E]),
                                ALU.is_equal).then_inc(s["onehot_ready"], 1)
                then(v.tensor_scalar(slot[:, g], gvm[:, g], -float(CAP), float(E * CAP), ALU.mult,
                                     ALU.add))

            def place(b):
                if b not in GROUP_ENDS:
                    return
                g = group(b)
                v.wait_ge(s["loc_ready"], GROUP_OF[b] + 1)
                v.wait_ge(s["onehot_ready"], GROUP_OF[b] + 1)
                v.tensor_tensor(gl[:, g, :], LOC_BANK[:, E * g.start:E * g.stop].rearrange(
                    "p (b e) -> p b e", e=E), onehot_b[:, g, :], ALU.mult).then_inc(s["loc_read"], 1)
                v.wait_ge(s["loc_read"], GROUP_OF[b] + 1)
                then(v.tensor_reduce(loc[:, g], gl[:, g, :], AX.X, ALU.add))
                v.tensor_tensor(put_f[:, g], slot[:, g], loc[:, g], ALU.add).then_inc(
                    s["dve_step"], 1)
                steps[0] += 1
                then(v.tensor_scalar(drop[:, g], loc[:, g], float(CAP), 4.0 * E * CAP, ALU.is_ge,
                                     ALU.mult))
                then(v.tensor_tensor(put_f[:, g], put_f[:, g], drop[:, g], ALU.add))
                v.tensor_copy(put_i[:, g], put_f[:, g]).then_inc(s["idx_ready"], 1)

            steps_of = {"ternary": ternary, "choose": choose, "place": place, "recip_c": recip_c, "norm_c": norm_c,
                        "x1": x1, "stats_f": stats(0, "x1_done"),
                        "aggr_f": aggr(0, ["f_norm"], "f_var"), "amax_f": amax_f, "step_f": step_f,
                        "inv_f": inv_f, "quant_f": quant_f, "gate_t": gate_t, "up_t": up_t,
                        "amax_t": amax_t, "step_t": step_t, "inv_t": inv_t, "quant_t": quant_t, "x2": x2,
                        "stats_a": stats(1, "x2_done"), "aggr_a": aggr(1, ["ax_ready"], "a_var"),
                        "max_a": max_a, "bias_a": bias_a, "recip_a": recip_a, "x3": x3,
                        "stats_e": stats(2, "x3_done"), "aggr_e": aggr(2, ["z_ready", "r_ready"], "e_var")}
            steps_of.update({f"max{u}": max_unit(u) for u in range(NU)})
            for t in range(SLOTS_N):
                for lag, name in DVE_PLAN:
                    b = batch_at(t, lag)
                    if b is not None:
                        steps_of[name](b)

            logit, clog = lg[:, :, 0:E], lg[:, :, E:E + 2]
            then(v.tensor_reduce(gm[:, :, 1], clog, AX.X, ALU.max))
            then(v.tensor_tensor(logit, logit, gm[:, :, 0:1].to_broadcast([P, NB, E]), ALU.subtract))
            v.tensor_tensor(clog, clog, gm[:, :, 1:2].to_broadcast([P, NB, 2]),
                            ALU.subtract).then_inc(s["lg_max"], 1)
            then(v.tensor_scalar(keep[:, :], loc[:, :], float(CAP), None, ALU.is_lt))
            v.wait_ge(s["cols_in"], 16)
            for half in range(2):
                v.wait_ge(s["dt_ready"], half + 1)
                v.tensor_scalar(d_t[:, 4 * half:4 * half + 4, :],
                                bank[2 + half][:, :].rearrange("p (e t) -> p e t", e=4),
                                nw, nb, ALU.mult, ALU.add).then_inc(s["dt_copied"], 1)
            for half in range(2):
                v.wait_ge(s[f"disp_in{half}"], 16)
            then(v.tensor_scalar(tok_f[:, :], disp[:, :, P], float(NO_TOKEN), None, ALU.add))
            v.tensor_copy(tok_i[:, :], tok_f[:, :]).then_inc(s["tok_ready"], 1)
            v.wait_ge(s["g_exp"], 1)
            v.tensor_reduce(gs[:, :, 0], ge[:, :, 0:E], AX.X, ALU.add).then_inc(s["dve_step"], 1)
            v.tensor_reduce(gs[:, :, 1], ge[:, :, E:E + 2], AX.X, ALU.add).then_inc(
                s["dve_step"], 1)
            steps[0] += 2
            v.wait_ge(s["dve_step"], steps[0])
            then(v.reciprocal(gs[:, :, :], gs[:, :, :]))
            then(v.tensor_scalar(gs[:, :, 1], gs[:, :, 1], tg[:, 3:4], None, ALU.mult))
            then(v.tensor_tensor(coef[:, 0, :], ge[:, :, E], gs[:, :, 1], ALU.mult))
            then(v.tensor_tensor(coef[:, 1, :], ge[:, :, E + 1], gs[:, :, 1], ALU.mult))
            then(v.tensor_tensor(gk[:, :], gs[:, :, 0], keep[:, :], ALU.mult))
            then(v.tensor_tensor(coef[:, 1, :], coef[:, 1, :], gk[:, :], ALU.mult))
            v.wait_ge(s["x4_done"], NB)
            for e in range(E):
                v.wait_ge(s["y_ready"], e + 1)
                v.tensor_tensor(y[:, e, :], bank[4 + e % 2][:, 0:P], ob[:, e, :], ALU.add).then_inc(
                    s["y_done"], 1)
                v.scalar_tensor_tensor(x[:, e, :], rob, coef[:, 0, e:e + 1], x[:, e, :],
                                       ALU.mult, ALU.add).then_inc(s["coef_ready"], 1)

            def x5(b):
                v.wait_ge(s["r2_ready"], b + 1)
                v.wait_ge(s["coef_ready"], b + 1)
                v.scalar_tensor_tensor(x[:, b, :], bank[R2_BANKS[b % 4]][:, 0:P],
                                       coef[:, 0, b:b + 1], x[:, b, :], ALU.mult,
                                       ALU.add).then_inc(s["x5_done"], 1)

            def x6(b):
                v.wait_ge(s["x5_done"], b + 1)
                v.wait_ge(s[f"moe_in{b // 4}"], 16)
                v.scalar_tensor_tensor(x[:, b, :], moe[:, b, :], coef[:, 1, b:b + 1], x[:, b, :],
                                       ALU.mult, ALU.add).then_inc(s["x6_done"], 1)

            for b in range(NB):
                x5(b)
                if b >= NB // 2:
                    x6(b - NB // 2)
            for b in range(NB // 2, NB):
                x6(b)

        @block.tensor
        def _(pe):
            last_use = {}

            def take(k, reader, count):
                if k in last_use:
                    pe.wait_ge(s[last_use[k][0]], last_use[k][1])
                last_use[k] = (reader, count)

            pe.wait_ge(s["watt_in"], 16)

            def project(n, w, tokens):
                take(n, "rest1", n + 1)
                pe.matmul(bank[n][:, :], w, tokens, start=True, stop=True).then_inc(
                    s["proj_ready"], 1)

            for half in range(2):
                tok = slice(512 * half, 512 * half + 512)
                pe.wait_ge(s[f"ctx_in{half}"], 16)
                project(2 * half, wk, ctx_t[:, tok])
                pe.wait_ge(s["consts"], 3)
                take(4 + half, "xt_copied", half + 1)
                for b in range(4):
                    pe.wait_ge(s["ln0_done"], 4 * half + b + 1)
                    last = pe.transpose(bank[4 + half][:, P * b:P * b + P], xn[:, 4 * half + b, :],
                                        ident[:, :])
                last.then_inc(s["xt_ready"], 1)
                pe.wait_ge(s["xt_copied"], half + 1)
                project(2 * half + 1, wq, xn_t[:, tok])
            for half in range(2):
                take(6 + half, "v_copied", half + 1)
                for b in range(4):
                    n = 4 * half + b
                    last = pe.matmul(bank[6 + half][:, P * b:P * b + P], ctx_t[:, P * n:P * n + P],
                                     wv, start=True, stop=True)
                last.then_inc(s["v_ready"], 1)
            def scores(u):
                def step(b):
                    n = NU * b + u
                    side, hp = unit_cols(u)
                    rows_ = slice(64 * side, 64 * side + ROWS)
                    half, tok = at(b)
                    if u == 0 and b % 4 == 0:
                        pe.wait_ge(s[f"k_loaded{half}"], 2 * 16)
                        pe.wait_ge(s[f"q_loaded{half}"], 2 * 16)
                    take(n % 2, "max_done", n + 1)
                    o = S_BANK[n % 2]
                    for j in range(HU):
                        pe.matmul(o[:, P * j:P * j + P], ident_b[:, :], mask_b[:, :], start=True,
                                  stop=False)
                        last = pe.matmul(o[:, P * j:P * j + P], q_st[rows_, half, hp + j, tok],
                                         k_st[rows_, half, hp + j, tok], start=False, stop=True)
                    last.then_inc(s["s_ready"], 1)
                return step

            def sum_w(b):
                if b > 0:
                    return
                pe.wait_ge(s["wsum_ready"], 1)
                take(4, "wstep_ready", 1)
                pe.matmul(bank[4][:, 0:3], ones[:, :], w_sum[:, :], start=True, stop=True).then_inc(
                    s["wsum_all"], 1)

            def turn_max(b):
                pe.wait_ge(s["nm_split"], b + 1)
                take(0, "nm_copied", b + 1)
                pe.transpose(S_BANK[0][0:ROWS, 0:P // 2].bitcast(BF16),
                             nm_p[:, b % 2].rearrange("p s c h -> p (s c h)"),
                             ident_b[:, :]).then_inc(s["nmt_ready"], 1)

            def scores_t(u):
                def step(b):
                    n = NU * b + u
                    side, hp = unit_cols(u)
                    rows_ = slice(64 * side, 64 * side + ROWS + MROW)
                    half, tok = at(b)
                    if u == 0:
                        pe.wait_ge(s[f"m_loaded{b % 2}"], 32 * (b // 2 + 1))
                    if n == 0:
                        pe.wait_ge(s["ones_in"], 32)
                    take(2 + n % 2, "exp_done", n + 1)
                    o = ST_BANK[n % 2]
                    for j in range(HU):
                        last = pe.matmul(o[:, P * j:P * j + P], k_st[rows_, half, hp + j, tok],
                                         q_st[rows_, half, hp + j, tok], start=True, stop=True)
                    last.then_inc(s["st_ready"], 1)
                return step

            def values(u):
                def step(b):
                    n = NU * b + u
                    if n == 0:
                        pe.wait_ge(s["v_copied"], 2)
                    pe.wait_ge(s["masked"], n + 1)
                    if u == 0:
                        take(4, "o_copied", b + 1)
                    for j in range(HU):
                        last = pe.matmul(O_BANK[32 * j:32 * j + 32, P * u:P * u + P],
                                         v_st[:, b, HU * u + j, :], pr[:, n % 4, j, :], start=True,
                                         stop=True)
                    last.then_inc(s["pv_done"], 1)
                return step

            def turn_o(b):
                pe.wait_ge(s["o_copied"], b + 1)
                take(5, "c_norm", b + 1)
                for u in range(NU):
                    last = pe.transpose(W_BANK[:, P * u:P * u + P],
                                        o_sb[:, b % 2, P * u:P * u + P], ident[:, :])
                last.then_inc(s["ot_ready"], 1)

            def turn_c(b):
                pe.wait_ge(s["c_norm"], b + 1)
                take(5, "ct_copied", b + 1)
                pe.transpose(W_BANK[:, 0:P], c_tok[:, b % 2].rearrange("p h d -> p (h d)"),
                             ident[:, :]).then_inc(s["ct_ready"], 1)

            def out_proj(b):
                pe.wait_ge(s["ct_copied"], b + 1)
                take(5, "x1_done", b + 1)
                pe.matmul(W_BANK[:, P:2 * P], c_t[:, b % 2, :], wo, start=True,
                          stop=True).then_inc(s["wo_ready"], 1)

            def turn_fq(b):
                pe.wait_ge(s["fq_ready"], b + 1)
                if b == 0:
                    pe.wait_ge(s["tern_ready"], 1)
                take(6, "fqt_copied", b + 1)
                pe.transpose(F_BANK[:, 0:P // 2].bitcast(BF16), fq[:, b % 2, :],
                             ident_b[:, :]).then_inc(s["fqt_ready"], 1)

            def gate_up(b):
                pe.wait_ge(s["fqt_copied"], b + 1)
                take(6, "gate_read", b + 1)
                pe.matmul(F_BANK[:, :], fq_t[:, b % 2, :], w_tern[:, 0, :], start=True,
                          stop=True).then_inc(s["gate_ready"], 1)
                take(7, "up_read", b + 1)
                pe.matmul(G_BANK[:, :], fq_t[:, b % 2, :], w_tern[:, 1, :], start=True,
                          stop=True).then_inc(s["up_ready"], 1)

            def turn_ft(b):
                pe.wait_ge(s["ftq_ready"], b + 1)
                take(7, "ftt_copied", b + 1)
                for k in range(NC):
                    last = pe.transpose(G_BANK[:, 0:FI // 2].bitcast(BF16)[:, P * k:P * k + P],
                                        ftq[:, b % 2, P * k:P * k + P], ident_b[:, :])
                last.then_inc(s["ftt_ready"], 1)

            def down(b):
                pe.wait_ge(s["ftt_copied"], b + 1)
                take(7, "x2_done", b + 1)
                for k in range(NC):
                    last = pe.matmul(G_BANK[:, 256:256 + P], ftq_t[:, b % 2, k, :],
                                     w_tern[:, 2, P * k:P * k + P], start=(k == 0),
                                     stop=(k == NC - 1))
                last.then_inc(s["down_ready"], 1)

            def turn_ax(b):
                pe.wait_ge(s["ax_ready"], b + 1)
                take(6, "axt_copied", b + 1)
                pe.transpose(F_BANK[:, 0:P], ax[:, b % 2, :], ident[:, :]).then_inc(
                    s["axt_ready"], 1)

            def att_scores(b):
                pe.wait_ge(s["axt_copied"], b + 1)
                take(6, "p_done", b + 1)
                pe.matmul(F_BANK[:, 128:256], ident_b[:, :], mask_b[:, :], start=True, stop=False)
                pe.matmul(F_BANK[:, 128:256], ax_t[:, b % 2, :], ctx_t[:, P * b:P * b + P],
                          start=False, stop=True).then_inc(s["as_ready"], 1)

            def turn_p(b):
                pe.wait_ge(s["p_done"], b + 1)
                take(6, "pt_copied", b + 1)
                pe.transpose(F_BANK[:, 0:P], ap_[:, b % 2, :], ident[:, :]).then_inc(
                    s["pt_ready"], 1)

            def att_values(b):
                if b == 0:
                    pe.wait_ge(s["values_ready"], 1)
                pe.wait_ge(s["pt_copied"], b + 1)
                take(6, "x3_done", b + 1)
                pe.matmul(F_BANK[:, 256:384], ap_t[:, b % 2, :], ctx_tok[:, b, :], start=True,
                          stop=True).then_inc(s["av_ready"], 1)

            def turn_z(b):
                pe.wait_ge(s["z_ready"], b + 1)
                take(7, "at_ready", b + 1)
                pe.transpose(G_BANK[:, 0:P], z_tok[:, b, 0:P], ident[:, :]).then_inc(
                    s["zt_ready"], 1)

            def logits(b):
                pe.wait_ge(s["at_ready"], b + 1)
                take(7, "lg_copied", b + 1)
                pe.matmul(G_BANK[:, 128:128 + E + 2], a_t[:, P * b:P * b + P], wgc,
                          start=True, stop=True).then_inc(s["lg_ready"], 1)

            def places(b):
                if b not in GROUP_ENDS:
                    return
                pe.wait_ge(s["onehot_ready"], GROUP_OF[b] + 1)
                pe.wait_ge(s["consts"], 6)
                take(7, "loc_read", GROUP_OF[b] + 1)
                for q in range(group(b).start, b + 1):
                    for before in range(q + 1):
                        last = pe.matmul(LOC_BANK[:, E * q:E * q + E],
                                         (before_b if before == q else ones_b)[:, :],
                                         onehot_b[:, before, :], start=(before == 0),
                                         stop=(before == q))
                last.then_inc(s["loc_ready"], 1)

            def hidden_res(n):
                half, k = n // NC, n % NC
                take(n, "rh_ready", n + 1)
                pe.matmul(bank[n][:, :], ri[:, P * k:P * k + P],
                          a_t[:, 512 * half:512 * half + 512], start=True, stop=True).then_inc(
                              s["r1_ready"], 1)

            def early_res(b):
                if b == NB - NC:
                    pe.wait_ge(s["wres_in"], 16)
                    pe.wait_ge(s["at_ready"], NB // 2)
                if b >= NB - NC:
                    hidden_res(b - (NB - NC))

            pe.wait_ge(s["consts"], 5)
            steps_of = {"early_res": early_res, "sum_w": sum_w, "places": places,"turn_max": turn_max, "turn_o": turn_o, "turn_c": turn_c,
                        "out_proj": out_proj, "turn_fq": turn_fq, "gate_up": gate_up,
                        "turn_ft": turn_ft, "down": down, "turn_ax": turn_ax,
                        "att_scores": att_scores, "turn_p": turn_p, "att_values": att_values,
                        "turn_z": turn_z, "logits": logits}
            steps_of.update({f"scores{u}": scores(u) for u in range(NU)})
            steps_of.update({f"scores_t{u}": scores_t(u) for u in range(NU)})
            steps_of.update({f"values{u}": values(u) for u in range(NU)})
            for t in range(SLOTS_N):
                for lag, name in PE_PLAN:
                    b = batch_at(t, lag)
                    if b is not None:
                        steps_of[name](b)

            for n in range(NC, 2 * NC):
                hidden_res(n)

            def output_res(b):
                if b % 4 == 0:
                    pe.wait_ge(s["rh_ready"], NC * (b // 4 + 1))
                take(R2_BANKS[b % 4], "x5_done", b + 1)
                for k in range(NC):
                    last = pe.matmul(bank[R2_BANKS[b % 4]][:, 0:P], rh[:, k, P * b:P * b + P],
                                     ro[:, k, :], start=(k == 0), stop=(k == NC - 1))
                last.then_inc(s["r2_ready"], 1)

            for b in range(R2_EARLY):
                output_res(b)
            for half in range(2):
                pe.wait_ge(s[f"disp_in{half}"], 16)
                take(2 + half, "dt_copied", half + 1)
                for e in range(4 * half, 4 * half + 4):
                    last = pe.transpose(bank[2 + half][:, P * (e % 4):P * (e % 4) + P],
                                        disp[:, e, 0:P], ident[:, :])
                last.then_inc(s["dt_ready"], 1)
            pe.wait_ge(s["iw_in"], 16)
            pe.wait_ge(s["ow_in"], 16)

            def hidden(e):
                pe.wait_ge(s["dt_copied"], e // 4 + 1)
                take(e % 2, "h_done", NC * (e + 1))
                for k in range(NC):
                    last = pe.matmul(bank[e % 2][:, P * k:P * k + P], iw[:, e, P * k:P * k + P],
                                     d_t[:, e, :], start=True, stop=True)
                last.then_inc(s["h_ready"], 1)

            hidden(0)
            for e in range(E):
                if e + 1 < E:
                    hidden(e + 1)
                pe.wait_ge(s["h_done"], NC * (e + 1))
                take(4 + e % 2, "y_done", e + 1)
                for k in range(NC):
                    last = pe.matmul(bank[4 + e % 2][:, 0:P], h_t[:, e % 2, k, :], ow[:, e, k, :],
                                     start=(k == 0), stop=(k == NC - 1))
                last.then_inc(s["y_ready"], 1)
            for b in range(R2_EARLY, NB):
                output_res(b)


Q_RUNS = ((0, 0, 3, 0, 0), (1, 3, 2, 1, 0), (2, 5, 1, 2, 0))
K_RUNS = ((2, 0, 3, 0, 1), (2, 3, 2, 0, 1), (2, 5, 1, 0, 1))

ROWS_N = P + 4 + P + E * P
COLS_N = 2 + E + 2 + NC + E * NC

PE_PLAN = [
    (3, "sum_w"), (13, "values0"), (14, "values2"), (0, "scores0"), (14, "values3"),
    (2, "scores3"), (23, "down"), (27, "turn_p"), (26, "att_scores"), (11, "scores_t0"),
    (15, "turn_c"), (33, "logits"), (22, "turn_ft"), (31, "turn_z"), (7, "turn_max"),
    (12, "scores_t2"), (19, "turn_fq"), (11, "scores_t1"), (25, "turn_ax"), (0, "scores1"),
    (14, "turn_o"), (15, "out_proj"), (0, "scores2"), (12, "scores_t3"), (34, "places"),
    (28, "att_values"), (13, "values1"), (41, "early_res"), (19, "gate_up")]
ACT_PLAN = [
    (8, "copy_nm"), (20, "copy_fq"), (13, "exp3"), (34, "copy_lg"), (23, "copy_ft"),
    (25, "copy_ax"), (12, "exp0"), (20, "tanh_g"), (27, "exp_a"), (31, "norm_z"), (21, "round_ft"),
    (12, "exp1"), (14, "copy_o"), (19, "round_f"), (12, "exp2"), (32, "norm_r"), (24, "norm_a"),
    (27, "copy_pt"), (15, "copy_ct"), (16, "norm_f"), (31, "copy_at")]
DVE_PLAN = [
    (9, "ternary"), (20, "quant_f"), (22, "step_t"), (24, "stats_a"), (18, "amax_f"), (4, "max3"),
    (27, "max_a"), (27, "bias_a"), (22, "inv_t"), (21, "gate_t"), (19, "inv_f"), (30, "aggr_e"),
    (1, "max0"), (15, "recip_c"), (21, "up_t"), (18, "step_f"), (24, "aggr_a"), (2, "max1"),
    (29, "x3"), (16, "x1"), (21, "amax_t"), (16, "stats_f"), (16, "aggr_f"), (35, "place"),
    (22, "quant_t"), (15, "norm_c"), (23, "x2"), (34, "choose"), (2, "max2"), (27, "recip_a"),
    (29, "stats_e")]
POOL_PLAN = [
    (14, "mask2"), (14, "mask3"), (17, "var_f"), (8, "max_l"), (24, "var_a"), (25, "shift_a"),
    (38, "x4"), (24, "rstd_a"), (31, "rstd_e"), (17, "rstd_f"), (17, "shift_f"), (7, "max_rest"),
    (13, "mask1"), (30, "var_e"), (7, "max_m"), (31, "shift_e"), (4, "max_h"), (12, "mask0"),
    (51, "scatter")]
LAST = max(lag for plan in (PE_PLAN, ACT_PLAN, DVE_PLAN, POOL_PLAN) for lag, _ in plan)


def layout(i):
    def heads(w):
        return w.T.reshape(P, 2, 2, HU, DK).transpose(0, 2, 4, 1, 3).reshape(P, P)

    return {
        "x": i["x"].transpose(1, 0, 2), "ctx_tok": i["ctx_1024"].transpose(1, 0, 2),
        "ctx_t": i["ctx_1024"].transpose(2, 0, 1).reshape(P, T),
        "w_att": np.stack([heads(i["L0_xattn_W_k"]), heads(i["L0_xattn_W_q"]),
                           i["L0_xattn_W_v"].T, i["L0_xattn_W_o"].T], 1),
        "rows": np.concatenate([i["L0_xattn_b_o"], i["g_xattn"], i["g_ffn"],
                                i["L1_ffn_res_output_b"], i["L1_ffn_output_b"].reshape(-1)]),
        "w_ffn": np.stack([i["L0_ffn_w_gate"].T, i["L0_ffn_w_up"].T,
                           i["L0_ffn_w_down"].T.reshape(NC, P, P).transpose(1, 0, 2).reshape(
                               P, FI)], 1),
        "cols": np.concatenate([i["L1_ffn_attn_nw"].reshape(P, 1), i["L1_ffn_attn_nb"].reshape(P, 1),
                                i["L1_ffn_wg"], i["L1_ffn_res_coef"],
                                i["L1_ffn_res_inter_b"].reshape(NC, P).T,
                                i["L1_ffn_inter_b"].reshape(E * NC, P).T], 1),
        "w_res": np.concatenate([i["L1_ffn_res_inter_w"],
                                 i["L1_ffn_res_output_w"].reshape(NC, P, P).transpose(
                                     1, 0, 2).reshape(P, FI)], 1),
        "iw": i["L1_ffn_inter_w"].transpose(1, 0, 2),
        "ow": i["L1_ffn_output_w"].reshape(E, NC, P, P).transpose(2, 0, 1, 3),
    }


def kernel(**inputs):
    import concourse.bacc as bacc
    from concourse.bass_utils import run_bass_kernel_spmd

    arrays = {n: np.ascontiguousarray(v) for n, v in
              layout({n: np.asarray(v) for n, v in inputs.items()}).items()}
    nc = bacc.Bacc("TRN2", target_bir_lowering=False, num_devices=1)
    aps = {n: nc.dram_tensor(f"{n}_in", v.shape, F32, kind="ExternalInput").ap()
           for n, v in arrays.items()}
    aps["out"] = nc.dram_tensor("tokens_out", (P, NB, P), F32, kind="ExternalOutput").ap()
    gated_flamingo(nc, aps)
    r = run_bass_kernel_spmd(nc, [{f"{n}_in": v for n, v in arrays.items()}], core_ids=[0])
    return np.ascontiguousarray(r.results[0]["tokens_out"].transpose(1, 0, 2))
```
